# Optimizing a Trainium2 kernel written in Bass

```python
import numpy as np
import jax
import jax.numpy as jnp

def _softmax(x, axis=-1):
    return jax.nn.softmax(x, axis=axis)

def _gelu(x):
    return jax.nn.gelu(x, approximate=True)

def _silu(x):
    return jax.nn.silu(x)

def _sigmoid(x):
    return jax.nn.sigmoid(x)

def _layernorm(x, axis=-1, eps=1e-05):
    m = jnp.mean(x, axis=axis, keepdims=True)
    v = jnp.var(x, axis=axis, keepdims=True)
    return (x - m) / jnp.sqrt(v + eps)

def _scatter_add(tgt, idx, src, axis=0):
    return tgt.at[idx].add(src)

def _segment_sum(src, seg, n):
    return jax.ops.segment_sum(src, seg, n)
kernel_name = 'mk_gnn_ffn_d4_gnn_r8_298be6'

def setup_inputs(seed: int=0):
    np.random.seed(seed)
    _w = jnp.asarray

    def _rec_inputs():
        import jax
        import jax.numpy as jnp
        _gk = jax.random.key(seed)
        x = -0.001003 + 1 * jax.random.normal(jax.random.fold_in(_gk, 1), (384, 512), jnp.float32)
        src = jax.random.randint(jax.random.fold_in(_gk, 2), (12288,), 0, 384, jnp.int32)
        dst = jnp.minimum((384 * jax.random.uniform(jax.random.fold_in(_gk, 3), (12288,)) ** 2.0).astype(jnp.int32), 3071)
        _o = jnp.argsort(dst, stable=True)
        src = src[_o]
        dst = dst[_o]
        edge_type_8 = jax.random.randint(jax.random.fold_in(_gk, 12), (12288,), 0, 8, jnp.int32)
        edge_weight = jax.random.uniform(jax.random.fold_in(_gk, 13), (12288,), jnp.float32, 0.0, 0.999999)
        node_vec1 = jax.random.uniform(jax.random.fold_in(_gk, 14), (384, 1), jnp.float32, 0.0, 0.999957)
        return (x, src, dst, edge_type_8, edge_weight, node_vec1)
    x, src, dst, edge_type_8, edge_weight, node_vec1 = _rec_inputs()

    def _L0_gnn_setup():
        import jax, jax.numpy as jnp
        import numpy as np
        N = 384
        HID = 512
        H = 8
        HD = HID // H
        E = 12288
        LN_EPS = 1e-05
        key = jax.random.key(seed)
        ks = jax.random.split(key, 12)
        x = jax.random.normal(ks[0], (N, HID), jnp.float32)
        lin = jax.random.permutation(ks[1], N * N)[:E]
        edges = jnp.stack([lin // N, lin % N]).astype(jnp.int32)
        s = 0.02
        Wv = jax.random.normal(ks[2], (HID, HID), jnp.float32) * s
        bv = jax.random.normal(ks[3], (HID,), jnp.float32) * s
        Ww = jax.random.normal(ks[4], (2 * HID, 2 * HID), jnp.float32) * s
        bw = jax.random.normal(ks[5], (2 * HID,), jnp.float32) * s
        Wa = jax.random.normal(ks[6], (2 * HD, 1), jnp.float32) * s
        ba = jax.random.normal(ks[7], (1,), jnp.float32) * s
        gamma = jnp.ones((HID,), jnp.float32)
        beta = jnp.zeros((HID,), jnp.float32)
        return dict(x=x, edges=edges, Wv=Wv, bv=bv, Ww=Ww, bw=bw, Wa=Wa, ba=ba, gamma=gamma, beta=beta)
    _L0_gnn_all = _L0_gnn_setup()
    _L0_gnn_in = {k: v for k, v in _L0_gnn_all.items() if k in ('Wv', 'bv', 'Ww', 'bw', 'Wa', 'ba', 'gamma', 'beta')}
    del _L0_gnn_all

    def _L0_ffn_setup():
        import jax, jax.numpy as jnp
        import numpy as np
        EPS = 1e-09
        LN_EPS = 1e-05

        def _layernorm(x, gamma):
            x = x.astype(jnp.float32)
            mu = jnp.mean(x, axis=-1, keepdims=True)
            var = jnp.var(x, axis=-1, keepdims=True)
            return (x - mu) * jax.lax.rsqrt(var + LN_EPS) * gamma
        key = jax.random.key(seed)
        ks = jax.random.split(key, 5)
        b, n, d, e, h = (4, 1024, 512, 6, 256)
        x = jax.random.normal(ks[0], (b, n, d), dtype=jnp.float32)
        w_gating = jax.random.normal(ks[1], (d, e), dtype=jnp.float32)
        std1 = 1.0 / np.sqrt(h)
        std2 = 1.0 / np.sqrt(d)
        w1 = jax.random.uniform(ks[2], (e, d, h), jnp.float32, -std1, std1)
        w2 = jax.random.uniform(ks[3], (e, h, d), jnp.float32, -std2, std2)
        gamma = jnp.ones((d,), dtype=jnp.float32)
        return {'x': x, 'w_gating': w_gating, 'gamma': gamma, 'w1': w1, 'w2': w2}
    _L0_ffn_all = _L0_ffn_setup()
    _L0_ffn_in = {k: v for k, v in _L0_ffn_all.items() if k in ('w_gating', 'gamma', 'w1', 'w2')}
    del _L0_ffn_all

    def _L1_gnn_setup():
        import jax, jax.numpy as jnp
        import numpy as np
        N_NODES = 40962
        LATENT_DIM = 512
        N_EDGES = 81924
        NUM_BLOCKS = 4
        NUM_HEADS = 4
        NUM_FREQ = 32
        BASE_PERIOD = 16
        NOISE_EMB_DIM = 16
        EPS = 1e-05

        def _cond_layer_norm(x, cond, sw, sb, bw, bb):
            mu = jnp.mean(x, axis=-1, keepdims=True)
            var = jnp.var(x, axis=-1, keepdims=True)
            xn = (x - mu) * jax.lax.rsqrt(var + EPS)
            scale = cond @ sw + sb
            bias = cond @ bw + bb
            return xn * (1.0 + scale) + bias

        def _sparse_attention(x, src, dst, wq, bq, wk, bk, wv, bv, wo, bo):
            N, D = x.shape
            H, Dh = (NUM_HEADS, D // NUM_HEADS)
            q = (x @ wq + bq).reshape(N, H, Dh) * Dh ** (-0.5)
            k = (x @ wk + bk).reshape(N, H, Dh)
            v = (x @ wv + bv).reshape(N, H, Dh)
            scores = jnp.einsum('ehd,ehd->eh', q[src], k[dst])
            smax = jax.ops.segment_max(scores, src, num_segments=N)
            ex = jnp.exp(scores - smax[src])
            denom = jax.ops.segment_sum(ex, src, num_segments=N)
            attn = ex / denom[src]
            out = jax.ops.segment_sum(attn[:, :, None] * v[dst], src, num_segments=N)
            return out.reshape(N, D) @ wo + bo

        def _forward(x, edge_index, noise_levels, f_w1, f_b1, f_w2, f_b2, s1_w, s1_b, b1_w, b1_b, wq, bq, wk, bk, wv, bv, wo, bo, s2_w, s2_b, b2_w, b2_b, m_w1, m_b1, m_w2, m_b2):
            src, dst = (edge_index[0], edge_index[1])
            freqs = jnp.arange(1, NUM_FREQ + 1, dtype=x.dtype) * (2.0 * np.pi / BASE_PERIOD)
            ph = noise_levels * freqs
            emb = jnp.concatenate([jnp.sin(ph), jnp.cos(ph)], axis=-1)
            cond = jax.nn.silu(emb @ f_w1 + f_b1) @ f_w2 + f_b2
            for i in range(NUM_BLOCKS):
                y = _cond_layer_norm(x, cond, s1_w[i], s1_b[i], b1_w[i], b1_b[i])
                y = _sparse_attention(y, src, dst, wq[i], bq[i], wk[i], bk[i], wv[i], bv[i], wo[i], bo[i])
                x = x + y
                y = _cond_layer_norm(x, cond, s2_w[i], s2_b[i], b2_w[i], b2_b[i])
                y = jax.nn.relu(y @ m_w1[i] + m_b1[i]) @ m_w2[i] + m_b2[i]
                x = x + y
            return x
        key = jax.random.key(seed)
        ks = jax.random.split(key, 20)

        def w(k, shape, s=0.02):
            return jax.random.normal(k, shape, dtype=jnp.float32) * s
        D, B, C = (LATENT_DIM, NUM_BLOCKS, NOISE_EMB_DIM)
        z = lambda *s: jnp.zeros(s, jnp.float32)
        return {'latent_mesh_nodes': jax.random.normal(ks[0], (N_NODES, D), dtype=jnp.float32), 'edge_index': jax.random.randint(ks[1], (2, N_EDGES), 0, N_NODES, dtype=jnp.int32), 'noise_levels': jax.random.uniform(ks[2], (N_NODES, 1), dtype=jnp.float32), 'f_w1': w(ks[3], (2 * NUM_FREQ, C)), 'f_b1': z(C), 'f_w2': w(ks[4], (C, C)), 'f_b2': z(C), 's1_w': w(ks[5], (B, C, D)), 's1_b': z(B, D), 'b1_w': w(ks[6], (B, C, D)), 'b1_b': z(B, D), 'wq': w(ks[7], (B, D, D)), 'bq': z(B, D), 'wk': w(ks[8], (B, D, D)), 'bk': z(B, D), 'wv': w(ks[9], (B, D, D)), 'bv': z(B, D), 'wo': w(ks[10], (B, D, D)), 'bo': z(B, D), 's2_w': w(ks[11], (B, C, D)), 's2_b': z(B, D), 'b2_w': w(ks[12], (B, C, D)), 'b2_b': z(B, D), 'm_w1': w(ks[13], (B, D, D)), 'm_b1': z(B, D), 'm_w2': w(ks[14], (B, D, D)), 'm_b2': z(B, D)}
    _L1_gnn_all = _L1_gnn_setup()
    _L1_gnn_in = {k: v for k, v in _L1_gnn_all.items() if k in ('f_w1', 'f_b1', 'f_w2', 'f_b2', 's1_w', 's1_b', 'b1_w', 'b1_b', 'wq', 'bq', 'wk', 'bk', 'wv', 'bv', 'wo', 'bo', 's2_w', 's2_b', 'b2_w', 'b2_b', 'm_w1', 'm_b1', 'm_w2', 'm_b2')}
    del _L1_gnn_all

    def _L1_ffn_setup():
        import jax, jax.numpy as jnp
        import numpy as np
        MIN_EXPERT_CAPACITY = 4
        EPS = 1e-09
        CAPACITY_FACTOR = 2.0

        def cumsum_exclusive(t, axis):
            return jnp.cumsum(t, axis=axis) - t

        def safe_one_hot(idx, depth):
            return jax.nn.one_hot(idx, depth + 1)[..., :depth]

        def top2_gating(x, w_gating):
            b, n, d = x.shape
            e = w_gating.shape[-1]
            raw_gates = jax.nn.softmax(jnp.einsum('bnd,de->bne', x, w_gating), axis=-1)
            gate_1 = jnp.max(raw_gates, axis=-1)
            index_1 = jnp.argmax(raw_gates, axis=-1)
            mask_1 = jax.nn.one_hot(index_1, e, dtype=raw_gates.dtype)
            gates_without_top1 = raw_gates * (1.0 - mask_1)
            gate_2 = jnp.max(gates_without_top1, axis=-1)
            index_2 = jnp.argmax(gates_without_top1, axis=-1)
            mask_2 = jax.nn.one_hot(index_2, e, dtype=raw_gates.dtype)
            denom = gate_1 + gate_2 + EPS
            gate_1 = gate_1 / denom
            gate_2 = gate_2 / denom
            density_1 = jnp.mean(mask_1, axis=-2)
            density_1_proxy = jnp.mean(raw_gates, axis=-2)
            loss = jnp.mean(density_1_proxy * density_1) * float(e * e)
            capacity = max(min(n, int(n * 2 * CAPACITY_FACTOR / e)), MIN_EXPERT_CAPACITY)
            cap_f = float(capacity)
            pos1 = cumsum_exclusive(mask_1, axis=-2) * mask_1
            mask_1 = mask_1 * (pos1 < cap_f).astype(mask_1.dtype)
            mask_1_count = jnp.sum(mask_1, axis=-2, keepdims=True)
            mask_1_flat = jnp.sum(mask_1, axis=-1)
            pos1 = jnp.sum(pos1, axis=-1)
            gate_1 = gate_1 * mask_1_flat
            pos2 = (cumsum_exclusive(mask_2, axis=-2) + mask_1_count) * mask_2
            mask_2 = mask_2 * (pos2 < cap_f).astype(mask_2.dtype)
            mask_2_flat = jnp.sum(mask_2, axis=-1)
            pos2 = jnp.sum(pos2, axis=-1)
            gate_2 = gate_2 * mask_2_flat
            combine = gate_1[..., None, None] * mask_1_flat[..., None, None] * jax.nn.one_hot(index_1, e, dtype=x.dtype)[..., None] * safe_one_hot(pos1.astype(jnp.int32), capacity)[..., None, :] + gate_2[..., None, None] * mask_2_flat[..., None, None] * jax.nn.one_hot(index_2, e, dtype=x.dtype)[..., None] * safe_one_hot(pos2.astype(jnp.int32), capacity)[..., None, :]
            dispatch = (combine > 0).astype(combine.dtype)
            return (dispatch, combine, loss)
        key = jax.random.key(seed)
        k_x, k_g, k_w1, k_w2 = jax.random.split(key, 4)
        b, n, d, e, h = (2, 512, 512, 16, 256)
        x = jax.random.normal(k_x, (b, n, d), dtype=jnp.float32)
        w_gating = jax.random.normal(k_g, (d, e), dtype=jnp.float32) / np.sqrt(d)
        w1 = jax.random.normal(k_w1, (e, d, h), dtype=jnp.float32) / np.sqrt(d)
        w2 = jax.random.normal(k_w2, (e, h, d), dtype=jnp.float32) / np.sqrt(h)
        return {'x': x, 'w_gating': w_gating, 'w1': w1, 'w2': w2}
    _L1_ffn_all = _L1_ffn_setup()
    _L1_ffn_in = {k: v for k, v in _L1_ffn_all.items() if k in ('w_gating', 'w1', 'w2')}
    del _L1_ffn_all

    def _L2_gnn_setup():
        import jax, jax.numpy as jnp
        import numpy as np
        N, IN_DIM, H, D, E = (6250, 512, 8, 64, 100000)
        NEG_SLOPE = 0.2
        LN_EPS = 1e-05
        key = jax.random.key(seed)
        ks = jax.random.split(key, 8)
        x = jax.random.normal(ks[0], (N, IN_DIM), dtype=jnp.float32)
        edge_index = jax.random.randint(ks[1], (2, E), 0, N, dtype=jnp.int64)
        edge_type = jax.random.randint(ks[2], (E,), 0, 8, dtype=jnp.int64)
        edge_weight = jax.random.uniform(ks[3], (E,), dtype=jnp.float32)
        W = jax.random.normal(ks[4], (H * D, IN_DIM), dtype=jnp.float32) * (1.0 / np.sqrt(IN_DIM))
        a_src = jax.random.normal(ks[5], (H, D), dtype=jnp.float32) * (1.0 / np.sqrt(D))
        a_dst = jax.random.normal(ks[6], (H, D), dtype=jnp.float32) * (1.0 / np.sqrt(D))
        et_emb = jax.random.normal(ks[7], (8, H), dtype=jnp.float32)
        ln_gamma = jnp.ones((H * D,), dtype=jnp.float32)
        ln_beta = jnp.zeros((H * D,), dtype=jnp.float32)
        return {'x': x, 'edge_index': edge_index, 'edge_type': edge_type, 'edge_weight': edge_weight, 'W': W, 'a_src': a_src, 'a_dst': a_dst, 'et_emb': et_emb, 'ln_gamma': ln_gamma, 'ln_beta': ln_beta}
    _L2_gnn_all = _L2_gnn_setup()
    _L2_gnn_in = {k: v for k, v in _L2_gnn_all.items() if k in ('W', 'a_src', 'a_dst', 'et_emb', 'ln_gamma', 'ln_beta')}
    del _L2_gnn_all

    def _L2_ffn_setup():
        import jax, jax.numpy as jnp
        import numpy as np
        B, S, D_IN, D_OUT, K = (4, 512, 512, 512, 8)
        key = jax.random.key(seed)
        k1, k2, k3, k4 = jax.random.split(key, 4)
        scale_w = 1.0 / np.sqrt(D_IN)
        return {'x': jax.random.normal(k1, (B, S, D_IN), dtype=jnp.float32), 'expert_weights': jax.random.normal(k2, (K, D_OUT, D_IN), dtype=jnp.float32) * scale_w, 'expert_biases': jax.random.normal(k3, (K, D_OUT), dtype=jnp.float32) * 0.02, 'mixer_w': jax.random.normal(k4, (K, D_IN), dtype=jnp.float32) * scale_w, 'mixer_b': jnp.zeros((K,), dtype=jnp.float32)}
    _L2_ffn_all = _L2_ffn_setup()
    _L2_ffn_in = {k: v for k, v in _L2_ffn_all.items() if k in ('expert_weights', 'expert_biases', 'mixer_w', 'mixer_b')}
    del _L2_ffn_all

    def _L3_gnn_setup():
        import jax, jax.numpy as jnp
        import numpy as np
        N, IN_DIM, OUT_DIM, H = (1024, 512, 512, 4)
        E = 16384
        HC = H * OUT_DIM
        key = jax.random.key(seed)
        ks = jax.random.split(key, 12)
        s = 1.0 / np.sqrt(IN_DIM)
        return {'x': jax.random.normal(ks[0], (N, IN_DIM), dtype=jnp.float32), 'edge_index': jax.random.randint(ks[1], (2, E), 0, N, dtype=jnp.int64), 'Wq': jax.random.normal(ks[2], (IN_DIM, HC), dtype=jnp.float32) * s, 'bq': jnp.zeros((HC,), dtype=jnp.float32), 'Wk': jax.random.normal(ks[3], (IN_DIM, HC), dtype=jnp.float32) * s, 'bk': jnp.zeros((HC,), dtype=jnp.float32), 'Wv': jax.random.normal(ks[4], (IN_DIM, HC), dtype=jnp.float32) * s, 'bv': jnp.zeros((HC,), dtype=jnp.float32), 'Wskip': jax.random.normal(ks[5], (IN_DIM, HC), dtype=jnp.float32) * s, 'bskip': jnp.zeros((HC,), dtype=jnp.float32), 'Wlin': jax.random.normal(ks[6], (HC, OUT_DIM), dtype=jnp.float32) / np.sqrt(HC), 'blin': jnp.zeros((OUT_DIM,), dtype=jnp.float32), 'gamma': jnp.ones((OUT_DIM,), dtype=jnp.float32), 'beta': jnp.zeros((OUT_DIM,), dtype=jnp.float32)}
    _L3_gnn_all = _L3_gnn_setup()
    _L3_gnn_in = {k: v for k, v in _L3_gnn_all.items() if k in ('Wq', 'bq', 'Wk', 'bk', 'Wv', 'bv', 'Wskip', 'bskip', 'Wlin', 'blin', 'gamma', 'beta')}
    del _L3_gnn_all

    def _L3_ffn_setup():
        import jax, jax.numpy as jnp
        import numpy as np
        D_MODEL = 512
        N_HEADS = 8
        KV_OPTS = (8, 4, 1)
        D_K = D_MODEL // N_HEADS

        def gqa(x, wq, wk, wv, wo, n_kv):
            B, S, _ = x.shape
            groups = N_HEADS // n_kv
            q = (x @ wq).reshape(B, S, N_HEADS, D_K).transpose(0, 2, 1, 3)
            k = (x @ wk).reshape(B, S, n_kv, D_K).transpose(0, 2, 1, 3)
            v = (x @ wv).reshape(B, S, n_kv, D_K).transpose(0, 2, 1, 3)
            k = jnp.repeat(k, groups, axis=1)
            v = jnp.repeat(v, groups, axis=1)
            scores = jnp.einsum('bhqd,bhkd->bhqk', q, k) / jnp.sqrt(jnp.float32(D_K))
            attn = jax.nn.softmax(scores, axis=-1)
            out = jnp.einsum('bhqk,bhkd->bhqd', attn, v)
            out = out.transpose(0, 2, 1, 3).reshape(B, S, D_MODEL)
            return out @ wo
        key = jax.random.key(seed)
        ks = jax.random.split(key, 32)
        it = iter(ks)
        s = 0.02
        inp = {'x': jax.random.normal(next(it), (64, 1024, D_MODEL), dtype=jnp.float32)}
        inp['r_w1'] = jax.random.normal(next(it), (D_MODEL, D_MODEL // 4), jnp.float32) * s
        inp['r_b1'] = jnp.zeros((D_MODEL // 4,), jnp.float32)
        inp['r_w2'] = jax.random.normal(next(it), (D_MODEL // 4, len(KV_OPTS)), jnp.float32) * s
        inp['r_b2'] = jnp.zeros((len(KV_OPTS),), jnp.float32)
        for i, nkv in enumerate(KV_OPTS):
            inp[f'wq{i}'] = jax.random.normal(next(it), (D_MODEL, D_MODEL), jnp.float32) * s
            inp[f'wk{i}'] = jax.random.normal(next(it), (D_MODEL, nkv * D_K), jnp.float32) * s
            inp[f'wv{i}'] = jax.random.normal(next(it), (D_MODEL, nkv * D_K), jnp.float32) * s
            inp[f'wo{i}'] = jax.random.normal(next(it), (D_MODEL, D_MODEL), jnp.float32) * s
        return inp
    _L3_ffn_all = _L3_ffn_setup()
    _L3_ffn_in = {k: v for k, v in _L3_ffn_all.items() if k in ('r_w1', 'r_b1', 'r_w2', 'r_b2', 'wq0', 'wk0', 'wv0', 'wo0', 'wq1', 'wk1', 'wv1', 'wo1', 'wq2', 'wk2', 'wv2', 'wo2')}
    del _L3_ffn_all
    return {'x': x, 'src': src, 'dst': dst, 'edge_type_8': edge_type_8, 'edge_weight': edge_weight, 'node_vec1': node_vec1, 'L0_gnn_Wv': _L0_gnn_in['Wv'], 'L0_gnn_bv': _L0_gnn_in['bv'], 'L0_gnn_Ww': _L0_gnn_in['Ww'], 'L0_gnn_bw': _L0_gnn_in['bw'], 'L0_gnn_Wa': _L0_gnn_in['Wa'], 'L0_gnn_ba': _L0_gnn_in['ba'], 'L0_gnn_gamma': _L0_gnn_in['gamma'], 'L0_gnn_beta': _L0_gnn_in['beta'], 'L0_ffn_w_gating': _L0_ffn_in['w_gating'], 'L0_ffn_gamma': _L0_ffn_in['gamma'], 'L0_ffn_w1': _L0_ffn_in['w1'], 'L0_ffn_w2': _L0_ffn_in['w2'], 'L1_gnn_f_w1': _L1_gnn_in['f_w1'], 'L1_gnn_f_b1': _L1_gnn_in['f_b1'], 'L1_gnn_f_w2': _L1_gnn_in['f_w2'], 'L1_gnn_f_b2': _L1_gnn_in['f_b2'], 'L1_gnn_s1_w': _L1_gnn_in['s1_w'], 'L1_gnn_s1_b': _L1_gnn_in['s1_b'], 'L1_gnn_b1_w': _L1_gnn_in['b1_w'], 'L1_gnn_b1_b': _L1_gnn_in['b1_b'], 'L1_gnn_wq': _L1_gnn_in['wq'], 'L1_gnn_bq': _L1_gnn_in['bq'], 'L1_gnn_wk': _L1_gnn_in['wk'], 'L1_gnn_bk': _L1_gnn_in['bk'], 'L1_gnn_wv': _L1_gnn_in['wv'], 'L1_gnn_bv': _L1_gnn_in['bv'], 'L1_gnn_wo': _L1_gnn_in['wo'], 'L1_gnn_bo': _L1_gnn_in['bo'], 'L1_gnn_s2_w': _L1_gnn_in['s2_w'], 'L1_gnn_s2_b': _L1_gnn_in['s2_b'], 'L1_gnn_b2_w': _L1_gnn_in['b2_w'], 'L1_gnn_b2_b': _L1_gnn_in['b2_b'], 'L1_gnn_m_w1': _L1_gnn_in['m_w1'], 'L1_gnn_m_b1': _L1_gnn_in['m_b1'], 'L1_gnn_m_w2': _L1_gnn_in['m_w2'], 'L1_gnn_m_b2': _L1_gnn_in['m_b2'], 'L1_ffn_w_gating': _L1_ffn_in['w_gating'], 'L1_ffn_w1': _L1_ffn_in['w1'], 'L1_ffn_w2': _L1_ffn_in['w2'], 'L2_gnn_W': _L2_gnn_in['W'], 'L2_gnn_a_src': _L2_gnn_in['a_src'], 'L2_gnn_a_dst': _L2_gnn_in['a_dst'], 'L2_gnn_et_emb': _L2_gnn_in['et_emb'], 'L2_gnn_ln_gamma': _L2_gnn_in['ln_gamma'], 'L2_gnn_ln_beta': _L2_gnn_in['ln_beta'], 'L2_ffn_expert_weights': _L2_ffn_in['expert_weights'], 'L2_ffn_expert_biases': _L2_ffn_in['expert_biases'], 'L2_ffn_mixer_w': _L2_ffn_in['mixer_w'], 'L2_ffn_mixer_b': _L2_ffn_in['mixer_b'], 'L3_gnn_Wq': _L3_gnn_in['Wq'], 'L3_gnn_bq': _L3_gnn_in['bq'], 'L3_gnn_Wk': _L3_gnn_in['Wk'], 'L3_gnn_bk': _L3_gnn_in['bk'], 'L3_gnn_Wv': _L3_gnn_in['Wv'], 'L3_gnn_bv': _L3_gnn_in['bv'], 'L3_gnn_Wskip': _L3_gnn_in['Wskip'], 'L3_gnn_bskip': _L3_gnn_in['bskip'], 'L3_gnn_Wlin': _L3_gnn_in['Wlin'], 'L3_gnn_blin': _L3_gnn_in['blin'], 'L3_gnn_gamma': _L3_gnn_in['gamma'], 'L3_gnn_beta': _L3_gnn_in['beta'], 'L3_ffn_r_w1': _L3_ffn_in['r_w1'], 'L3_ffn_r_b1': _L3_ffn_in['r_b1'], 'L3_ffn_r_w2': _L3_ffn_in['r_w2'], 'L3_ffn_r_b2': _L3_ffn_in['r_b2'], 'L3_ffn_wq0': _L3_ffn_in['wq0'], 'L3_ffn_wk0': _L3_ffn_in['wk0'], 'L3_ffn_wv0': _L3_ffn_in['wv0'], 'L3_ffn_wo0': _L3_ffn_in['wo0'], 'L3_ffn_wq1': _L3_ffn_in['wq1'], 'L3_ffn_wk1': _L3_ffn_in['wk1'], 'L3_ffn_wv1': _L3_ffn_in['wv1'], 'L3_ffn_wo1': _L3_ffn_in['wo1'], 'L3_ffn_wq2': _L3_ffn_in['wq2'], 'L3_ffn_wk2': _L3_ffn_in['wk2'], 'L3_ffn_wv2': _L3_ffn_in['wv2'], 'L3_ffn_wo2': _L3_ffn_in['wo2']}

def reference(x, src, dst, edge_type_8, edge_weight, node_vec1, L0_gnn_Wv, L0_gnn_bv, L0_gnn_Ww, L0_gnn_bw, L0_gnn_Wa, L0_gnn_ba, L0_gnn_gamma, L0_gnn_beta, L0_ffn_w_gating, L0_ffn_gamma, L0_ffn_w1, L0_ffn_w2, L1_gnn_f_w1, L1_gnn_f_b1, L1_gnn_f_w2, L1_gnn_f_b2, L1_gnn_s1_w, L1_gnn_s1_b, L1_gnn_b1_w, L1_gnn_b1_b, L1_gnn_wq, L1_gnn_bq, L1_gnn_wk, L1_gnn_bk, L1_gnn_wv, L1_gnn_bv, L1_gnn_wo, L1_gnn_bo, L1_gnn_s2_w, L1_gnn_s2_b, L1_gnn_b2_w, L1_gnn_b2_b, L1_gnn_m_w1, L1_gnn_m_b1, L1_gnn_m_w2, L1_gnn_m_b2, L1_ffn_w_gating, L1_ffn_w1, L1_ffn_w2, L2_gnn_W, L2_gnn_a_src, L2_gnn_a_dst, L2_gnn_et_emb, L2_gnn_ln_gamma, L2_gnn_ln_beta, L2_ffn_expert_weights, L2_ffn_expert_biases, L2_ffn_mixer_w, L2_ffn_mixer_b, L3_gnn_Wq, L3_gnn_bq, L3_gnn_Wk, L3_gnn_bk, L3_gnn_Wv, L3_gnn_bv, L3_gnn_Wskip, L3_gnn_bskip, L3_gnn_Wlin, L3_gnn_blin, L3_gnn_gamma, L3_gnn_beta, L3_ffn_r_w1, L3_ffn_r_b1, L3_ffn_r_w2, L3_ffn_r_b2, L3_ffn_wq0, L3_ffn_wk0, L3_ffn_wv0, L3_ffn_wo0, L3_ffn_wq1, L3_ffn_wk1, L3_ffn_wv1, L3_ffn_wo1, L3_ffn_wq2, L3_ffn_wk2, L3_ffn_wv2, L3_ffn_wo2):
    import jax
    import jax.numpy as jnp

    def _L0_gnn_ref(x, edges, Wv, bv, Ww, bw, Wa, ba, gamma, beta):
        import jax, jax.numpy as jnp
        import numpy as np
        N = 384
        HID = 512
        H = 8
        HD = HID // H
        E = 12288
        LN_EPS = 1e-05
        residual = x
        n = x.shape[0]
        out = (x @ Wv + bv).reshape(n, H, HD).transpose(1, 0, 2)
        x1 = x[edges[0]]
        x2 = x[edges[1]]
        e = jnp.concatenate([x1, x2], axis=1) @ Ww + bw
        e = e.reshape(-1, H, 2 * HD).transpose(1, 0, 2)
        e = jax.nn.leaky_relu(e, 0.01)
        w = (e @ Wa + ba)[..., 0]
        mat = jnp.full((H, n, n), -jnp.inf, jnp.float32)
        mat = mat.at[:, edges[0], edges[1]].set(w)
        mat = jax.nn.softmax(mat, axis=-1)
        mat = jnp.nan_to_num(mat)
        y = jnp.matmul(mat, out).transpose(1, 0, 2)
        y = jax.nn.elu(y).reshape(n, HID) + residual
        mu = jnp.mean(y, axis=-1, keepdims=True)
        var = jnp.var(y, axis=-1, keepdims=True)
        y = (y - mu) / jnp.sqrt(var + LN_EPS) * gamma + beta
        return y

    def _L0_ffn_ref(x, w_gating, gamma, w1, w2):
        import jax, jax.numpy as jnp
        import numpy as np
        EPS = 1e-09
        LN_EPS = 1e-05

        def _layernorm(x, gamma):
            x = x.astype(jnp.float32)
            mu = jnp.mean(x, axis=-1, keepdims=True)
            var = jnp.var(x, axis=-1, keepdims=True)
            return (x - mu) * jax.lax.rsqrt(var + LN_EPS) * gamma
        b, n, d = x.shape
        E = w_gating.shape[-1]
        C = max(min(n, int(n * 6.0 / E)), 4)
        raw = jnp.einsum('bnd,de->bne', x, w_gating)
        probs = jax.nn.softmax(raw, axis=-1)
        gate1 = jnp.max(probs, axis=-1)
        idx1 = jnp.argmax(probs, axis=-1)
        mask1 = jax.nn.one_hot(idx1, E, dtype=jnp.float32)
        gates_wo1 = probs * (1.0 - mask1)
        gate2 = jnp.max(gates_wo1, axis=-1)
        denom = gate1 + gate2 + EPS
        gate1 = gate1 / denom
        pos1 = (jnp.cumsum(mask1, axis=-2) - mask1) * mask1
        mask1 = mask1 * (pos1 < float(C)).astype(jnp.float32)
        mask1_flat = jnp.sum(mask1, axis=-1)
        pos1_flat = jnp.sum(pos1, axis=-1).astype(jnp.int32)
        gate1 = gate1 * mask1_flat
        combine = gate1[..., None, None] * mask1_flat[..., None, None] * jax.nn.one_hot(idx1, E, dtype=jnp.float32)[..., None] * jax.nn.one_hot(pos1_flat, C, dtype=jnp.float32)[..., None, :]
        dispatch = (combine != 0).astype(jnp.float32)
        expert_in = jnp.einsum('bnd,bnec->ebcd', x, dispatch)
        xn = _layernorm(expert_in, gamma)
        hidden = jax.nn.gelu(jnp.einsum('ebcd,edh->ebch', xn, w1), approximate=False)
        expert_out = jnp.einsum('ebch,ehd->ebcd', hidden, w2)
        out = jnp.einsum('ebcd,bnec->bnd', expert_out, combine)
        return out

    def _L1_gnn_ref(latent_mesh_nodes, edge_index, noise_levels, f_w1, f_b1, f_w2, f_b2, s1_w, s1_b, b1_w, b1_b, wq, bq, wk, bk, wv, bv, wo, bo, s2_w, s2_b, b2_w, b2_b, m_w1, m_b1, m_w2, m_b2):
        import jax, jax.numpy as jnp
        import numpy as np
        N_NODES = 40962
        LATENT_DIM = 512
        N_EDGES = 81924
        NUM_BLOCKS = 4
        NUM_HEADS = 4
        NUM_FREQ = 32
        BASE_PERIOD = 16
        NOISE_EMB_DIM = 16
        EPS = 1e-05

        def _cond_layer_norm(x, cond, sw, sb, bw, bb):
            mu = jnp.mean(x, axis=-1, keepdims=True)
            var = jnp.var(x, axis=-1, keepdims=True)
            xn = (x - mu) * jax.lax.rsqrt(var + EPS)
            scale = cond @ sw + sb
            bias = cond @ bw + bb
            return xn * (1.0 + scale) + bias

        def _sparse_attention(x, src, dst, wq, bq, wk, bk, wv, bv, wo, bo):
            N, D = x.shape
            H, Dh = (NUM_HEADS, D // NUM_HEADS)
            q = (x @ wq + bq).reshape(N, H, Dh) * Dh ** (-0.5)
            k = (x @ wk + bk).reshape(N, H, Dh)
            v = (x @ wv + bv).reshape(N, H, Dh)
            scores = jnp.einsum('ehd,ehd->eh', q[src], k[dst])
            smax = jax.ops.segment_max(scores, src, num_segments=N)
            ex = jnp.exp(scores - smax[src])
            denom = jax.ops.segment_sum(ex, src, num_segments=N)
            attn = ex / denom[src]
            out = jax.ops.segment_sum(attn[:, :, None] * v[dst], src, num_segments=N)
            return out.reshape(N, D) @ wo + bo

        def _forward(x, edge_index, noise_levels, f_w1, f_b1, f_w2, f_b2, s1_w, s1_b, b1_w, b1_b, wq, bq, wk, bk, wv, bv, wo, bo, s2_w, s2_b, b2_w, b2_b, m_w1, m_b1, m_w2, m_b2):
            src, dst = (edge_index[0], edge_index[1])
            freqs = jnp.arange(1, NUM_FREQ + 1, dtype=x.dtype) * (2.0 * np.pi / BASE_PERIOD)
            ph = noise_levels * freqs
            emb = jnp.concatenate([jnp.sin(ph), jnp.cos(ph)], axis=-1)
            cond = jax.nn.silu(emb @ f_w1 + f_b1) @ f_w2 + f_b2
            for i in range(NUM_BLOCKS):
                y = _cond_layer_norm(x, cond, s1_w[i], s1_b[i], b1_w[i], b1_b[i])
                y = _sparse_attention(y, src, dst, wq[i], bq[i], wk[i], bk[i], wv[i], bv[i], wo[i], bo[i])
                x = x + y
                y = _cond_layer_norm(x, cond, s2_w[i], s2_b[i], b2_w[i], b2_b[i])
                y = jax.nn.relu(y @ m_w1[i] + m_b1[i]) @ m_w2[i] + m_b2[i]
                x = x + y
            return x
        return _forward(latent_mesh_nodes, edge_index, noise_levels, f_w1, f_b1, f_w2, f_b2, s1_w, s1_b, b1_w, b1_b, wq, bq, wk, bk, wv, bv, wo, bo, s2_w, s2_b, b2_w, b2_b, m_w1, m_b1, m_w2, m_b2)

    def _L1_ffn_ref(x, w_gating, w1, w2):
        import jax, jax.numpy as jnp
        import numpy as np
        MIN_EXPERT_CAPACITY = 4
        EPS = 1e-09
        CAPACITY_FACTOR = 2.0

        def cumsum_exclusive(t, axis):
            return jnp.cumsum(t, axis=axis) - t

        def safe_one_hot(idx, depth):
            return jax.nn.one_hot(idx, depth + 1)[..., :depth]

        def top2_gating(x, w_gating):
            b, n, d = x.shape
            e = w_gating.shape[-1]
            raw_gates = jax.nn.softmax(jnp.einsum('bnd,de->bne', x, w_gating), axis=-1)
            gate_1 = jnp.max(raw_gates, axis=-1)
            index_1 = jnp.argmax(raw_gates, axis=-1)
            mask_1 = jax.nn.one_hot(index_1, e, dtype=raw_gates.dtype)
            gates_without_top1 = raw_gates * (1.0 - mask_1)
            gate_2 = jnp.max(gates_without_top1, axis=-1)
            index_2 = jnp.argmax(gates_without_top1, axis=-1)
            mask_2 = jax.nn.one_hot(index_2, e, dtype=raw_gates.dtype)
            denom = gate_1 + gate_2 + EPS
            gate_1 = gate_1 / denom
            gate_2 = gate_2 / denom
            density_1 = jnp.mean(mask_1, axis=-2)
            density_1_proxy = jnp.mean(raw_gates, axis=-2)
            loss = jnp.mean(density_1_proxy * density_1) * float(e * e)
            capacity = max(min(n, int(n * 2 * CAPACITY_FACTOR / e)), MIN_EXPERT_CAPACITY)
            cap_f = float(capacity)
            pos1 = cumsum_exclusive(mask_1, axis=-2) * mask_1
            mask_1 = mask_1 * (pos1 < cap_f).astype(mask_1.dtype)
            mask_1_count = jnp.sum(mask_1, axis=-2, keepdims=True)
            mask_1_flat = jnp.sum(mask_1, axis=-1)
            pos1 = jnp.sum(pos1, axis=-1)
            gate_1 = gate_1 * mask_1_flat
            pos2 = (cumsum_exclusive(mask_2, axis=-2) + mask_1_count) * mask_2
            mask_2 = mask_2 * (pos2 < cap_f).astype(mask_2.dtype)
            mask_2_flat = jnp.sum(mask_2, axis=-1)
            pos2 = jnp.sum(pos2, axis=-1)
            gate_2 = gate_2 * mask_2_flat
            combine = gate_1[..., None, None] * mask_1_flat[..., None, None] * jax.nn.one_hot(index_1, e, dtype=x.dtype)[..., None] * safe_one_hot(pos1.astype(jnp.int32), capacity)[..., None, :] + gate_2[..., None, None] * mask_2_flat[..., None, None] * jax.nn.one_hot(index_2, e, dtype=x.dtype)[..., None] * safe_one_hot(pos2.astype(jnp.int32), capacity)[..., None, :]
            dispatch = (combine > 0).astype(combine.dtype)
            return (dispatch, combine, loss)
        dispatch, combine, loss = top2_gating(x, w_gating)
        expert_inputs = jnp.einsum('bnd,bnec->ebcd', x, dispatch)
        hidden = jax.nn.relu(jnp.einsum('ebcd,edh->ebch', expert_inputs, w1))
        expert_outputs = jnp.einsum('ebch,ehd->ebcd', hidden, w2)
        output = jnp.einsum('ebcd,bnec->bnd', expert_outputs, combine)
        return output

    def _L2_gnn_ref(x, edge_index, edge_type, edge_weight, W, a_src, a_dst, et_emb, ln_gamma, ln_beta):
        import jax, jax.numpy as jnp
        import numpy as np
        N, IN_DIM, H, D, E = (6250, 512, 8, 64, 100000)
        NEG_SLOPE = 0.2
        LN_EPS = 1e-05
        n, h_, d_ = (x.shape[0], a_src.shape[0], a_src.shape[1])
        h = (x @ W.T).reshape(n, h_, d_)
        src, dst = (edge_index[0], edge_index[1])
        h_src = h[src]
        e_src = jnp.einsum('ehd,hd->eh', h_src, a_src)
        e_dst = jnp.einsum('ehd,hd->eh', h[dst], a_dst)
        e = jax.nn.leaky_relu(e_src + e_dst, NEG_SLOPE)
        e = e * (1.0 + et_emb[edge_type])
        e = e * edge_weight[:, None]
        e_max = jnp.zeros((n, h_), x.dtype).at[dst].max(e)
        e = jnp.exp(e - e_max[dst])
        e_sum = jnp.zeros((n, h_), x.dtype).at[dst].add(e)
        alpha = e / (e_sum[dst] + 1e-10)
        msg = h_src * alpha[:, :, None]
        out = jnp.zeros((n, h_, d_), x.dtype).at[dst].add(msg).reshape(n, h_ * d_)
        out = out + x
        mu = jnp.mean(out, axis=-1, keepdims=True)
        var = jnp.var(out, axis=-1, keepdims=True)
        return (out - mu) / jnp.sqrt(var + LN_EPS) * ln_gamma + ln_beta

    def _L2_ffn_ref(x, expert_weights, expert_biases, mixer_w, mixer_b):
        import jax, jax.numpy as jnp
        import numpy as np
        B, S, D_IN, D_OUT, K = (4, 512, 512, 512, 8)
        logits = jnp.einsum('bsi,ki->bsk', x, mixer_w) + mixer_b
        coeffs = jax.nn.softmax(logits, axis=-1)
        expert_out = jnp.einsum('bsi,koi->bsko', x, expert_weights)
        y = jnp.einsum('bsk,bsko->bso', coeffs, expert_out)
        y = y + jnp.einsum('bsk,ko->bso', coeffs, expert_biases)
        return y

    def _L3_gnn_ref(x, edge_index, Wq, bq, Wk, bk, Wv, bv, Wskip, bskip, Wlin, blin, gamma, beta):
        import jax, jax.numpy as jnp
        import numpy as np
        N, IN_DIM, OUT_DIM, H = (1024, 512, 512, 4)
        E = 16384
        HC = H * OUT_DIM
        n = x.shape[0]
        src, dst = (edge_index[0], edge_index[1])
        q = (x @ Wq + bq).reshape(n, H, OUT_DIM)
        k = (x @ Wk + bk).reshape(n, H, OUT_DIM)
        v = (x @ Wv + bv).reshape(n, H, OUT_DIM)
        alpha = jnp.einsum('ehc,ehc->eh', q[dst], k[src]) / np.sqrt(OUT_DIM)
        amax = jax.ops.segment_max(alpha, dst, num_segments=n)
        ex = jnp.exp(alpha - amax[dst])
        denom = jax.ops.segment_sum(ex, dst, num_segments=n)
        attn = ex / denom[dst]
        msg = attn[:, :, None] * v[src]
        agg = jax.ops.segment_sum(msg, dst, num_segments=n).reshape(n, HC)
        x_attn = agg + x @ Wskip + bskip
        x_lin = x_attn @ Wlin + blin
        h = x_lin + x_attn[:, :OUT_DIM]
        mu = jnp.mean(h, axis=-1, keepdims=True)
        var = jnp.mean((h - mu) ** 2, axis=-1, keepdims=True)
        return gamma * (h - mu) / jnp.sqrt(var + 1e-05) + beta

    def _L3_ffn_ref(x, r_w1, r_b1, r_w2, r_b2, wq0, wk0, wv0, wo0, wq1, wk1, wv1, wo1, wq2, wk2, wv2, wo2):
        import jax, jax.numpy as jnp
        import numpy as np
        D_MODEL = 512
        N_HEADS = 8
        KV_OPTS = (8, 4, 1)
        D_K = D_MODEL // N_HEADS

        def gqa(x, wq, wk, wv, wo, n_kv):
            B, S, _ = x.shape
            groups = N_HEADS // n_kv
            q = (x @ wq).reshape(B, S, N_HEADS, D_K).transpose(0, 2, 1, 3)
            k = (x @ wk).reshape(B, S, n_kv, D_K).transpose(0, 2, 1, 3)
            v = (x @ wv).reshape(B, S, n_kv, D_K).transpose(0, 2, 1, 3)
            k = jnp.repeat(k, groups, axis=1)
            v = jnp.repeat(v, groups, axis=1)
            scores = jnp.einsum('bhqd,bhkd->bhqk', q, k) / jnp.sqrt(jnp.float32(D_K))
            attn = jax.nn.softmax(scores, axis=-1)
            out = jnp.einsum('bhqk,bhkd->bhqd', attn, v)
            out = out.transpose(0, 2, 1, 3).reshape(B, S, D_MODEL)
            return out @ wo
        routing_input = x.mean(axis=1)
        logits = jax.nn.relu(routing_input @ r_w1 + r_b1) @ r_w2 + r_b2
        sel = jnp.argmax(jax.nn.softmax(logits, axis=-1), axis=-1)
        params = [(wq0, wk0, wv0, wo0), (wq1, wk1, wv1, wo1), (wq2, wk2, wv2, wo2)]
        out = jnp.zeros_like(x)
        for i, nkv in enumerate(KV_OPTS):
            yi = gqa(x, *params[i], nkv)
            mask = (sel == i)[:, None, None]
            out = jnp.where(mask, yi, out)
        return out
    edge_index = jnp.stack([src, dst])
    x = x + _L0_gnn_ref(_layernorm(x, axis=-1), edge_index, L0_gnn_Wv, L0_gnn_bv, L0_gnn_Ww, L0_gnn_bw, L0_gnn_Wa, L0_gnn_ba, L0_gnn_gamma, L0_gnn_beta)
    x = x + _L0_ffn_ref(_layernorm(x, axis=-1)[None], L0_ffn_w_gating, L0_ffn_gamma, L0_ffn_w1, L0_ffn_w2)[0]
    x = x + _L1_gnn_ref(_layernorm(x, axis=-1), edge_index, node_vec1, L1_gnn_f_w1, L1_gnn_f_b1, L1_gnn_f_w2, L1_gnn_f_b2, L1_gnn_s1_w, L1_gnn_s1_b, L1_gnn_b1_w, L1_gnn_b1_b, L1_gnn_wq, L1_gnn_bq, L1_gnn_wk, L1_gnn_bk, L1_gnn_wv, L1_gnn_bv, L1_gnn_wo, L1_gnn_bo, L1_gnn_s2_w, L1_gnn_s2_b, L1_gnn_b2_w, L1_gnn_b2_b, L1_gnn_m_w1, L1_gnn_m_b1, L1_gnn_m_w2, L1_gnn_m_b2)
    x = x + _L1_ffn_ref(_layernorm(x, axis=-1)[None], L1_ffn_w_gating, L1_ffn_w1, L1_ffn_w2)[0]
    x = x + _L2_gnn_ref(_layernorm(x, axis=-1), edge_index, edge_type_8, edge_weight, L2_gnn_W, L2_gnn_a_src, L2_gnn_a_dst, L2_gnn_et_emb, L2_gnn_ln_gamma, L2_gnn_ln_beta)
    x = x + _L2_ffn_ref(_layernorm(x, axis=-1)[None], L2_ffn_expert_weights, L2_ffn_expert_biases, L2_ffn_mixer_w, L2_ffn_mixer_b)[0]
    x = x + _L3_gnn_ref(_layernorm(x, axis=-1), edge_index, L3_gnn_Wq, L3_gnn_bq, L3_gnn_Wk, L3_gnn_bk, L3_gnn_Wv, L3_gnn_bv, L3_gnn_Wskip, L3_gnn_bskip, L3_gnn_Wlin, L3_gnn_blin, L3_gnn_gamma, L3_gnn_beta)
    x = x + _L3_ffn_ref(_layernorm(x, axis=-1)[None], L3_ffn_r_w1, L3_ffn_r_b1, L3_ffn_r_w2, L3_ffn_r_b2, L3_ffn_wq0, L3_ffn_wk0, L3_ffn_wv0, L3_ffn_wo0, L3_ffn_wq1, L3_ffn_wk1, L3_ffn_wv1, L3_ffn_wo1, L3_ffn_wq2, L3_ffn_wk2, L3_ffn_wv2, L3_ffn_wo2)[0]
    return x

_drawn_inputs = setup_inputs


def setup_inputs(seed=0):
    import zlib

    import numpy as np

    out = dict(_drawn_inputs(seed))
    spreads = {'L0_gnn_gamma': (1.0, 0.2),
     'L0_gnn_beta': (0.0, 0.1),
     'L0_ffn_gamma': (1.0, 0.2),
     'L1_gnn_f_b1': (0.0, 0.8),
     'L1_gnn_f_b2': (0.0, 0.8),
     'L1_gnn_s1_b': (0.0, 0.74),
     'L1_gnn_b1_b': (0.0, 0.1),
     'L1_gnn_bq': (0.0, 0.8),
     'L1_gnn_bk': (0.0, 0.8),
     'L1_gnn_bv': (0.0, 0.1),
     'L1_gnn_bo': (0.0, 0.1),
     'L1_gnn_s2_b': (0.0, 0.47),
     'L1_gnn_b2_b': (0.0, 0.388),
     'L1_gnn_m_b1': (0.0, 0.1),
     'L1_gnn_m_b2': (0.0, 0.1),
     'L2_gnn_ln_gamma': (1.0, 0.2),
     'L2_gnn_ln_beta': (0.0, 0.297),
     'L2_ffn_mixer_b': (0.0, 0.8),
     'L3_gnn_bq': (0.0, 0.8),
     'L3_gnn_bk': (0.0, 0.8),
     'L3_gnn_bv': (0.0, 0.371),
     'L3_gnn_bskip': (0.0, 0.318),
     'L3_gnn_blin': (0.0, 0.499),
     'L3_gnn_gamma': (1.0, 0.2),
     'L3_gnn_beta': (0.0, 0.335),
     'L3_ffn_r_b1': (0.0, 0.1),
     'L3_ffn_r_b2': (0.0, 0.724)}
    factors = {'node_vec1': 8.0,
     'L0_gnn_bv': 3.137,
     'L0_gnn_Ww': 4.783,
     'L0_gnn_bw': 8.0,
     'L0_gnn_Wa': 5.091,
     'L1_gnn_f_w1': 8.0,
     'L1_gnn_f_w2': 8.0,
     'L1_gnn_s1_w': 8.0,
     'L1_gnn_b1_w': 8.0,
     'L1_gnn_wq': 4.354,
     'L1_gnn_wk': 4.534,
     'L1_gnn_s2_w': 8.0,
     'L1_gnn_b2_w': 8.0,
     'L2_ffn_expert_biases': 8.0,
     'L3_ffn_wq2': 8.0,
     'L3_ffn_wk2': 8.0,
     'L3_ffn_wv2': 8.0,
     'L3_ffn_wo2': 7.384}
    for name, (base, spread) in spreads.items():
        noise = np.random.default_rng([zlib.crc32(name.encode()), seed]).standard_normal(out[name].shape)
        drawn = base * np.exp(spread * noise) if base else spread * noise
        out[name] = jnp.asarray(drawn.astype(out[name].dtype))
    for name, factor in factors.items():
        out[name] = (out[name] * factor).astype(out[name].dtype)
    return out
```

```python
from contextlib import ExitStack, contextmanager

import concourse.bass as bass
from concourse import mybir

P = 128
N = 384
NT = N // P
D = 512
KC = D // P
E = 12288
ET = E // P
H8 = 8
HD = D // H8
EPS = 1e-5
MASKED = -1.0e30
SLOTS = 8
NB = 8
F32 = mybir.dt.float32
BF16 = mybir.dt.bfloat16
I32 = mybir.dt.int32
U32 = mybir.dt.uint32
ALU = mybir.AluOpType
ACT = mybir.ActivationFunctionType
AX = mybir.AxisListType.X


class Banks:

    def __init__(self, psum, full, free):
        self.psum, self.full, self.free = psum, full, free
        self.uses, self.at, self.jobs, self.per = [0] * NB, 0, {}, None

    def open(self, pe, name, i=None):
        b = self.at
        self.at = (b + 1) % NB
        before, coef = self.uses[b], (self.per[b] if self.per else 0)
        self.uses[b] += 1
        self.jobs[name] = (b, before, coef)
        if before > 0:
            pe.wait_ge(self.free[b], before + i * coef if coef else before)
        return self.psum[:, b, :]

    @contextmanager
    def loop(self, trips, jobs):
        start, first = list(self.uses), self.at
        self.per = [sum((first + j) % NB == b for j in range(jobs)) for b in range(NB)]
        yield
        done = [u - s for u, s in zip(self.uses, start)]
        assert done == self.per, (sum(done), jobs)
        self.uses = [s + trips * k for s, k in zip(start, self.per)]
        self.per = None

    def count(self, name, i):
        b, before, coef = self.jobs[name]
        return b, (before + 1 + i * coef if coef and i is not None else before + 1)

    def full_of(self, name):
        return self.full[self.jobs[name][0]]

    def free_of(self, name):
        return self.free[self.jobs[name][0]]

    def filled(self, eng, name, i=None):
        b, n = self.count(name, i)
        eng.wait_ge(self.full[b], n)
        return self.psum[:, b, :]

    def drained(self, eng, name, i=None):
        b, n = self.count(name, i)
        eng.wait_ge(self.free[b], n)


class Order:

    def __init__(self, eng, sem):
        self.eng, self.sem, self.n, self.more, self.looping = eng, sem, 0, 0, False

    def link(self, ins):
        self.n += 1
        ins.then_inc(self.sem, 1)
        self.eng.wait_ge(self.sem, self.n + self.more)

    def settle(self):
        if self.looping:
            self.eng.nop(nofuse=True)

    @contextmanager
    def loop(self, trips, per):
        start, self.looping = self.n, True
        with self.eng.Fori(0, trips) as i:
            self.more = i * per
            yield i
        assert self.n - start == per, (self.n - start, per)
        self.n, self.more, self.looping = start + trips * per, 0, False


class Ring:

    def __init__(self, slots, arrived):
        self.slots, self.arrived = slots, arrived
        self.got, self.per = [0] * SLOTS, None
        self.last = [None] * SLOTS

    def slot(self, s):
        return self.slots[:, s, :, :]

    def get(self, pe, s, i=None):
        self.got[s] += 1
        n = 16 * self.got[s]
        pe.wait_ge(self.arrived[s], n if i is None else n + i * 16)
        return self.slot(s)

    def after_loop(self, slots, trips):
        for s in slots:
            self.got[s] += trips - 1

    def load(self, sp, banks, s, pairs, used=None, i=None):
        job = used if used is not None else self.last[s]
        if job is not None:
            banks.filled(sp, *job)
            if used is not None:
                sp.nop(nofuse=True)
        assert len(pairs) == 1
        for dst, src in pairs:
            sp.dma_start(dst, src).then_inc(self.arrived[s], 16)


def gnn_ffn_program(nc, A, out):
    ctx = ExitStack()
    with ctx:
        def sb(name, shape, dt=F32):
            return ctx.enter_context(nc.sbuf_tensor(name, shape, dt))

        def sem(name):
            return ctx.enter_context(nc.semaphore(name))

        def sems(name, n):
            return [sem(f"{name}{i}") for i in range(n)]

        def dram(name, shape):
            return nc.dram_tensor(name, shape, F32, kind="Internal").ap()

        psum = ctx.enter_context(nc.psum_tensor("psum", [P, NB, 512], F32))
        banks = Banks(psum, sems("bank_full", NB), sems("bank_free", NB))
        ring = Ring(sb("ring", [P, SLOTS, KC, D]), sems("slot_arrived", SLOTS))

        x = sb("x", [P, NT, D])
        xn = sb("xn", [P, NT, D])
        xT = sb("xT", [P, KC, N])
        xn2 = sb("xn2", [P, NT, D])
        xT2 = sb("xT2", [P, KC, N])
        cnt_src = sb("cnt_src", [P, NT, N])
        cnt_dst = sb("cnt_dst", [P, NT, N])
        mask_src = sb("mask_src", [P, NT, N])
        mask_dst = sb("mask_dst", [P, NT, N])
        ident = sb("ident", [P, P])
        tri = sb("tri", [P, P])
        ones = sb("ones", [P, P])
        zeros = sb("zeros", [P, 512])
        iota = sb("iota", [P, N])
        iota_back = sb("iota_back", [P, 16])
        src_i = sb("src_i", [P, ET], I32)
        dst_i = sb("dst_i", [P, ET], I32)
        typ_i = sb("typ_i", [P, ET], I32)
        src_f = sb("src_f", [P, ET])
        dst_f = sb("dst_f", [P, ET])
        typ_f = sb("typ_f", [P, ET])
        ew = sb("ew", [P, ET])
        stats = sb("stats", [P, NT, 6])
        mv = sb("mv", [P, NT, 2])
        vare = sb("vare", [P, NT])
        std = sb("std", [P, NT])
        rstd = sb("rstd", [P, NT])
        gate = sb("gate", [P, 16, 64])
        idx = sb("idx", [P, 4, 1], I32)

        cols = sb("cols", [P, 160])
        rows = sb("rows", [1, 1536])
        bc = sb("bc", [P, 7, D])
        small = sb("small", [P, 512])
        blk_rows = sb("blk_rows", [1, 3, D])
        AW = 13400
        arena = sb("arena", [P, AW])

        def view(off, *shape):
            n = 1
            for s in shape:
                n *= s
            assert off + n <= AW, (off, n)
            v = arena[:, off:off + n]
            if len(shape) == 2:
                v = v.rearrange("p (a b) -> p a b", a=shape[0])
            elif len(shape) == 3:
                v = v.rearrange("p (a b c) -> p a b c", a=shape[0], b=shape[1])
            return v

        params = sem("params")
        x_loaded = sem("x_loaded")
        edges_loaded = sem("edges_loaded")
        consts_ready = sem("consts_ready")
        pool_order = sem("pool_order")
        dve_order = sem("dve_order")
        act_order = sem("act_order")
        var_ready = sem("var_ready")
        std_ready = sem("std_ready")
        xn_ready = sem("xn_ready")
        hot_ready = sem("hot_ready")
        hot_used = sem("hot_used")
        mask_done = sem("mask_done")
        logits_ready = sem("logits_ready")
        gate_exp = sem("gate_exp")
        tables_stored = sem("tables_stored")
        rows_landed = sems("rows_landed", 2)
        cols_landed = sems("cols_landed", 2)
        edge_free = sem("edge_free")
        z_ready = sem("z_ready")
        lrelu_done = sem("lrelu_done")
        scores_max = sem("scores_max")
        max_ready = sem("max_ready")
        max_stored = sem("max_stored")
        diff_ready = sem("diff_ready")
        ex_done = sem("ex_done")
        msg_free = sem("msg_free")
        msg_ready = sem("msg_ready")
        msg_used = sem("msg_used")
        elu_in = sem("elu_in")
        elu_exp = sem("elu_exp")
        mod_ready = sem("mod_ready")
        t_ready = sem("t_ready")
        e_done = sem("e_done")
        p_ready = sem("p_ready")
        step_ready = sem("step_ready")
        pe_col = sem("pe_col")
        out_ready = sem("out_ready")
        stored = sem("stored")

        bc0 = 10336
        loads = []

        def col(name, n, p=P, off=[0]):
            o = off[0]
            off[0] += n
            loads.append((cols[0:p, o:o + n], A[name], n, p))
            return cols[0:p, o:o + n]

        c_s1b = col("L1_gnn_s1_b", 16)
        c_b1b = col("L1_gnn_b1_b", 16)
        c_bq = col("L1_gnn_bq", 16)
        c_bk = col("L1_gnn_bk", 16)
        c_s2b = col("L1_gnn_s2_b", 16)
        c_b2b = col("L1_gnn_b2_b", 16)
        c_mb1 = col("L1_gnn_m_b1", 16)
        c_bq3 = col("L3_gnn_bq", 16)
        c_bk3 = col("L3_gnn_bk", 16)
        c_bs3 = col("L3_gnn_bskip", 16)
        loads = [(d, (s.rearrange("b (c p) -> p (b c)", p=P) if len(s.shape) == 2 else s.rearrange("(c p) -> p c", p=P)))
                 for d, s, n, p in loads]
        c_g0 = small[:, 0:4]
        loads.append((c_g0, A["L0_ffn_gamma"].rearrange("(c p) -> p c", p=P)))
        c_fb1, c_fb2 = small[0:16, 4:5], small[0:16, 5:6]
        loads.append((c_fb1, A["L1_gnn_f_b1"].unsqueeze(1)))
        loads.append((c_fb2, A["L1_gnn_f_b2"].unsqueeze(1)))
        c_rb1 = small[:, 6:7]
        loads.append((c_rb1, A["L3_ffn_r_b1"].unsqueeze(1)))
        r_rb2 = small[0:1, 7:10]
        loads.append((r_rb2, A["L3_ffn_r_b2"].unsqueeze(0)))
        ba0 = small[:, 10:11]
        loads.append((ba0, A["L0_gnn_ba"].partition_broadcast(P)))
        r_mixb = small[0:1, 12:20]
        loads.append((r_mixb, A["L2_ffn_mixer_b"].unsqueeze(0)))
        et_bc = small[:, 20:84]
        loads.append((et_bc, A["L2_gnn_et_emb"].rearrange("a b -> (a b)").partition_broadcast(P)))
        wg0 = small[:, 84:108].rearrange("p (c e) -> p c e", c=KC)
        loads.append((wg0, A["L0_ffn_w_gating"].rearrange("(c p) e -> p c e", p=P)))
        wg1 = small[:, 108:172].rearrange("p (c e) -> p c e", c=KC)
        loads.append((wg1, A["L1_ffn_w_gating"].rearrange("(c p) e -> p c e", p=P)))
        fw1 = small[0:64, 172:188]
        loads.append((fw1, A["L1_gnn_f_w1"]))
        fw2 = small[0:16, 188:204]
        loads.append((fw2, A["L1_gnn_f_w2"]))
        rw2 = small[:, 204:207]
        loads.append((rw2, A["L3_ffn_r_w2"]))
        mixT = small[:, 208:240].rearrange("p (c e) -> p c e", c=KC)
        wa = small[:, 240:368]
        loads.append((wa, A["L0_gnn_Wa"].rearrange("d a -> (a d)").partition_broadcast(P)))
        r_bw = rows[0:1, 0:1024]
        loads.append((r_bw, A["L0_gnn_bw"].unsqueeze(0)))
        r_bv0 = rows[0:1, 1024:1536]
        loads.append((r_bv0, A["L0_gnn_bv"].unsqueeze(0)))
        BC = {}
        for j, nm in enumerate(("L2_gnn_a_src", "L2_gnn_a_dst", "L2_gnn_ln_gamma", "L2_gnn_ln_beta", "L3_gnn_gamma",
                                "L3_gnn_beta", "L3_gnn_blin")):
            a = A[nm]
            BC[nm] = bc[:, j, :]
            loads.append((bc[:, j, :], (a.rearrange("a b -> (a b)") if len(a.shape) == 2 else a).partition_broadcast(P)))
        BC["L0_gnn_gamma"], BC["L0_gnn_beta"] = view(bc0, D), view(bc0 + D, D)
        for nm in ("L0_gnn_gamma", "L0_gnn_beta"):
            loads.append((BC[nm], A[nm].partition_broadcast(P)))
        PARAMS = 16 * len(loads)

        tab_u = dram("tab_u", (N, 1024 + N))
        tab_v = dram("tab_v", (N, 1024))
        tab_o = dram("tab_o", (N, D))
        tab_m = dram("tab_m", (N, H8))
        tab_h = dram("tab_h", (N, D))
        tab_es = dram("tab_es", (N, H8))
        tab_ed = dram("tab_ed", (N, H8))
        tab_m2 = dram("tab_m2", (N, H8))

        def tiled(t):
            return t.rearrange("(c p) n -> p c n", p=P)

        def mm(o, a, b, start, stop):
            return nc.tensor.matmul(o, a, b, start=start, stop=stop)

        def pe_transpose(pe, tag, src, i=None):
            for c in range(KC):
                b = banks.open(pe, f"{tag}{c}", i)
                for t in range(NT):
                    last = nc.tensor.transpose(b[:, t * P:(t + 1) * P], src[:, t, c * P:(c + 1) * P], ident[:])
                last.then_inc(banks.full_of(f"{tag}{c}"), 1)

        def act_copy(act, name, dst, w=512, i=None):
            b = banks.filled(act, name, i)
            nc.scalar.activation(dst, b[:, 0:w], ACT.Copy).then_inc(banks.free_of(name), 1)

        def act_transposed(act, tag, dst, i=None):
            for c in range(KC):
                act_copy(act, f"{tag}{c}", dst[:, c, :], N, i)

        def pe_rows(pe, name, aT, w, t, bias=None, i=None, col0=0, n=D):
            b = banks.open(pe, name, i)
            for c in range(KC):
                last = mm(b[:, 0:n], aT[:, c, t * P:(t + 1) * P], w[:, c, col0:col0 + n], c == 0,
                          c == KC - 1 and bias is None)
            if bias is not None:
                last = mm(b[:, 0:n], ones[0:1, :], bias, False, True)
            last.then_inc(banks.full_of(name), 1)

        def pe_cols(pe, name, aT, w, col0, i=None):
            b = banks.open(pe, name, i)
            for c in range(KC):
                last = mm(b[:, 0:N], w[:, c, col0:col0 + P], aT[:, c, :], c == 0, c == KC - 1)
            last.then_inc(banks.full_of(name), 1)

        def dve_norm(dve, od, call, src, dst, gamma=None, beta=None):
            od.settle()
            for t in range(NT):
                last = nc.vector.bn_stats(stats[:, t, :], src[:, t, :])
            od.link(last)
            od.settle()
            for t in range(NT):
                last = nc.vector.bn_aggr(mv[:, t, :], stats[:, t, :])
            od.link(last)
            nc.vector.tensor_scalar_add(vare[:], mv[:, :, 1], EPS).then_inc(var_ready, 1)
            dve.wait_ge(std_ready, call + 1)
            od.link(nc.vector.reciprocal(rstd[:], std[:]))
            for t in range(NT):
                last = nc.vector.tensor_scalar(dst[:, t, :], src[:, t, :], mv[:, t, 0:1], rstd[:, t:t + 1],
                                               ALU.subtract, ALU.mult)
            if gamma is not None:
                od.link(last)
                for t in range(NT):
                    last = nc.vector.tensor_tensor(dst[:, t, :], dst[:, t, :], gamma, ALU.mult)
            if beta is not None:
                od.link(last)
                for t in range(NT):
                    last = nc.vector.tensor_tensor(dst[:, t, :], dst[:, t, :], beta, ALU.add)
            last.then_inc(xn_ready, 1)

        def act_norm(act, call):
            act.wait_ge(var_ready, call + 1)
            nc.scalar.activation(std[:], vare[:], ACT.Sqrt).then_inc(std_ready, 1)

        def dve_softmax_logits(dve, od, name, e, call):
            b = banks.filled(dve, name)[:, 0:NT * e].rearrange("p (t e) -> p t e", t=NT)
            pr, mx = g3(0, e), gate[:, 1, 0:NT]
            od.link(nc.vector.tensor_reduce(mx, b, AX, ALU.max))
            nc.vector.tensor_tensor(g3(2, e), b, mx.unsqueeze(2).broadcast_to([P, NT, e]),
                                    ALU.subtract).then_inc(banks.free_of(name), 1)
            dve.wait_ge(gate_exp, call + 1)
            od.link(nc.vector.tensor_reduce(gate[:, 1, 8:8 + NT], pr, AX, ALU.add))
            od.link(nc.vector.reciprocal(gate[:, 1, 16:16 + NT], gate[:, 1, 8:8 + NT]))
            od.link(nc.vector.tensor_tensor(pr, pr, gate[:, 1, 16:16 + NT].unsqueeze(2).broadcast_to([P, NT, e]), ALU.mult))

        def act_softmax_logits(act, name, e):
            banks.drained(act, name)
            nc.scalar.activation(g3(0, e), g3(2, e), ACT.Exp).then_inc(gate_exp, 1)

        def g3(j, e):
            return gate[:, j, 0:NT * e].rearrange("p (t e) -> p t e", t=NT)

        def dve_top1(od, pr, e, g, onehot, tmp):
            od.link(nc.vector.tensor_reduce(g, pr, AX, ALU.max))
            od.link(nc.vector.tensor_tensor(tmp, pr, g.unsqueeze(2).broadcast_to([P, NT, e]), ALU.is_equal))
            back = iota_back[:, 0:e].unsqueeze(1).broadcast_to([P, NT, e])
            od.link(nc.vector.tensor_tensor(tmp, tmp, back, ALU.mult))
            first = gate[:, 3, 0:NT]
            od.link(nc.vector.tensor_reduce(first, tmp, AX, ALU.min))
            od.link(nc.vector.tensor_tensor(onehot, back, first.unsqueeze(2).broadcast_to([P, NT, e]), ALU.is_equal))

        def pe_logits(pe, name, aT, w, e, bias=None):
            b = banks.open(pe, name)
            for t in range(NT):
                for c in range(KC):
                    last = mm(b[:, t * e:(t + 1) * e], aT[:, c, t * P:(t + 1) * P], w[:, c, :], c == 0,
                              c == KC - 1 and bias is None)
                if bias is not None:
                    last = mm(b[:, t * e:(t + 1) * e], ones[0:1, :], bias, False, True)
            last.then_inc(banks.full_of(name), 1)

        probs = view(AW - 4 * NT * N, 2, NT, N)
        probsT = view(AW - 2 * NT * N, 2, NT, N)
        amax = sb("amax", [P, 2, NT])
        asum = sb("asum", [P, 2, NT])

        def dve_att_scores(dve, od, tag, u, g, par, scale, mask, i):
            for t in range(NT):
                b = banks.filled(dve, f"{tag}s{t}", i)
                if mask is not None:
                    last = nc.vector.scalar_tensor_tensor(out=probs[:, par, t, :], in0=b[:, 0:N], scalar=scale,
                                                          in1=mask[:, t, :], op0=ALU.mult, op1=ALU.add)
                else:
                    last = nc.vector.tensor_scalar(probs[:, par, t, :], b[:, 0:N], scale, None, ALU.mult)
                last.then_inc(banks.free_of(f"{tag}s{t}"), 1)
            for t in range(NT):
                banks.drained(dve, f"{tag}s{t}", i)
            od.link(nc.vector.tensor_reduce(amax[:, par, :], probs[:, par, :, :], AX, ALU.max))
            nc.vector.tensor_scalar(amax[:, par, :], amax[:, par, :], -1.0, None, ALU.mult).then_inc(t_ready, 1)

        def act_att_exp(act, u, par):
            act.wait_ge(t_ready, u + 1)
            for t in range(NT):
                last = nc.scalar.activation(probs[:, par, t, :], probs[:, par, t, :], ACT.Exp, bias=amax[:, par, t:t + 1])
            last.then_inc(e_done, 1)

        def dve_att_probs(dve, od, u, par, count):
            dve.wait_ge(e_done, u + 1)
            pv = probs[:, par, :, :]
            if count is not None:
                od.link(nc.vector.tensor_tensor(pv, pv, count[:], ALU.mult))
            od.link(nc.vector.tensor_reduce(asum[:, par, :], pv, AX, ALU.add))
            od.link(nc.vector.tensor_scalar_max(asum[:, par, :], asum[:, par, :], 1.0e-30))
            od.link(nc.vector.reciprocal(asum[:, par, :], asum[:, par, :]))
            nc.vector.tensor_tensor(pv, pv, asum[:, par, :].unsqueeze(2).broadcast_to([P, NT, N]),
                                    ALU.mult).then_inc(p_ready, 1)

        def pe_att_transpose(pe, tag, u, par, i):
            pe.wait_ge(p_ready, u + 1)
            for c in range(NT):
                b = banks.open(pe, f"{tag}p{c}", i)
                for t in range(NT):
                    last = nc.tensor.transpose(b[:, t * P:(t + 1) * P], probs[:, par, t, c * P:(c + 1) * P], ident[:])
                last.then_inc(banks.full_of(f"{tag}p{c}"), 1)

        def act_att_transposed(act, tag, par, i):
            for c in range(NT):
                act_copy(act, f"{tag}p{c}", probsT[:, par, c, :], N, i)

        gbuf_u = view(0, 2, 1024 + N)
        gbuf_v = view(2816, 2, 1024)
        seg_max = view(4864, H8, N)
        w_edge = view(7936, ET, H8)
        cnt_edge = view(8704, ET)
        hot = view(8800, 2, N)
        neg = view(9568, 2, N)
        seg_node = view(bc0 + 2 * D, NT, H8)
        hotb = arena[:, 0:768].bitcast(BF16).rearrange("p (b k n) -> p b k n", b=2, k=2)
        ust = view(0, NT, 1024 + N)
        vst = view(4864, NT, 1024)
        ost = view(4864 + 3072, NT, D)
        go = view(0, 2, D)
        gm = view(1024, 2, H8)
        ex = view(1040, 2, H8)
        msg = view(1100, 2, 2, 264)

        def dve_segment_max(od, key, t, b):
            for h in range(H8):
                last = nc.vector.scalar_tensor_tensor(out=seg_max[:, h, :], in0=neg[:, b, :],
                                                      scalar=w_edge[:, bass.ds(t, 1), h], in1=seg_max[:, h, :],
                                                      op0=ALU.add, op1=ALU.max)
            return last

        def pe_segment_max(pe, tag):
            for j in range(6):
                b = banks.open(pe, f"{tag}m{j}")
                for q in range(4):
                    c, h = (4 * j + q) // H8, (4 * j + q) % H8
                    last = nc.tensor.transpose(b[:, q * P:(q + 1) * P], seg_max[:, h, c * P:(c + 1) * P], ident[:])
                last.then_inc(banks.full_of(f"{tag}m{j}"), 1)

        def dve_segment_node(dve, tag):
            for j in range(6):
                b = banks.filled(dve, f"{tag}m{j}")
                flat = seg_node[:].rearrange("p c h -> p (c h)")[:, 4 * j:4 * j + 4]
                nc.vector.tensor_reduce(flat, b.rearrange("p (q l) -> p q l", q=4), AX,
                                        ALU.max).then_inc(banks.free_of(f"{tag}m{j}"), 1)

        def pool_gather(o, table, column):
            return nc.gpsimd.indirect_dma_start(o, None, table, bass.IndirectOffsetOnAxis(ap=column.bitcast(U32), axis=0))

        def pool_scatter_rows(pool, op, val_idx, table, key_idx, maxima, first):
            with op.loop(ET // 2, 2) as i:
                for b in range(2):
                    t = 2 * i + b
                    pool.wait_ge(msg_free, t + 1 + first)
                    nc.gpsimd.tensor_copy(idx[:, 2 * b, :], val_idx[:, bass.ds(t, 1)])
                    op.link(nc.gpsimd.tensor_copy(idx[:, 2 * b + 1, :], key_idx[:, bass.ds(t, 1)]))
                    pool.nop(nofuse=True)
                    pool_gather(go[:, b, :], table, idx[:, 2 * b, :]).then_inc(rows_landed[b], 16)
                    pool_gather(gm[:, b, :], maxima, idx[:, 2 * b + 1, :]).then_inc(cols_landed[b], 16)

        def act_scatter_rows(act, tiles_before):
            with act.Fori(0, ET // 2) as i:
                for b in range(2):
                    act.wait_ge(diff_ready, 2 * i + b + 1 + tiles_before)
                    nc.scalar.activation(ex[:, b, :], gm[:, b, :], ACT.Exp).then_inc(ex_done, 1)

        def pe_scatter_rows(pe, tag, tiles_before):
            bk = [[banks.open(pe, f"{tag}a{c}{hf}") for hf in range(2)] for c in range(NT)]
            for c in range(NT):
                for hf in range(2):
                    last = mm(bk[c][hf][:, 0:264], zeros[:, 0:P], zeros[:, 0:264], True, False)
            last.then_inc(msg_used, 2)
            with pe.Fori(0, ET // 2) as i:
                for b in range(2):
                    pe.wait_ge(msg_ready, 2 * i + b + 1 + tiles_before)
                    for c in range(NT):
                        for hf in range(2):
                            last = mm(bk[c][hf][:, 0:264], hot[:, b, c * P:(c + 1) * P], msg[:, b, hf, :], False, False)
                    last.then_inc(msg_used, 1)
            for c in range(NT):
                for hf in range(2):
                    mm(bk[c][hf][:, 0:264], zeros[:, 0:P], zeros[:, 0:264], False, True).then_inc(
                        banks.full_of(f"{tag}a{c}{hf}"), 1)

        def dve_scatter_sums(dve, od, tag, tiny, add):
            for c in range(NT):
                for hf in range(2):
                    b = banks.filled(dve, f"{tag}a{c}{hf}")
                    den = gate[:, 4, 8 * (2 * c + hf):8 * (2 * c + hf) + 8]
                    od.link(nc.vector.tensor_scalar(den, b[:, 256:264], tiny, None, ALU.add if add else ALU.max))
                    od.link(nc.vector.reciprocal(den, den))
                    nc.vector.tensor_tensor(
                        xn2[:, c, hf * 256:hf * 256 + 256].rearrange("p (h d) -> p h d", h=4),
                        b[:, 0:256].rearrange("p (h d) -> p h d", h=4),
                        den[:, hf * 4:hf * 4 + 4].unsqueeze(2).broadcast_to([P, 4, HD]),
                        ALU.mult).then_inc(banks.free_of(f"{tag}a{c}{hf}"), 1)
            for c in range(NT):
                for hf in range(2):
                    banks.drained(dve, f"{tag}a{c}{hf}")

        layers = {"sp": [], "act": [], "dve": [], "pe": [], "pool": []}

        def on(engine):
            def add(f):
                layers[engine].append(f)
                return f
            return add

        NORM = dict(l0=0, l0b=1, f0=2, f0b=3, l1=4, blk=5, f1=13, l2=14, l2b=15, f2=16, l3=17, l3b=18, f3=19)

        @on("sp")
        def _(sp, o):
            sp.dma_start(x[:], tiled(A["x"])).then_inc(x_loaded, 16)
            for dst, nm in ((src_i, "src"), (dst_i, "dst"), (typ_i, "edge_type_8"), (ew, "edge_weight")):
                sp.dma_start(dst[:], A[nm].rearrange("(p t) -> p t", p=P)).then_inc(edges_loaded, 16)

        @on("act")
        def _(act, o):
            for dst, src in loads:
                act.dma_start(dst, src).then_inc(params, 16)

        @on("pool")
        def _(pool, op):
            nc.gpsimd.memset(ident[:], 0.0)
            nc.gpsimd.memset(ones[:], 1.0)
            nc.gpsimd.memset(zeros[:], 0.0)
            nc.gpsimd.iota(iota[:], pattern=[[1, N]], base=0, channel_multiplier=0, allow_small_or_imprecise_dtypes=True)
            op.link(nc.gpsimd.iota(iota_back[:], pattern=[[1, 16]], base=-64, channel_multiplier=0,
                                   allow_small_or_imprecise_dtypes=True))
            nc.gpsimd.affine_select(out=ident[:], in_=ident[:], compare_op=ALU.not_equal, fill=1.0, base=0,
                                    pattern=[[-1, P]], channel_multiplier=1)
            nc.gpsimd.affine_select(out=tri[:], in_=ones[:], compare_op=ALU.is_gt, fill=0.0, base=0,
                                    pattern=[[1, P]], channel_multiplier=-1).then_inc(consts_ready, 1)

        @on("dve")
        def _(dve, od):
            dve.wait_ge(edges_loaded, 64)
            dve.wait_ge(consts_ready, 1)
            nc.vector.tensor_copy(src_f[:], src_i[:])
            nc.vector.tensor_copy(typ_f[:], typ_i[:])
            od.link(nc.vector.tensor_copy(dst_f[:], dst_i[:]))
            with dve.Fori(0, ET // 2) as i:
                for b in range(2):
                    t = 2 * i + b
                    dve.wait_ge(hot_used, t + 1)
                    nc.vector.tensor_scalar(hotb[:, b, 0, :], iota[:], src_f[:, bass.ds(t, 1)], None, ALU.is_equal)
                    nc.vector.tensor_scalar(hotb[:, b, 1, :], iota[:], dst_f[:, bass.ds(t, 1)], None,
                                            ALU.is_equal).then_inc(hot_ready, 1)
            for c in range(NT):
                b = banks.filled(dve, f"cnt{c}")
                nc.vector.tensor_copy(cnt_src[:, c, :], b[:, 0:N]).then_inc(banks.free_of(f"cnt{c}"), 1)
            for c in range(NT):
                b = banks.filled(dve, f"cntT{c}")
                nc.vector.tensor_copy(cnt_dst[:, c, :], b[:, 0:N]).then_inc(banks.free_of(f"cntT{c}"), 1)
            for c in range(NT):
                banks.drained(dve, f"cntT{c}")
            nc.vector.tensor_scalar(mask_src[:], cnt_src[:], 0.5, MASKED, ALU.is_lt, ALU.mult)
            nc.vector.tensor_scalar(mask_dst[:], cnt_dst[:], 0.5, MASKED, ALU.is_lt, ALU.mult).then_inc(mask_done, 1)
            dve.wait_ge(mask_done, 1)

        @on("pe")
        def _(pe, o):
            pe.wait_ge(consts_ready, 1)
            bk = [banks.open(pe, f"cnt{c}") for c in range(NT)]
            for c in range(NT):
                last = mm(bk[c][:, 0:N], zeros[:, 0:P], zeros[:, 0:N], True, False)
            last.then_inc(hot_used, 2)
            with pe.Fori(0, ET // 2) as i:
                for b in range(2):
                    pe.wait_ge(hot_ready, 2 * i + b + 1)
                    for c in range(NT):
                        last = mm(bk[c][:, 0:N], hotb[:, b, 0, c * P:(c + 1) * P], hotb[:, b, 1, :], False, False)
                    last.then_inc(hot_used, 1)
            for c in range(NT):
                mm(bk[c][:, 0:N], zeros[:, 0:P], zeros[:, 0:N], False, True).then_inc(banks.full_of(f"cnt{c}"), 1)
            for c in range(NT):
                banks.drained(pe, f"cnt{c}")
            for c in range(NT):
                b = banks.open(pe, f"cntT{c}")
                for t in range(NT):
                    last = nc.tensor.transpose(b[:, t * P:(t + 1) * P], cnt_src[:, t, c * P:(c + 1) * P], ident[:])
                last.then_inc(banks.full_of(f"cntT{c}"), 1)

        @on("sp")
        def _(sp, o):
            Ww = A["L0_gnn_Ww"].rearrange("(r c p) (q n) -> r q p c n", r=2, p=P, q=2)
            for r in range(2):
                for q in range(2):
                    ring.load(sp, banks, 2 * r + q, [(ring.slot(2 * r + q), Ww[r, q])])
                    ring.last[2 * r + q] = (f"l0uv{r}{q}2",)
            ring.load(sp, banks, 4, [(ring.slot(4), A["L0_gnn_Wv"].rearrange("(c p) n -> p c n", p=P))])
            ring.last[4] = ("l0o2",)

        def l0_store_tables(sp):
            for nm in [f"l0uv{r}{q}{t}" for r in range(2) for q in range(2) for t in range(NT)] + [f"l0o{t}" for t in range(NT)]:
                banks.drained(sp, nm)
            sp.wait_ge(step_ready, 1)
            sp.dma_start(tiled(tab_u), ust[:]).then_inc(tables_stored, 16)
            sp.dma_start(tiled(tab_v), vst[:]).then_inc(tables_stored, 16)
            sp.dma_start(tiled(tab_o), ost[:]).then_inc(tables_stored, 16)

        def store_maxima(sp, n, table):
            sp.wait_ge(max_ready, n)
            sp.dma_start(tiled(table), seg_node[:]).then_inc(max_stored, 16)

        @on("pe")
        def _(pe, o):
            pe.wait_ge(params, PARAMS)
            pe.wait_ge(xn_ready, NORM["l0"] + 1)
            pe_transpose(pe, "l0x", xn)
            for c in range(KC):
                banks.drained(pe, f"l0x{c}")
            for r in range(2):
                for q in range(2):
                    w = ring.get(pe, 2 * r + q)
                    for t in range(NT):
                        pe_rows(pe, f"l0uv{r}{q}{t}", xT, w, t, r_bw[:, q * 512:q * 512 + 512] if r else None)
            w = ring.get(pe, 4)
            for t in range(NT):
                pe_rows(pe, f"l0o{t}", xT, w, t, r_bv0)
            pe.wait_ge(scores_max, 1)
            pe_segment_max(pe, "l0")
            pe_scatter_rows(pe, "l0", 0)

        @on("act")
        def _(act, o):
            act_norm(act, NORM["l0"])
            act_transposed(act, "l0x", xT)
            act.wait_ge(mask_done, 1)
            for r in range(2):
                for q in range(2):
                    for t in range(NT):
                        act_copy(act, f"l0uv{r}{q}{t}", (vst if r else ust)[:, t, q * 512:q * 512 + 512])
            for t in range(NT):
                act_copy(act, f"l0o{t}", ost[:, t, :])
            with act.Fori(0, ET // 2) as i:
                for b in range(2):
                    act.wait_ge(z_ready, 2 * i + b + 1)
                    nc.scalar.activation(gbuf_u[:, b, 0:1024], gbuf_v[:, b, :], ACT.Copy, scale=0.01).then_inc(lrelu_done, 1)
            act_scatter_rows(act, 0)
            act.wait_ge(elu_in, 1)
            nc.scalar.activation(xn2b[:], xn2b[:], ACT.Exp).then_inc(elu_exp, 1)
            act_norm(act, NORM["l0b"])

        xn2b = view(2200, NT, D)

        @on("pool")
        def _(pool, op):
            pool.wait_ge(tables_stored, 48)
            with op.loop(ET // 2, 2) as i:
                for b in range(2):
                    t = 2 * i + b
                    pool.wait_ge(edge_free, t + 1)
                    nc.gpsimd.tensor_copy(idx[:, 2 * b, :], src_i[:, bass.ds(t, 1)])
                    op.link(nc.gpsimd.tensor_copy(idx[:, 2 * b + 1, :], dst_i[:, bass.ds(t, 1)]))
                    pool.nop(nofuse=True)
                    pool_gather(gbuf_u[:, b, :], tab_u, idx[:, 2 * b, :]).then_inc(rows_landed[b], 16)
                    pool_gather(gbuf_v[:, b, :], tab_v, idx[:, 2 * b + 1, :]).then_inc(cols_landed[b], 16)
            pool.wait_ge(max_stored, 16)
            pool_scatter_rows(pool, op, dst_i, tab_o, src_i, tab_m, 0)

        @on("dve")
        def _(dve, od):
            dve.wait_ge(x_loaded, 16)
            dve_norm(dve, od, NORM["l0"], x, xn)
            banks.drained(dve, "l0uv002")
            for t in range(NT):
                last = nc.vector.tensor_copy(ust[:, t, 1024:1024 + N], cnt_src[:, t, :])
            last.then_inc(step_ready, 1)
            dve.wait_ge(params, PARAMS)
            dve.wait_ge(tables_stored, 48)
            od.link(nc.vector.memset(seg_max[:], MASKED))
            nc.vector.memset(neg[:], 0.0).then_inc(edge_free, 2)
            wa_bc = wa.unsqueeze(1).broadcast_to([P, H8, P])
            with od.loop(ET // 2, 10) as i:
                for b in range(2):
                    t = 2 * i + b
                    dve.wait_ge(rows_landed[b], 16 * (i + 1))
                    dve.wait_ge(cols_landed[b], 16 * (i + 1))
                    nc.vector.tensor_tensor(gbuf_v[:, b, :], gbuf_v[:, b, :], gbuf_u[:, b, 0:1024],
                                            ALU.add).then_inc(z_ready, 1)
                    nc.vector.tensor_scalar(neg[:, b, :], iota[:], src_f[:, bass.ds(t, 1)], MASKED, ALU.not_equal, ALU.mult)
                    od.link(nc.vector.tensor_scalar(hot[:, b, :], iota[:], dst_f[:, bass.ds(t, 1)], None, ALU.is_equal))
                    nc.vector.tensor_tensor_reduce(out=hot[:, b, :], in0=hot[:, b, :], in1=gbuf_u[:, b, 1024:1024 + N],
                                                   scale=1.0, scalar=0.0, op0=ALU.mult, op1=ALU.add,
                                                   accum_out=gate[:, 14, b:b + 1])
                for b in range(2):
                    t = 2 * i + b
                    dve.wait_ge(lrelu_done, t + 1)
                    z3 = gbuf_v[:, b, :].rearrange("p (h d) -> p h d", h=H8)
                    od.link(nc.vector.tensor_tensor(gbuf_v[:, b, :], gbuf_v[:, b, :], gbuf_u[:, b, 0:1024], ALU.max))
                    od.link(nc.vector.tensor_tensor(z3, z3, wa_bc, ALU.mult))
                    od.link(nc.vector.tensor_reduce(w_edge[:, bass.ds(t, 1), :].rearrange("p a h -> p (a h)"), z3, AX, ALU.add))
                    od.link(dve_segment_max(od, None, t, b))
                    nc.vector.tensor_copy(cnt_edge[:, bass.ds(t, 1)], gate[:, 14, b:b + 1]).then_inc(edge_free, 1)
            nc.vector.tensor_scalar(w_edge[:], w_edge[:], ba0, None, ALU.add)
            od.link(nc.vector.tensor_scalar(seg_max[:], seg_max[:], ba0, None, ALU.add))
            od.link(nc.vector.reciprocal(cnt_edge[:], cnt_edge[:]))
            nc.vector.memset(gate[:, 15, 0:1], 0.0).then_inc(scores_max, 1)
            dve_segment_node(dve, "l0")
            for j in range(6):
                banks.drained(dve, f"l0m{j}")
            nc.vector.memset(gate[:, 15, 1:2], 0.0).then_inc(max_ready, 1)
            nc.vector.memset(gate[:, 15, 2:3], 0.0).then_inc(msg_free, 2)
            dve_scatter_rows(dve, od, src_f, 16 * (ET // 2), 0, True)
            dve_scatter_sums(dve, od, "l0", 1.0e-30, False)
            nc.vector.tensor_scalar(xn2b[:], xn2[:], 0.0, None, ALU.min).then_inc(elu_in, 1)
            dve.wait_ge(elu_exp, 1)
            od.link(nc.vector.scalar_tensor_tensor(out=flat(xn2), in0=flat(xn2), scalar=0.0, in1=flat(xn2b), op0=ALU.max,
                                                   op1=ALU.add))
            od.link(nc.vector.scalar_tensor_tensor(out=flat(xn2), in0=flat(xn2), scalar=-1.0, in1=flat(xn), op0=ALU.add,
                                                   op1=ALU.add))
            dve_norm(dve, od, NORM["l0b"], xn2, xn2, BC["L0_gnn_gamma"], BC["L0_gnn_beta"])
            dve.wait_ge(xn_ready, NORM["l0b"] + 1)
            od.link(nc.vector.tensor_tensor(x[:], x[:], xn2[:], ALU.add))

        def flat(a):
            return a[:].rearrange("p t n -> p (t n)")

        def dve_scatter_rows(dve, od, key, landed_before, tiles_before, divide):
            with od.loop(ET // 2, 4 if divide else 2) as i:
                for b in range(2):
                    t = 2 * i + b
                    dve.wait_ge(cols_landed[b], 16 * (i + 1) + landed_before)
                    dve.wait_ge(msg_used, t + 1 + 2 * (tiles_before // ET) + tiles_before)
                    nc.vector.tensor_tensor(gm[:, b, :], w_edge[:, bass.ds(t, 1), :].rearrange("p a h -> p (a h)"),
                                            gm[:, b, :], ALU.subtract).then_inc(diff_ready, 1)
                    nc.vector.tensor_scalar(hot[:, b, :], iota[:], key[:, bass.ds(t, 1)], None, ALU.is_equal)
                for b in range(2):
                    t = 2 * i + b
                    dve.wait_ge(ex_done, t + 1 + tiles_before)
                    if divide:
                        od.link(nc.vector.tensor_scalar(ex[:, b, :], ex[:, b, :], cnt_edge[:, bass.ds(t, 1)], None, ALU.mult))
                    nc.vector.tensor_copy(msg[:, b, 0, 256:264], ex[:, b, :])
                    nc.vector.tensor_copy(msg[:, b, 1, 256:264], ex[:, b, :])
                    dve.wait_ge(rows_landed[b], 16 * (i + 1) + landed_before)
                    for hf in range(2):
                        last = nc.vector.tensor_tensor(
                            msg[:, b, hf, 0:256].rearrange("p (h d) -> p h d", h=4),
                            go[:, b, hf * 256:hf * 256 + 256].rearrange("p (h d) -> p h d", h=4),
                            ex[:, b, hf * 4:hf * 4 + 4].unsqueeze(2).broadcast_to([P, 4, HD]), ALU.mult)
                    od.link(last)
                    nc.vector.memset(gate[:, 15, 0:1], 0.0).then_inc(msg_free, 1)
                    nc.vector.memset(gate[:, 15, 3:4], 0.0).then_inc(msg_ready, 1)

        @on("sp")
        def _(sp, o):
            l0_store_tables(sp)

        E0, E1 = A["L0_ffn_w1"].shape[0], A["L1_ffn_w1"].shape[0]
        HE = A["L0_ffn_w1"].shape[2]
        FC = HE // P
        CAP1 = max(min(N, int(N * 2 * 2.0 / E1)), 4)
        hid = view(0, 2 * FC, N).rearrange("p (b f) n -> p b f n", b=2)
        acc = view(4 * N, NT, D)

        def w1_of(s):
            return ring.slot(s).rearrange("p c n -> p (c n)").rearrange("p (e c h) -> p e c h", e=2, c=KC)

        def w2_of(s):
            return ring.slot(s).rearrange("p (e f) n -> p e f n", e=2)

        def load_pair(sp, w1, w2, e, s1, s2):
            ring.load(sp, banks, s1, [(w1_of(s1), w1[e:e + 2].rearrange("e (c p) h -> p e c h", p=P))])
            ring.load(sp, banks, s2, [(w2_of(s2), w2[e:e + 2].rearrange("e (f p) n -> p e f n", p=P))])

        def pe_expert_up(pe, tag, e, aT, s1, i=None):
            if e % 2 == 0:
                ring.get(pe, s1, i)
            for f in range(FC):
                b = banks.open(pe, f"{tag}h{e}{f}", i)
                for c in range(KC):
                    last = mm(b[:, 0:N], w1_of(s1)[:, e % 2, c, f * P:(f + 1) * P], aT[:, c, :], c == 0, c == KC - 1)
                last.then_inc(banks.full_of(f"{tag}h{e}{f}"), 1)

        def pe_expert_down(pe, tag, e, s2, i=None):
            if e % 2 == 0:
                ring.get(pe, s2, i)
            for f in range(FC):
                banks.drained(pe, f"{tag}h{e}{f}", i)
            for t in range(NT):
                b = banks.open(pe, f"{tag}e{e}{t}", i)
                for f in range(FC):
                    last = mm(b, hid[:, e % 2, f, t * P:(t + 1) * P], w2_of(s2)[:, e % 2, f, :], f == 0, f == FC - 1)
                last.then_inc(banks.full_of(f"{tag}e{e}{t}"), 1)

        def act_expert(act, tag, e, func, i=None):
            for f in range(FC):
                name = f"{tag}h{e}{f}"
                b = banks.filled(act, name, i)
                nc.scalar.activation(hid[:, e % 2, f, :], b[:, 0:N], func).then_inc(banks.free_of(name), 1)

        def dve_expert(dve, tag, e, weight, i=None):
            for t in range(NT):
                name = f"{tag}e{e}{t}"
                if e > 0:
                    banks.drained(dve, f"{tag}e{e - 1}{t}", i)
                b = banks.filled(dve, name, i)
                nc.vector.scalar_tensor_tensor(out=acc[:, t, :], in0=b, scalar=weight(t), in1=acc[:, t, :], op0=ALU.mult,
                                               op1=ALU.add).then_inc(banks.free_of(name), 1)

        F0_SLOTS = [(5, 6), (7, 0), (1, 2)]

        @on("sp")
        def _(sp, o):
            for j, (s1, s2) in enumerate(F0_SLOTS):
                load_pair(sp, A["L0_ffn_w1"], A["L0_ffn_w2"], 2 * j, s1, s2)
                ring.last[s1] = (f"f0h{2 * j + 1}{FC - 1}",)
                ring.last[s2] = (f"f0e{2 * j + 1}{NT - 1}",)
            store_maxima(sp, 1, tab_m)

        @on("pe")
        def _(pe, o):
            pe.wait_ge(xn_ready, NORM["f0"] + 1)
            pe_transpose(pe, "f0x", xn)
            for c in range(KC):
                banks.drained(pe, f"f0x{c}")
            pe_logits(pe, "f0g", xT, wg0, E0)
            pe.wait_ge(xn_ready, NORM["f0b"] + 1)
            pe_transpose(pe, "f0y", xn2)
            for c in range(KC):
                banks.drained(pe, f"f0y{c}")
            for e in range(E0 + 1):
                if e < E0:
                    pe_expert_up(pe, "f0", e, xT2, F0_SLOTS[e // 2][0])
                if e >= 1:
                    pe_expert_down(pe, "f0", e - 1, F0_SLOTS[(e - 1) // 2][1])

        @on("act")
        def _(act, o):
            act_norm(act, NORM["f0"])
            act_transposed(act, "f0x", xT)
            act_norm(act, NORM["f0b"])
            for c in range(KC):
                b = banks.filled(act, f"f0y{c}")
                nc.scalar.activation(xT2[:, c, :], b[:, 0:N], ACT.Copy, scale=c_g0[:, c:c + 1]).then_inc(
                    banks.free_of(f"f0y{c}"), 1)
            act_softmax_logits(act, "f0g", E0)
            for e in range(E0):
                act_expert(act, "f0", e, ACT.Gelu)

        @on("dve")
        def _(dve, od):
            dve_norm(dve, od, NORM["f0"], x, xn)
            dve.wait_ge(xn_ready, NORM["f0"] + 1)
            dve_norm(dve, od, NORM["f0b"], xn, xn2)
            dve_softmax_logits(dve, od, "f0g", E0, 0)
            pr, one, wo1, comb = g3(0, E0), g3(4, E0), g3(5, E0), g3(6, E0)
            g1, g2 = gate[:, 1, 24:24 + NT], gate[:, 1, 32:32 + NT]
            dve_top1(od, pr, E0, g1, one, g3(2, E0))
            od.link(nc.vector.tensor_scalar(wo1, one, -1.0, 1.0, ALU.mult, ALU.add))
            od.link(nc.vector.tensor_tensor(wo1, wo1, pr, ALU.mult))
            od.link(nc.vector.tensor_reduce(g2, wo1, AX, ALU.max))
            od.link(nc.vector.scalar_tensor_tensor(out=g2, in0=g2, scalar=1e-9, in1=g1, op0=ALU.add, op1=ALU.add))
            od.link(nc.vector.reciprocal(g2, g2))
            od.link(nc.vector.tensor_tensor(g1, g1, g2, ALU.mult))
            od.link(nc.vector.tensor_tensor(comb, one, g1.unsqueeze(2).broadcast_to([P, NT, E0]), ALU.mult))
            od.link(nc.vector.memset(acc[:], 0.0))
            for e in range(E0):
                dve_expert(dve, "f0", e, lambda t: comb[:, t, e:e + 1])
            for t in range(NT):
                banks.drained(dve, f"f0e{E0 - 1}{t}")
            od.link(nc.vector.tensor_tensor(x[:], x[:], acc[:], ALU.add))

        BLK, CDIM = A["L1_gnn_s1_w"].shape[0], A["L1_gnn_s1_w"].shape[1]
        NF = A["L1_gnn_f_w1"].shape[0] // 2
        HA = D // P
        TWO_PI_HI, TWO_PI_MID = 6.28125, 0.0019353071795864769
        ROUND = 12582912.0
        noise = view(11400, N)
        ph = view(11800, N)
        turns = view(12200, N)
        condT = view(0, N)
        mod = view(N, 2, N)
        qT = view(3 * N, HA, N)
        kT = view(3 * N + 1536, HA, N)
        vrow = view(3 * N + 3072, NT, D)
        modw = view(3 * N + 4608, 4, D)
        oT = qT
        blk_in = sem("blk_in")
        noise_in = sem("noise_in")
        L1W = ("wq", "wk", "wv", "wo", "m_w1", "m_w2")

        def block_of(name, i):
            a = A["L1_gnn_" + name]
            return a[i] if isinstance(i, int) else a[bass.ds(i, 1)].rearrange("a k n -> (a k) n")

        def load_block_rows(sp, i):
            for j, nm in enumerate(("s1_w", "b1_w", "s2_w", "b2_w")):
                sp.dma_start(modw[0:CDIM, j, :], block_of(nm, i)).then_inc(blk_in, 16)
            for j, nm in enumerate(("bv", "bo", "m_b2")):
                a = A["L1_gnn_" + nm]
                sp.dma_start(blk_rows[0:1, j, :], a[bass.ds(i, 1), :]).then_inc(blk_in, 16)

        L1_LAST = ("l1q3", "l1k3", "l1v2", "l1w2", "l1u3", "l1d2")

        @on("sp")
        def _(sp, o):
            sp.wait_ge(xn_ready, NORM["f0"] + 1)
            sp.dma_start(noise[0:2 * NF, :], A["node_vec1"].rearrange("n a -> (a n)").partition_broadcast(2 * NF)).then_inc(noise_in, 16)
            for s, nm in enumerate(L1W):
                ring.load(sp, banks, s, [(ring.slot(s), block_of(nm, 0).rearrange("(c p) n -> p c n", p=P))])
            sp.wait_ge(xn_ready, NORM["l1"] + 1)
            load_block_rows(sp, 0)
            with sp.Fori(0, BLK - 1) as i:
                for s, nm in enumerate(L1W):
                    ring.load(sp, banks, s, [(ring.slot(s), block_of(nm, i + 1).rearrange("(c p) n -> p c n", p=P))],
                              used=(L1_LAST[s], i))
                banks.filled(sp, "l1d2", i)
                load_block_rows(sp, i + 1)
            for s in range(6):
                ring.last[s] = (L1_LAST[s], BLK - 1)

        @on("pe")
        def _(pe, o):
            pe.wait_ge(pe_col, 1)
            b = banks.open(pe, "cond1")
            mm(b[0:CDIM, 0:N], fw1, ph[0:2 * NF, :], True, True).then_inc(banks.full_of("cond1"), 1)
            banks.drained(pe, "cond1")
            b = banks.open(pe, "cond2")
            mm(b[0:CDIM, 0:N], fw2, turns[0:CDIM, :], True, True).then_inc(banks.full_of("cond2"), 1)
            banks.drained(pe, "cond2")

            def modulated(k, i):
                for c in range(KC):
                    for j, nm in ((2 * k, f"l1s{k}{c}"), (2 * k + 1, f"l1b{k}{c}")):
                        b = banks.open(pe, nm, i)
                        mm(b[:, 0:N], modw[0:CDIM, j, c * P:(c + 1) * P], condT[0:CDIM, :], True, True).then_inc(
                            banks.full_of(nm), 1)
                    if c == 0:
                        pe.wait_ge(xn_ready, NORM["blk"] + 2 * i + k + 1)
                    b = banks.open(pe, f"l1x{k}{c}", i)
                    for t in range(NT):
                        last = nc.tensor.transpose(b[:, t * P:(t + 1) * P], xn[:, t, c * P:(c + 1) * P], ident[:])
                    last.then_inc(banks.full_of(f"l1x{k}{c}"), 1)
                for c in range(KC):
                    banks.drained(pe, f"l1b{k}{c}", i)

            def head_scores(h, i):
                for t in range(NT):
                    b = banks.open(pe, f"l1h{h}s{t}", i)
                    mm(b[:, 0:N], qT[:, h, t * P:(t + 1) * P], kT[:, h, :], True, True).then_inc(
                        banks.full_of(f"l1h{h}s{t}"), 1)

            def head_values(h, i):
                pe_att_transpose(pe, f"l1h{h}", HA * i + h, h % 2, i)
                for c in range(NT):
                    banks.drained(pe, f"l1h{h}p{c}", i)
                b = banks.open(pe, f"l1o{h}", i)
                for c in range(NT):
                    last = mm(b[:, 0:N], vrow[:, c, h * P:(h + 1) * P], probsT[:, h % 2, c, :], c == 0, c == NT - 1)
                last.then_inc(banks.full_of(f"l1o{h}"), 1)

            with banks.loop(BLK, 73), pe.Fori(0, BLK) as i:
                pe.wait_ge(blk_in, 16 * 7 * (i + 1))
                modulated(0, i)
                for s, nm in ((0, "q"), (1, "k")):
                    w = ring.get(pe, s, i)
                    for h in range(HA):
                        pe_cols(pe, f"l1{nm}{h}", xT, w, h * P, i)
                w = ring.get(pe, 2, i)
                for t in range(NT):
                    pe_rows(pe, f"l1v{t}", xT, w, t, blk_rows[0:1, 0, :], i)
                for h in range(HA):
                    banks.drained(pe, f"l1q{h}", i)
                    banks.drained(pe, f"l1k{h}", i)
                for t in range(NT):
                    banks.drained(pe, f"l1v{t}", i)
                for h in range(HA + 1):
                    if h < HA:
                        head_scores(h, i)
                    if h >= 1:
                        head_values(h - 1, i)
                for h in range(HA):
                    banks.drained(pe, f"l1o{h}", i)
                w = ring.get(pe, 3, i)
                for t in range(NT):
                    pe_rows(pe, f"l1w{t}", oT, w, t, blk_rows[0:1, 1, :], i)
                modulated(1, i)
                w = ring.get(pe, 4, i)
                for c in range(KC):
                    pe_cols(pe, f"l1u{c}", xT, w, c * P, i)
                for c in range(KC):
                    banks.drained(pe, f"l1u{c}", i)
                w = ring.get(pe, 5, i)
                for t in range(NT):
                    pe_rows(pe, f"l1d{t}", kT, w, t, blk_rows[0:1, 2, :], i)
            ring.after_loop(range(6), BLK)

        @on("act")
        def _(act, o):
            act.wait_ge(step_ready, 2)
            nc.scalar.activation(ph[0:2 * NF, :], ph[0:2 * NF, :], ACT.Sin).then_inc(pe_col, 1)
            b = banks.filled(act, "cond1")
            nc.scalar.activation(turns[0:CDIM, :], b[0:CDIM, 0:N], ACT.Silu, bias=c_fb1).then_inc(banks.free_of("cond1"), 1)
            b = banks.filled(act, "cond2")
            nc.scalar.activation(condT[0:CDIM, :], b[0:CDIM, 0:N], ACT.Identity, bias=c_fb2).then_inc(banks.free_of("cond2"), 1)
            act_norm(act, NORM["l1"])

            def biased(name, dst, table, c, i, func=ACT.Identity):
                b = banks.filled(act, name, i)
                nc.scalar.activation(dst, b[:, 0:N], func, bias=table[:, bass.ds(KC * i + c, 1)]).then_inc(
                    banks.free_of(name), 1)

            with act.Fori(0, BLK) as i:
                for k, table in ((0, c_s1b), (1, c_s2b)):
                    if k == 0:
                        act_norm(act, NORM["blk"] + 2 * i)
                    for c in range(KC):
                        if c >= 2:
                            banks.drained(act, f"l1x{k}{c - 2}", i)
                        biased(f"l1s{k}{c}", mod[:, c % 2, :], table, c, i)
                    if k == 0:
                        for nm, dst, tb in (("q", qT, c_bq), ("k", kT, c_bk)):
                            for h in range(HA):
                                biased(f"l1{nm}{h}", dst[:, h, :], tb, h, i)
                        for t in range(NT):
                            act_copy(act, f"l1v{t}", vrow[:, t, :], D, i)
                        for h in range(HA + 1):
                            if h < HA:
                                act_att_exp(act, HA * i + h, h % 2)
                            if h >= 1:
                                act_att_transposed(act, f"l1h{h - 1}", (h - 1) % 2, i)
                                act_copy(act, f"l1o{h - 1}", oT[:, h - 1, :], N, i)
                        act_norm(act, NORM["blk"] + 2 * i + 1)
                    else:
                        for c in range(KC):
                            biased(f"l1u{c}", kT[:, c, :], c_mb1, c, i, ACT.Relu)

        @on("dve")
        def _(dve, od):
            dve.wait_ge(noise_in, 16)
            dve.wait_ge(consts_ready, 2)
            fr = gate[0:2 * NF, 7, 0:1]
            od.link(nc.vector.tensor_scalar(fr, fr, float(2.0 * 3.141592653589793 / 16), None, ALU.mult))
            z, tn = ph[0:2 * NF, :], turns[0:2 * NF, :]
            od.link(nc.vector.tensor_scalar(z, noise[0:2 * NF, :], fr, None, ALU.mult))
            od.link(nc.vector.tensor_scalar(tn, z, 0.15915494309189535, ROUND, ALU.mult, ALU.add))
            od.link(nc.vector.tensor_scalar(tn, tn, -ROUND, None, ALU.add))
            od.link(nc.vector.scalar_tensor_tensor(out=z, in0=tn, scalar=-TWO_PI_HI, in1=z, op0=ALU.mult, op1=ALU.add))
            od.link(nc.vector.scalar_tensor_tensor(out=z, in0=tn, scalar=-TWO_PI_MID, in1=z, op0=ALU.mult, op1=ALU.add))
            od.link(nc.vector.tensor_scalar(z, z, 3.1415925, -3.1415925, ALU.min, ALU.max))
            zc = ph[NF:2 * NF, :]
            od.link(nc.vector.scalar_tensor_tensor(out=zc, in0=zc, scalar=-1.0, in1=zc, op0=ALU.mult, op1=ALU.max))
            nc.vector.tensor_scalar(zc, zc, -1.0, 1.5707963267948966, ALU.mult, ALU.add).then_inc(step_ready, 1)
            for tb in (c_s1b, c_s2b):
                od.link(nc.vector.tensor_scalar(tb, tb, 1.0, None, ALU.add))
            dve_norm(dve, od, NORM["l1"], x, xn2)
            dve.wait_ge(xn_ready, NORM["l1"] + 1)

            def modulated(k, table, i):
                for c in range(KC):
                    banks.drained(dve, f"l1s{k}{c}", i)
                    b = banks.filled(dve, f"l1x{k}{c}", i)
                    nc.vector.tensor_tensor(xT[:, c, :], b[:, 0:N], mod[:, c % 2, :], ALU.mult).then_inc(
                        banks.free_of(f"l1x{k}{c}"), 1)
                    banks.drained(dve, f"l1x{k}{c}", i)
                    b = banks.filled(dve, f"l1b{k}{c}", i)
                    nc.vector.scalar_tensor_tensor(out=xT[:, c, :], in0=b[:, 0:N], scalar=table[:, bass.ds(KC * i + c, 1)],
                                                   in1=xT[:, c, :], op0=ALU.add, op1=ALU.add).then_inc(
                        banks.free_of(f"l1b{k}{c}"), 1)

            def add_rows(tag, i):
                for t in range(NT):
                    b = banks.filled(dve, f"{tag}{t}", i)
                    nc.vector.tensor_tensor(xn2[:, t, :], xn2[:, t, :], b, ALU.add).then_inc(banks.free_of(f"{tag}{t}"), 1)
                for t in range(NT):
                    banks.drained(dve, f"{tag}{t}", i)

            with od.loop(BLK, 26) as i:
                dve_norm(dve, od, NORM["blk"] + 2 * i, xn2, xn)
                modulated(0, c_b1b, i)
                for h in range(HA + 1):
                    if h < HA:
                        dve_att_scores(dve, od, f"l1h{h}", HA * i + h, h, h % 2, float(P) ** -0.5, mask_src, i)
                    if h >= 1:
                        dve_att_probs(dve, od, HA * i + h - 1, (h - 1) % 2, cnt_src)
                add_rows("l1w", i)
                dve_norm(dve, od, NORM["blk"] + 2 * i + 1, xn2, xn)
                modulated(1, c_b2b, i)
                add_rows("l1d", i)
            od.link(nc.vector.tensor_tensor(x[:], x[:], xn2[:], ALU.add))

        @on("pool")
        def _(pool, op):
            fr = gate[0:2 * NF, 7, 0:1]
            nc.gpsimd.iota(fr[0:NF, :], pattern=[[0, 1]], base=1, channel_multiplier=1, allow_small_or_imprecise_dtypes=True)
            nc.gpsimd.iota(gate[NF:2 * NF, 7, 0:1], pattern=[[0, 1]], base=1, channel_multiplier=1,
                           allow_small_or_imprecise_dtypes=True).then_inc(consts_ready, 1)

        HALF = E1 // 2

        @on("sp")
        def _(sp, o):
            for i in range(2):
                for j in range(HALF // 2):
                    load_pair(sp, A["L1_ffn_w1"], A["L1_ffn_w2"], HALF * i + 2 * j, 2 * j, 2 * j + 1)
                    ring.last[2 * j] = (f"f1h{2 * j + 1}{FC - 1}", i)
                    ring.last[2 * j + 1] = (f"f1e{2 * j + 1}{NT - 1}", i)

        @on("pe")
        def _(pe, o):
            pe.wait_ge(xn_ready, NORM["f1"] + 1)
            pe_transpose(pe, "f1x", xn)
            for c in range(KC):
                banks.drained(pe, f"f1x{c}")
            pe_logits(pe, "f1g", xT, wg1, E1)

            def before(name, mask, total):
                b = banks.open(pe, name)
                for t in range(NT):
                    ks = range(NT) if total else range(t + 1)
                    for k in ks:
                        last = mm(b[:, t * E1:(t + 1) * E1], tri[:] if k == t and not total else ones[:], mask[:, k, :],
                                  k == 0, k == ks[-1])
                last.then_inc(banks.full_of(name), 1)

            pe.wait_ge(step_ready, 3)
            before("f1p1", g3(4, E1), False)
            before("f1p2", g3(5, E1), False)
            pe.wait_ge(step_ready, 4)
            before("f1n1", g3(4, E1), True)
            with banks.loop(2, HALF * (FC + NT)), pe.Fori(0, 2) as i:
                for e in range(HALF + 1):
                    if e < HALF:
                        pe_expert_up(pe, "f1", e, xT, e // 2 * 2, i)
                    if e >= 1:
                        pe_expert_down(pe, "f1", e - 1, (e - 1) // 2 * 2 + 1, i)
            ring.after_loop(range(8), 2)

        @on("act")
        def _(act, o):
            act_norm(act, NORM["f1"])
            act_transposed(act, "f1x", xT)
            act_softmax_logits(act, "f1g", E1)
            with act.Fori(0, 2) as i:
                for e in range(HALF):
                    act_expert(act, "f1", e, ACT.Relu, i)

        @on("dve")
        def _(dve, od):
            dve_norm(dve, od, NORM["f1"], x, xn)
            dve_softmax_logits(dve, od, "f1g", E1, 1)
            pr, m1, m2, rest, tmp = g3(0, E1), g3(4, E1), g3(5, E1), g3(6, E1), g3(2, E1)
            g1, g2, dn = gate[:, 1, 24:24 + NT], gate[:, 1, 32:32 + NT], gate[:, 1, 40:40 + NT]
            dve_top1(od, pr, E1, g1, m1, tmp)
            od.link(nc.vector.tensor_scalar(rest, m1, -1.0, 1.0, ALU.mult, ALU.add))
            od.link(nc.vector.tensor_tensor(rest, rest, pr, ALU.mult))
            dve_top1(od, rest, E1, g2, m2, tmp)
            nc.vector.memset(gate[:, 15, 4:5], 0.0).then_inc(step_ready, 1)
            od.link(nc.vector.scalar_tensor_tensor(out=dn, in0=g1, scalar=1e-9, in1=g2, op0=ALU.add, op1=ALU.add))
            od.link(nc.vector.reciprocal(dn, dn))
            nc.vector.tensor_tensor(g1, g1, dn, ALU.mult)
            od.link(nc.vector.tensor_tensor(g2, g2, dn, ALU.mult))

            def bank3(name):
                return banks.filled(dve, name)[:, 0:NT * E1].rearrange("p (t e) -> p t e", t=NT)

            p1, p2 = g3(8, E1), g3(9, E1)
            nc.vector.tensor_scalar(p1, bank3("f1p1"), float(CAP1), None, ALU.is_lt).then_inc(banks.free_of("f1p1"), 1)
            nc.vector.tensor_copy(p2, bank3("f1p2")).then_inc(banks.free_of("f1p2"), 1)
            banks.drained(dve, "f1p2")
            od.link(nc.vector.tensor_tensor(m1, m1, p1, ALU.mult))
            nc.vector.memset(gate[:, 15, 4:5], 0.0).then_inc(step_ready, 1)
            nc.vector.tensor_tensor(p2, p2, bank3("f1n1"), ALU.add).then_inc(banks.free_of("f1n1"), 1)
            banks.drained(dve, "f1n1")
            od.link(nc.vector.tensor_scalar(p2, p2, float(CAP1), None, ALU.is_lt))
            od.link(nc.vector.tensor_tensor(m2, m2, p2, ALU.mult))
            nc.vector.tensor_tensor(m1, m1, g1.unsqueeze(2).broadcast_to([P, NT, E1]), ALU.mult)
            od.link(nc.vector.tensor_tensor(m2, m2, g2.unsqueeze(2).broadcast_to([P, NT, E1]), ALU.mult))
            od.link(nc.vector.tensor_tensor(m1, m1, m2, ALU.add))
            od.link(nc.vector.memset(acc[:], 0.0))
            with dve.Fori(0, 2) as i:
                for e in range(HALF):
                    dve_expert(dve, "f1", e, lambda t: m1[:, t, bass.ds(HALF * i + e, 1)], i)
                for t in range(NT):
                    banks.drained(dve, f"f1e{HALF - 1}{t}", i)
            for t in range(NT):
                banks.drained(dve, f"f1e{HALF - 1}{t}", 1)
            od.link(nc.vector.tensor_tensor(x[:], x[:], acc[:], ALU.add))

        hrows = view(0, NT, D)
        prod = view(NT * D, NT, D)
        wT = view(2 * NT * D, KC, D)
        es_n, ed_n = view(11400, NT, H8), view(11430, NT, H8)
        es_b, ed_b = view(11500, 2, H8), view(11520, 2, H8)
        fac = view(10336, ET, H8)
        sel8 = view(11600, ET, H8)
        TYPES = A["L2_gnn_et_emb"].shape[0]

        @on("sp")
        def _(sp, o):
            ring.load(sp, banks, 0, [(ring.slot(0), A["L2_gnn_W"].rearrange("(c p) n -> p c n", p=P))])
            ring.last[0] = ("l2t3",)
            sp.wait_ge(step_ready, 5)
            sp.dma_start(tiled(tab_h), hrows[:]).then_inc(tables_stored, 16)
            sp.dma_start(tiled(tab_es), es_n[:]).then_inc(tables_stored, 16)
            sp.dma_start(tiled(tab_ed), ed_n[:]).then_inc(tables_stored, 16)

        def pe_weight_transpose(pe, tag, w, i=None):
            for c in range(KC):
                b = banks.open(pe, f"{tag}{c}", i)
                for q in range(KC):
                    last = nc.tensor.transpose(b[:, q * P:(q + 1) * P], w[:, q, c * P:(c + 1) * P], ident[:])
                last.then_inc(banks.full_of(f"{tag}{c}"), 1)

        @on("pe")
        def _(pe, o):
            pe_weight_transpose(pe, "l2t", ring.get(pe, 0))
            pe.wait_ge(xn_ready, NORM["l2"] + 1)
            pe_transpose(pe, "l2x", xn)
            for c in range(KC):
                banks.drained(pe, f"l2t{c}")
                banks.drained(pe, f"l2x{c}")
            for t in range(NT):
                pe_rows(pe, f"l2r{t}", xT, wT, t)
            pe.wait_ge(scores_max, 2)
            pe_segment_max(pe, "l2")
            pe_scatter_rows(pe, "l2", ET)

        @on("act")
        def _(act, o):
            act.wait_ge(var_ready, NORM["l2"] + 1)
            for c in range(KC):
                act_copy(act, f"l2t{c}", wT[:, c, :])
            act_norm(act, NORM["l2"])
            act_transposed(act, "l2x", xT)
            for t in range(NT):
                act_copy(act, f"l2r{t}", hrows[:, t, :])
            act_scatter_rows(act, ET)
            act_norm(act, NORM["l2b"])

        @on("pool")
        def _(pool, op):
            pool.wait_ge(tables_stored, 96)
            with op.loop(ET // 2, 2) as i:
                for b in range(2):
                    t = 2 * i + b
                    pool.wait_ge(edge_free, t + 1 + ET)
                    nc.gpsimd.tensor_copy(idx[:, 2 * b, :], src_i[:, bass.ds(t, 1)])
                    op.link(nc.gpsimd.tensor_copy(idx[:, 2 * b + 1, :], dst_i[:, bass.ds(t, 1)]))
                    pool.nop(nofuse=True)
                    pool_gather(es_b[:, b, :], tab_es, idx[:, 2 * b, :]).then_inc(rows_landed[b], 16)
                    pool_gather(ed_b[:, b, :], tab_ed, idx[:, 2 * b + 1, :]).then_inc(cols_landed[b], 16)
            pool.wait_ge(max_stored, 32)
            pool_scatter_rows(pool, op, src_i, tab_h, dst_i, tab_m2, ET)

        @on("dve")
        def _(dve, od):
            dve_norm(dve, od, NORM["l2"], x, xn)
            for t in range(NT):
                banks.drained(dve, f"l2r{t}")
            for vec, dst in ((BC["L2_gnn_a_src"], es_n), (BC["L2_gnn_a_dst"], ed_n)):
                for t in range(NT):
                    last = nc.vector.tensor_tensor(prod[:, t, :], hrows[:, t, :], vec, ALU.mult)
                od.link(last)
                od.link(nc.vector.tensor_reduce(dst[:].rearrange("p c h -> p (c h)"),
                                                prod[:].rearrange("p c (h d) -> p (c h) d", d=HD), AX, ALU.add))
            nc.vector.memset(gate[:, 15, 5:6], 0.0).then_inc(step_ready, 1)
            et3 = et_bc.rearrange("p (y h) -> p y h", h=H8)
            od.link(nc.vector.memset(fac[:], 1.0))
            for y in range(TYPES):
                od.link(nc.vector.scalar_tensor_tensor(
                    out=sel8[:], in0=typ_f[:].unsqueeze(2).broadcast_to([P, ET, H8]), scalar=float(y),
                    in1=et3[:, y:y + 1, :].broadcast_to([P, ET, H8]), op0=ALU.is_equal, op1=ALU.mult))
                od.link(nc.vector.tensor_tensor(fac[:], fac[:], sel8[:], ALU.add))
            od.link(nc.vector.tensor_tensor(fac[:], fac[:], ew[:].unsqueeze(2).broadcast_to([P, ET, H8]), ALU.mult))
            with dve.Fori(0, ET // 2) as i:
                for b in range(2):
                    t = 2 * i + b
                    dve.wait_ge(rows_landed[b], 16 * (i + 1) + 16 * ET)
                    dve.wait_ge(cols_landed[b], 16 * (i + 1) + 16 * ET)
                    nc.vector.tensor_tensor(w_edge[:, bass.ds(t, 1), :].rearrange("p a h -> p (a h)"), es_b[:, b, :], ed_b[:, b, :],
                                            ALU.add).then_inc(edge_free, 1)
            dve.wait_ge(edge_free, 2 + 2 * ET)
            wf, ff = w_edge[:].rearrange("p t h -> p (t h)"), fac[:].rearrange("p t h -> p (t h)")
            od.link(nc.vector.scalar_tensor_tensor(out=wf, in0=wf, scalar=0.2, in1=wf, op0=ALU.mult, op1=ALU.max))
            od.link(nc.vector.tensor_tensor(wf, wf, ff, ALU.mult))
            od.link(nc.vector.memset(seg_max[:], 0.0))
            with od.loop(ET // 2, 3) as i:
                for b in range(2):
                    last = nc.vector.tensor_scalar(neg[:, b, :], iota[:], dst_f[:, bass.ds(2 * i + b, 1)], MASKED,
                                                   ALU.not_equal, ALU.mult)
                od.link(last)
                for b in range(2):
                    od.link(dve_segment_max(od, None, 2 * i + b, b))
            nc.vector.memset(gate[:, 15, 0:1], 0.0).then_inc(scores_max, 1)
            dve_segment_node(dve, "l2")
            for j in range(6):
                banks.drained(dve, f"l2m{j}")
            nc.vector.memset(gate[:, 15, 1:2], 0.0).then_inc(max_ready, 1)
            dve_scatter_rows(dve, od, dst_f, 16 * (ET + ET // 2), ET, False)
            dve_scatter_sums(dve, od, "l2", 1.0e-10, True)
            od.link(nc.vector.tensor_tensor(xn2[:], xn2[:], xn[:], ALU.add))
            dve_norm(dve, od, NORM["l2b"], xn2, xn2, BC["L2_gnn_ln_gamma"], BC["L2_gnn_ln_beta"])
            dve.wait_ge(xn_ready, NORM["l2b"] + 1)
            od.link(nc.vector.tensor_tensor(x[:], x[:], xn2[:], ALU.add))

        K2 = A["L2_ffn_expert_weights"].shape[0]
        wTs = [view(0, KC, D), view(KC * D, KC, D)]
        coefT = view(2 * KC * D, N)
        acc2 = view(2 * KC * D + N, NT, D)
        mixw = xT2[0:K2, :, :].rearrange("p c n -> p (c n)")[:, 0:D]
        mixb = xT2[0:K2, :, :].rearrange("p c n -> p (c n)")[:, D:2 * D]
        mix_in = sem("mix_in")
        Q2 = K2 // 2

        @on("sp")
        def _(sp, o):
            sp.dma_start(mixw, A["L2_ffn_mixer_w"]).then_inc(mix_in, 16)
            sp.dma_start(mixb, A["L2_ffn_expert_biases"]).then_inc(mix_in, 16)
            for i in range(2):
                for e in range(Q2):
                    s = e + 1
                    ring.load(sp, banks, s, [(ring.slot(s), A["L2_ffn_expert_weights"][Q2 * i + e].rearrange("(c p) n -> p c n", p=P))])
                    ring.last[s] = (f"f2t{e}{KC - 1}", i)
                if i == 0:
                    store_maxima(sp, 2, tab_m2)

        @on("pe")
        def _(pe, o):
            pe.wait_ge(mix_in, 32)
            b = banks.open(pe, "f2m")
            for c in range(KC):
                last = nc.tensor.transpose(b[:, c * K2:(c + 1) * K2], mixw[:, c * P:(c + 1) * P], ident[0:K2, 0:K2])
            last.then_inc(banks.full_of("f2m"), 1)
            pe.wait_ge(xn_ready, NORM["f2"] + 1)
            pe_transpose(pe, "f2x", xn)
            banks.drained(pe, "f2m")
            for c in range(KC):
                banks.drained(pe, f"f2x{c}")
            pe_logits(pe, "f2g", xT, mixT, K2, r_mixb)
            pe.wait_ge(step_ready, 6)
            b = banks.open(pe, "f2c")
            for t in range(NT):
                last = nc.tensor.transpose(b[0:K2, t * P:(t + 1) * P], g3(0, K2)[:, t, :], ident[:])
            last.then_inc(banks.full_of("f2c"), 1)
            banks.drained(pe, "f2c")
            for t in range(NT):
                b = banks.open(pe, f"f2b{t}")
                mm(b, coefT[0:K2, t * P:(t + 1) * P], mixb, True, True).then_inc(banks.full_of(f"f2b{t}"), 1)
            with banks.loop(2, Q2 * (KC + NT)), pe.Fori(0, 2) as i:
                for e in range(Q2 + 1):
                    if e < Q2:
                        pe_weight_transpose(pe, f"f2t{e}", ring.get(pe, e + 1, i), i)
                    if e >= 1:
                        for c in range(KC):
                            banks.drained(pe, f"f2t{e - 1}{c}", i)
                        for t in range(NT):
                            pe_rows(pe, f"f2y{e - 1}{t}", xT, wTs[(e - 1) % 2], t, None, i)
            ring.after_loop(range(1, Q2 + 1), 2)

        @on("act")
        def _(act, o):
            act_copy(act, "f2m", small[:, 208:240], KC * K2)
            act_norm(act, NORM["f2"])
            act_transposed(act, "f2x", xT)
            act_softmax_logits(act, "f2g", K2)
            b = banks.filled(act, "f2c")
            nc.scalar.activation(coefT[0:K2, :], b[0:K2, 0:N], ACT.Copy).then_inc(banks.free_of("f2c"), 1)
            with act.Fori(0, 2) as i:
                for e in range(Q2):
                    for c in range(KC):
                        act_copy(act, f"f2t{e}{c}", wTs[e % 2][:, c, :], D, i)

        @on("dve")
        def _(dve, od):
            dve_norm(dve, od, NORM["f2"], x, xn)
            dve_softmax_logits(dve, od, "f2g", K2, 2)
            nc.vector.memset(gate[:, 15, 6:7], 0.0).then_inc(step_ready, 1)
            for t in range(NT):
                b = banks.filled(dve, f"f2b{t}")
                nc.vector.tensor_copy(acc2[:, t, :], b).then_inc(banks.free_of(f"f2b{t}"), 1)
            for t in range(NT):
                banks.drained(dve, f"f2b{t}")
            with dve.Fori(0, 2) as i:
                for e in range(Q2):
                    for t in range(NT):
                        name = f"f2y{e}{t}"
                        if e > 0:
                            banks.drained(dve, f"f2y{e - 1}{t}", i)
                        b = banks.filled(dve, name, i)
                        nc.vector.scalar_tensor_tensor(out=acc2[:, t, :], in0=b, scalar=g3(0, K2)[:, t, bass.ds(Q2 * i + e, 1)],
                                                       in1=acc2[:, t, :], op0=ALU.mult, op1=ALU.add).then_inc(
                            banks.free_of(name), 1)
                for t in range(NT):
                    banks.drained(dve, f"f2y{Q2 - 1}{t}", i)
            for t in range(NT):
                banks.drained(dve, f"f2y{Q2 - 1}{t}", 1)
            od.link(nc.vector.tensor_tensor(x[:], x[:], acc2[:], ALU.add))

        H3 = A["L3_gnn_Wq"].shape[1] // D
        U3 = BLK * HA
        q3, k3, v3, xa = view(0, KC, N), view(1536, KC, N), view(3072, NT, D), view(4608, KC, N)
        acc3 = view(6144, NT, D)
        row_in = sem("row_in")

        def head_cols(name, i):
            return A["L3_gnn_" + name][:, bass.ds((H3 - 1 - i) * D, D)].rearrange("(c p) n -> p c n", p=P)

        L3W = (("Wq", 5, "l3q3"), ("Wk", 6, "l3k3"), ("Wv", 7, "l3v2"), ("Wskip", 0, "l3a3"), ("Wlin", 1, "l3l2"))

        def load_head(sp, i, before):
            for nm, s, job in L3W:
                src = (A["L3_gnn_Wlin"][bass.ds((H3 - 1 - i) * D, D), :].rearrange("(c p) n -> p c n", p=P) if nm == "Wlin"
                       else head_cols(nm, i))
                ring.load(sp, banks, s, [(ring.slot(s), src)], used=None if before is None else (job, before))
            if before is not None:
                banks.filled(sp, "l3v2", before)
                sp.nop(nofuse=True)
            sp.dma_start(blk_rows[0:1, 0, :], A["L3_gnn_bv"].unsqueeze(0)[:, bass.ds((H3 - 1 - i) * D, D)]).then_inc(row_in, 16)

        @on("sp")
        def _(sp, o):
            load_head(sp, 0, None)
            with sp.Fori(0, H3 - 1) as i:
                load_head(sp, i + 1, i)
            for nm, s, job in L3W:
                ring.last[s] = (job, H3 - 1)

        @on("pe")
        def _(pe, o):
            pe.wait_ge(xn_ready, NORM["l3"] + 1)
            pe_transpose(pe, "l3x", xn)
            for c in range(KC):
                banks.drained(pe, f"l3x{c}")
            with banks.loop(H3, 24), pe.Fori(0, H3) as i:
                pe.wait_ge(row_in, 16 * (i + 1))
                for nm, s in (("q", 5), ("k", 6)):
                    w = ring.get(pe, s, i)
                    for c in range(KC):
                        pe_cols(pe, f"l3{nm}{c}", xT, w, c * P, i)
                w = ring.get(pe, 7, i)
                for t in range(NT):
                    pe_rows(pe, f"l3v{t}", xT, w, t, blk_rows[0:1, 0, :], i)
                for c in range(KC):
                    banks.drained(pe, f"l3q{c}", i)
                    banks.drained(pe, f"l3k{c}", i)
                for t in range(NT):
                    b = banks.open(pe, f"l3s{t}", i)
                    for c in range(KC):
                        last = mm(b[:, 0:N], q3[:, c, t * P:(t + 1) * P], k3[:, c, :], c == 0, c == KC - 1)
                    last.then_inc(banks.full_of(f"l3s{t}"), 1)
                for t in range(NT):
                    banks.drained(pe, f"l3v{t}", i)
                pe_att_transpose(pe, "l3", U3 + i, 0, i)
                w = ring.get(pe, 0, i)
                for c in range(NT):
                    banks.drained(pe, f"l3p{c}", i)
                for d in range(KC):
                    b = banks.open(pe, f"l3a{d}", i)
                    for c in range(NT):
                        mm(b[:, 0:N], v3[:, c, d * P:(d + 1) * P], probsT[:, 0, c, :], c == 0, False)
                    for c in range(KC):
                        last = mm(b[:, 0:N], w[:, c, d * P:(d + 1) * P], xT[:, c, :], False, c == KC - 1)
                    last.then_inc(banks.full_of(f"l3a{d}"), 1)
                w = ring.get(pe, 1, i)
                for d in range(KC):
                    banks.drained(pe, f"l3a{d}", i)
                for t in range(NT):
                    pe_rows(pe, f"l3l{t}", xa, w, t, None, i)
            ring.after_loop((5, 6, 7, 0, 1), H3)
            for t in range(NT):
                b = banks.open(pe, f"l3f{t}")
                for c in range(KC):
                    last = nc.tensor.transpose(b[:, c * P:(c + 1) * P], xa[:, c, t * P:(t + 1) * P], ident[:])
                last.then_inc(banks.full_of(f"l3f{t}"), 1)

        @on("act")
        def _(act, o):
            act_norm(act, NORM["l3"])
            act_transposed(act, "l3x", xT)

            def biased(name, dst, table, c, i):
                b = banks.filled(act, name, i)
                nc.scalar.activation(dst, b[:, 0:N], ACT.Identity, bias=table[:, bass.ds((H3 - 1 - i) * KC + c, 1)]).then_inc(
                    banks.free_of(name), 1)

            with act.Fori(0, H3) as i:
                for c in range(KC):
                    biased(f"l3q{c}", q3[:, c, :], c_bq3, c, i)
                for c in range(KC):
                    biased(f"l3k{c}", k3[:, c, :], c_bk3, c, i)
                for t in range(NT):
                    act_copy(act, f"l3v{t}", v3[:, t, :], D, i)
                act_att_exp(act, U3 + i, 0)
                act_att_transposed(act, "l3", 0, i)
                for d in range(KC):
                    biased(f"l3a{d}", xa[:, d, :], c_bs3, d, i)
            act_norm(act, NORM["l3b"])

        @on("dve")
        def _(dve, od):
            dve_norm(dve, od, NORM["l3"], x, xn)
            for t in range(NT):
                last = nc.vector.tensor_copy(acc3[:, t, :], BC["L3_gnn_blin"])
            od.link(last)
            with od.loop(H3, 5) as i:
                dve_att_scores(dve, od, "l3", U3 + i, 0, 0, float(D) ** -0.5, mask_dst, i)
                dve_att_probs(dve, od, U3 + i, 0, cnt_dst)
                for t in range(NT):
                    b = banks.filled(dve, f"l3l{t}", i)
                    nc.vector.tensor_tensor(acc3[:, t, :], acc3[:, t, :], b, ALU.add).then_inc(banks.free_of(f"l3l{t}"), 1)
                for t in range(NT):
                    banks.drained(dve, f"l3l{t}", i)
            for t in range(NT):
                banks.drained(dve, f"l3l{t}", H3 - 1)
                b = banks.filled(dve, f"l3f{t}")
                nc.vector.tensor_tensor(acc3[:, t, :], acc3[:, t, :], b, ALU.add).then_inc(banks.free_of(f"l3f{t}"), 1)
            for t in range(NT):
                banks.drained(dve, f"l3f{t}")
            dve_norm(dve, od, NORM["l3b"], acc3, acc3, BC["L3_gnn_gamma"], BC["L3_gnn_beta"])
            dve.wait_ge(xn_ready, NORM["l3b"] + 1)
            od.link(nc.vector.tensor_tensor(x[:], x[:], acc3[:], ALU.add))

        OPTS = 3
        H = 8
        DK = D // H
        U4 = U3 + H3
        q4, k4, v4, o4 = view(0, KC, N), view(1536, KC, N), view(3072, NT, D), view(4608, KC, N)
        acc4 = view(6144, NT, D)
        route = sb("route", [P, 32])
        kv_in = sems("kv_in", 2)
        q_slot, k_slot, v_slot, o_slot, r_slot = 2, 3, 4, 5, 6

        @on("sp")
        def _(sp, o):
            ring.load(sp, banks, r_slot, [(ring.slot(r_slot)[:, :, 0:P], A["L3_ffn_r_w1"].rearrange("(c p) n -> p c n", p=P))])
            for i in range(OPTS):
                for nm, s, job in (("wq", q_slot, "f3q3"), ("wo", o_slot, "f3y2")):
                    ring.load(sp, banks, s, [(ring.slot(s), A[f"L3_ffn_{nm}{i}"].rearrange("(c p) n -> p c n", p=P))])
                    ring.last[s] = (job, i)
                for nm, s, j, job in (("wk", k_slot, 0, "f3k3"), ("wv", v_slot, 1, "f3v2")):
                    if ring.last[s] is not None:
                        banks.filled(sp, *ring.last[s])
                    w = A[f"L3_ffn_{nm}{i}"]
                    rep = H // (w.shape[1] // DK)
                    for h in range(H):
                        sp.dma_start(ring.slot(s)[:, :, h * DK:(h + 1) * DK],
                                     w[:, h // rep * DK:(h // rep + 1) * DK].rearrange("(c p) n -> p c n", p=P)).then_inc(kv_in[j], 16)
                    ring.last[s] = (job, i)

        @on("pe")
        def _(pe, o):
            pe.wait_ge(xn_ready, NORM["f3"] + 1)
            pe_transpose(pe, "f3x", xn)
            rw1 = ring.get(pe, r_slot)
            for c in range(KC):
                banks.drained(pe, f"f3x{c}")
            pe.wait_ge(step_ready, 7)
            b = banks.open(pe, "f3r")
            for c in range(KC):
                last = mm(b[:, 0:1], rw1[:, c, 0:P], route[:, c:c + 1], c == 0, c == KC - 1)
            last.then_inc(banks.full_of("f3r"), 1)
            banks.drained(pe, "f3r")
            b = banks.open(pe, "f3g")
            mm(b[0:1, 0:OPTS], route[:, 4:5], rw2, True, False)
            mm(b[0:1, 0:OPTS], ones[0:1, 0:1], r_rb2, False, True).then_inc(banks.full_of("f3g"), 1)
            pe.wait_ge(step_ready, 8)
            b = banks.open(pe, "f3s")
            mm(b[:, 0:OPTS], ones[0:1, :], route[0:1, 20:20 + OPTS], True, True).then_inc(banks.full_of("f3s"), 1)

            def scores(h, i):
                r = slice(DK * (h % 2), DK * (h % 2) + DK)
                for t in range(NT):
                    b = banks.open(pe, f"f3h{h}s{t}", i)
                    mm(b[:, 0:N], q4[r, h // 2, t * P:(t + 1) * P], k4[r, h // 2, :], True, True).then_inc(
                        banks.full_of(f"f3h{h}s{t}"), 1)

            def values(h, i):
                pe_att_transpose(pe, f"f3h{h}", U4 + H * i + h, h % 2, i)
                for c in range(NT):
                    banks.drained(pe, f"f3h{h}p{c}", i)
                b = banks.open(pe, f"f3o{h}", i)
                for c in range(NT):
                    last = mm(b[:, 0:N], v4[:, c, h // 2 * P:(h // 2 + 1) * P], probsT[:, h % 2, c, :], c == 0, c == NT - 1)
                last.then_inc(banks.full_of(f"f3o{h}"), 1)

            with banks.loop(OPTS, 70), pe.Fori(0, OPTS) as i:
                w = ring.get(pe, q_slot, i)
                for c in range(KC):
                    pe_cols(pe, f"f3q{c}", xT, w, c * P, i)
                pe.wait_ge(kv_in[0], 16 * H * (i + 1))
                for c in range(KC):
                    pe_cols(pe, f"f3k{c}", xT, ring.slot(k_slot), c * P, i)
                pe.wait_ge(kv_in[1], 16 * H * (i + 1))
                for t in range(NT):
                    pe_rows(pe, f"f3v{t}", xT, ring.slot(v_slot), t, None, i)
                for c in range(KC):
                    banks.drained(pe, f"f3q{c}", i)
                    banks.drained(pe, f"f3k{c}", i)
                for t in range(NT):
                    banks.drained(pe, f"f3v{t}", i)
                for h in range(H + 1):
                    if h < H:
                        scores(h, i)
                    if h >= 1:
                        values(h - 1, i)
                for h in range(H):
                    banks.drained(pe, f"f3o{h}", i)
                w = ring.get(pe, o_slot, i)
                for t in range(NT):
                    pe_rows(pe, f"f3y{t}", o4, w, t, None, i)

        @on("act")
        def _(act, o):
            act_norm(act, NORM["f3"])
            act_transposed(act, "f3x", xT)
            b = banks.filled(act, "f3r")
            nc.scalar.activation(route[:, 4:5], b[:, 0:1], ACT.Relu, bias=c_rb1).then_inc(banks.free_of("f3r"), 1)
            banks.drained(act, "f3g")
            nc.scalar.activation(route[0:1, 12:15], route[0:1, 8:11], ACT.Exp).then_inc(gate_exp, 1)
            with act.Fori(0, OPTS) as i:
                for c in range(KC):
                    act_copy(act, f"f3q{c}", q4[:, c, :], N, i)
                for c in range(KC):
                    act_copy(act, f"f3k{c}", k4[:, c, :], N, i)
                for t in range(NT):
                    act_copy(act, f"f3v{t}", v4[:, t, :], D, i)
                for h in range(H + 1):
                    if h < H:
                        act_att_exp(act, U4 + H * i + h, h % 2)
                    if h >= 1:
                        g = h - 1
                        act_att_transposed(act, f"f3h{g}", g % 2, i)
                        r = slice(DK * (g % 2), DK * (g % 2) + DK)
                        b = banks.filled(act, f"f3o{g}", i)
                        nc.scalar.activation(o4[r, g // 2, :], b[r, 0:N], ACT.Copy).then_inc(banks.free_of(f"f3o{g}"), 1)

        @on("dve")
        def _(dve, od):
            dve_norm(dve, od, NORM["f3"], x, xn)
            for c in range(KC):
                banks.drained(dve, f"f3x{c}")
            od.link(nc.vector.tensor_reduce(route[:, 0:4], xT[:], AX, ALU.add))
            nc.vector.tensor_scalar(route[:, 0:4], route[:, 0:4], 1.0 / N, None, ALU.mult).then_inc(step_ready, 1)
            b = banks.filled(dve, "f3g")[0:1, 0:OPTS]
            od.link(nc.vector.tensor_reduce(route[0:1, 5:6], b, AX, ALU.max))
            nc.vector.tensor_scalar(route[0:1, 8:11], b, route[0:1, 5:6], None, ALU.subtract).then_inc(banks.free_of("f3g"), 1)
            dve.wait_ge(gate_exp, 4)
            od.link(nc.vector.tensor_reduce(route[0:1, 5:6], route[0:1, 12:15], AX, ALU.add))
            od.link(nc.vector.reciprocal(route[0:1, 5:6], route[0:1, 5:6]))
            od.link(nc.vector.tensor_scalar(route[0:1, 12:15], route[0:1, 12:15], route[0:1, 5:6], None, ALU.mult))
            od.link(nc.vector.tensor_reduce(route[0:1, 6:7], route[0:1, 12:15], AX, ALU.max))
            od.link(nc.vector.tensor_scalar(route[0:1, 16:19], route[0:1, 12:15], route[0:1, 6:7], None, ALU.is_equal))
            od.link(nc.vector.tensor_tensor(route[0:1, 16:19], route[0:1, 16:19], iota_back[0:1, 0:OPTS], ALU.mult))
            od.link(nc.vector.tensor_reduce(route[0:1, 6:7], route[0:1, 16:19], AX, ALU.min))
            nc.vector.tensor_scalar(route[0:1, 20:23], iota_back[0:1, 0:OPTS], route[0:1, 6:7], None,
                                    ALU.is_equal).then_inc(step_ready, 1)
            b = banks.filled(dve, "f3s")
            nc.vector.tensor_copy(route[:, 24:24 + OPTS], b[:, 0:OPTS]).then_inc(banks.free_of("f3s"), 1)
            banks.drained(dve, "f3s")
            od.link(nc.vector.memset(acc4[:], 0.0))
            with od.loop(OPTS, 5 * H - H) as i:
                for h in range(H + 1):
                    if h < H:
                        dve_att_scores(dve, od, f"f3h{h}", 0, h, h % 2, float(DK) ** -0.5, None, i)
                    if h >= 1:
                        dve_att_probs(dve, od, U4 + H * i + h - 1, (h - 1) % 2, None)
                for t in range(NT):
                    b = banks.filled(dve, f"f3y{t}", i)
                    nc.vector.scalar_tensor_tensor(out=acc4[:, t, :], in0=b, scalar=route[:, bass.ds(24 + i, 1)],
                                                   in1=acc4[:, t, :], op0=ALU.mult, op1=ALU.add).then_inc(banks.free_of(f"f3y{t}"), 1)
                for t in range(NT):
                    banks.drained(dve, f"f3y{t}", i)
            for t in range(NT):
                banks.drained(dve, f"f3y{t}", OPTS - 1)
            od.link(nc.vector.tensor_tensor(x[:], x[:], acc4[:], ALU.add))

        engines = (("sync", "sp"), ("scalar", "act"), ("vector", "dve"), ("tensor", "pe"), ("gpsimd", "pool"))
        block = ctx.enter_context(nc.Block())

        @block.tensor
        def _(pe):
            for f in layers["pe"]:
                f(pe, None)

        @block.scalar
        def _(act):
            o = Order(act, act_order)
            for f in layers["act"]:
                f(act, o)

        @block.vector
        def _(dve):
            od = Order(dve, dve_order)
            for f in layers["dve"]:
                f(dve, od)
            nc.vector.memset(gate[:, 15, 0:1], 0.0).then_inc(out_ready, 1)

        @block.gpsimd
        def _(pool):
            op = Order(pool, pool_order)
            for f in layers["pool"]:
                f(pool, op)

        @block.sync
        def _(sp):
            for f in layers["sp"]:
                f(sp, None)
            sp.wait_ge(out_ready, 1)
            sp.dma_start(tiled(out), x[:]).then_inc(stored, 16)
            sp.wait_ge(stored, 16)


INPUTS = ["x", "src", "dst", "edge_type_8", "edge_weight", "node_vec1"] + ["L0_gnn_" + n for n in (
    "Wv bv Ww bw Wa ba gamma beta").split()] + ["L0_ffn_" + n for n in "w_gating gamma w1 w2".split()] + [
    "L1_gnn_" + n for n in (
        "f_w1 f_b1 f_w2 f_b2 s1_w s1_b b1_w b1_b wq bq wk bk wv bv wo bo s2_w s2_b b2_w b2_b m_w1 m_b1 m_w2 m_b2").split()] + [
    "L1_ffn_" + n for n in "w_gating w1 w2".split()] + [
    "L2_gnn_" + n for n in "W a_src a_dst et_emb ln_gamma ln_beta".split()] + [
    "L2_ffn_" + n for n in "expert_weights expert_biases mixer_w mixer_b".split()] + [
    "L3_gnn_" + n for n in "Wq bq Wk bk Wv bv Wskip bskip Wlin blin gamma beta".split()] + [
    "L3_ffn_" + n for n in "r_w1 r_b1 r_w2 r_b2 wq0 wk0 wv0 wo0 wq1 wk1 wv1 wo1 wq2 wk2 wv2 wo2".split()]


def kernel(**inputs):
    import numpy as _np
    import concourse.bacc as _bacc
    from concourse import mybir as _mybir
    from concourse.bass_utils import run_bass_kernel_spmd as _run

    nc = _bacc.Bacc("TRN2", target_bir_lowering=False, num_devices=1)
    arrays, aps = {}, {}
    for name in INPUTS:
        a = _np.ascontiguousarray(inputs[name])
        arrays[f"in_{name}"] = a
        aps[name] = nc.dram_tensor(f"in_{name}", a.shape, _mybir.dt.from_np(a.dtype), kind="ExternalInput").ap()
    out = nc.dram_tensor("out_x", (N, D), F32, kind="ExternalOutput").ap()
    with nc.allow_non_contiguous_dma("bias columns and weight tiles are loaded in the layout that the engines read"):
        gnn_ffn_program(nc, aps, out)
    r = _run(nc, [arrays], core_ids=[0])
    return r.results[0]["out_x"]
```

```python
from contextlib import ExitStack, contextmanager

import concourse.bass as bass
from concourse import mybir

P = 128
N = 384
NT = N // P
D = 512
KC = D // P
E = 12288
ET = E // P
H8 = 8
HD = D // H8
EPS = 1e-5
MASKED = -1.0e30
SLOTS = 8
UNROLL = 8
ZB = 4
RB = 4
NB = 8
F32 = mybir.dt.float32
BF16 = mybir.dt.bfloat16
I32 = mybir.dt.int32
U32 = mybir.dt.uint32
ALU = mybir.AluOpType
ACT = mybir.ActivationFunctionType
AX = mybir.AxisListType.X


class Banks:

    def __init__(self, psum, full, free):
        self.psum, self.full, self.free = psum, full, free
        self.uses, self.at, self.jobs, self.per = [0] * NB, 0, {}, None

    def open(self, pe, name, i=None):
        b = self.at
        self.at = (b + 1) % NB
        before, coef = self.uses[b], (self.per[b] if self.per else 0)
        self.uses[b] += 1
        self.jobs[name] = (b, before, coef)
        if before > 0:
            pe.wait_ge(self.free[b], before + i * coef if coef else before)
        return self.psum[:, b, :]

    @contextmanager
    def loop(self, trips, jobs, first=0):
        self.at = first
        start = list(self.uses)
        self.per = [sum((first + j) % NB == b for j in range(jobs)) for b in range(NB)]
        yield
        done = [u - s for u, s in zip(self.uses, start)]
        assert done == self.per, (sum(done), jobs)
        self.uses = [s + trips * k for s, k in zip(start, self.per)]
        self.per = None

    def count(self, name, i):
        b, before, coef = self.jobs[name]
        return b, (before + 1 + i * coef if coef and i is not None else before + 1)

    def full_of(self, name):
        return self.full[self.jobs[name][0]]

    def free_of(self, name):
        return self.free[self.jobs[name][0]]

    def filled(self, eng, name, i=None):
        b, n = self.count(name, i)
        eng.wait_ge(self.full[b], n)
        return self.psum[:, b, :]

    def drained(self, eng, name, i=None):
        b, n = self.count(name, i)
        eng.wait_ge(self.free[b], n)


class Order:

    def __init__(self, eng, sem):
        self.eng, self.sem, self.n, self.more, self.looping = eng, sem, 0, 0, False

    def link(self, ins):
        self.n += 1
        ins.then_inc(self.sem, 1)
        self.eng.wait_ge(self.sem, self.n + self.more)

    def settle(self):
        if self.looping:
            self.eng.nop(nofuse=True)

    @contextmanager
    def loop(self, trips, per):
        start, self.looping = self.n, True
        with self.eng.Fori(0, trips) as i:
            self.more = i * per
            yield i
        assert self.n - start == per, (self.n - start, per)
        self.n, self.more, self.looping = start + trips * per, 0, False


class Ring:

    def __init__(self, slots, arrived):
        self.slots, self.arrived = slots, arrived
        self.got, self.per = [0] * SLOTS, None
        self.last = [None] * SLOTS

    def slot(self, s):
        return self.slots[:, s, :, :]

    def get(self, pe, s, i=None):
        self.got[s] += 1
        n = 16 * self.got[s]
        pe.wait_ge(self.arrived[s], n if i is None else n + i * 16)
        return self.slot(s)

    def after_loop(self, slots, trips):
        for s in slots:
            self.got[s] += trips - 1

    def load(self, sp, banks, s, pairs, used=None, i=None):
        job = used if used is not None else self.last[s]
        if job is not None:
            banks.filled(sp, *job)
            if used is not None:
                sp.nop(nofuse=True)
        assert len(pairs) == 1
        for dst, src in pairs:
            sp.dma_start(dst, src).then_inc(self.arrived[s], 16)


def gnn_ffn_program(nc, A, out):
    ctx = ExitStack()
    with ctx:
        def sb(name, shape, dt=F32):
            return ctx.enter_context(nc.sbuf_tensor(name, shape, dt))

        def sem(name):
            return ctx.enter_context(nc.semaphore(name))

        def sems(name, n):
            return [sem(f"{name}{i}") for i in range(n)]

        def dram(name, shape):
            return nc.dram_tensor(name, shape, F32, kind="Internal").ap()

        psum = ctx.enter_context(nc.psum_tensor("psum", [P, NB, 512], F32))
        banks = Banks(psum, sems("bank_full", NB), sems("bank_free", NB))
        ring = Ring(sb("ring", [P, SLOTS, KC, D]), sems("slot_arrived", SLOTS))

        x = sb("x", [P, NT, D])
        xn = sb("xn", [P, NT, D])
        xT = sb("xT", [P, KC, N])
        xn2 = sb("xn2", [P, NT, D])
        xT2 = sb("xT2", [P, KC, N])
        cnt_src = sb("cnt_src", [P, NT, N])
        cnt_dst = sb("cnt_dst", [P, NT, N])
        mask_src = sb("mask_src", [P, NT, N])
        mask_dst = sb("mask_dst", [P, NT, N])
        ident = sb("ident", [P, P])
        tri = sb("tri", [P, P])
        ones = sb("ones", [P, P])
        zeros = sb("zeros", [P, 512])
        iota = sb("iota", [P, N])
        iota_back = sb("iota_back", [P, 16])
        src_i = sb("src_i", [P, ET], I32)
        dst_i = sb("dst_i", [P, ET], I32)
        typ_i = sb("typ_i", [P, ET], I32)
        sd_i = sb("sd_i", [P, ET, 3], I32)
        src_f = sb("src_f", [P, ET])
        dst_f = sb("dst_f", [P, ET])
        typ_f = sb("typ_f", [P, ET])
        ew = sb("ew", [P, ET])
        stats = sb("stats", [P, NT, 6])
        mv = sb("mv", [P, NT, 2])
        vare = sb("vare", [P, NT])
        std = sb("std", [P, NT])
        rstd = sb("rstd", [P, NT])
        gate = sb("gate", [P, 16, 64])
        idx = sb("idx", [P, UNROLL, 3], I32)

        cols = sb("cols", [P, 160])
        rows = sb("rows", [1, 1536])
        bc = sb("bc", [P, 7, D])
        small = sb("small", [P, 512])
        blk_rows = sb("blk_rows", [1, 3, D])
        AW = 13400
        arena = sb("arena", [P, AW])

        def view(off, *shape):
            n = 1
            for s in shape:
                n *= s
            assert off + n <= AW, (off, n)
            v = arena[:, off:off + n]
            if len(shape) == 2:
                v = v.rearrange("p (a b) -> p a b", a=shape[0])
            elif len(shape) == 3:
                v = v.rearrange("p (a b c) -> p a b c", a=shape[0], b=shape[1])
            return v

        params = sem("params")
        x_loaded = sem("x_loaded")
        edges_loaded = sem("edges_loaded")
        consts_ready = sem("consts_ready")
        pool_order = sem("pool_order")
        dve_order = sem("dve_order")
        act_order = sem("act_order")
        var_ready = sem("var_ready")
        std_ready = sem("std_ready")
        xn_ready = sem("xn_ready")
        hot_ready = sem("hot_ready")
        hot_used = sem("hot_used")
        mask_done = sem("mask_done")
        logits_ready = sem("logits_ready")
        gate_exp = sem("gate_exp")
        tables_stored = sem("tables_stored")
        rows_landed = sems("rows_landed", ZB)
        cols_landed = sems("cols_landed", ZB)
        w_landed = sems("w_landed", UNROLL)
        w_loaded = sem("w_loaded")
        masked_ready = sem("masked_ready")
        neg_max = sem("neg_max")
        exp_done = sem("exp_done")
        relu_done = sem("relu_done")
        w_ready = sem("w_ready")
        edge_free = sem("edge_free")
        scores_max = sem("scores_max")
        max_ready = sem("max_ready")
        max_stored = sem("max_stored")
        diff_ready = sem("diff_ready")
        ex_done = sem("ex_done")
        msg_free = sem("msg_free")
        msg_ready = sem("msg_ready")
        msg_used = sem("msg_used")
        elu_in = sem("elu_in")
        elu_exp = sem("elu_exp")
        mod_ready = sem("mod_ready")
        t_ready = sem("t_ready")
        e_done = sem("e_done")
        p_ready = sem("p_ready")
        step_ready = sem("step_ready")
        pe_col = sem("pe_col")
        out_ready = sem("out_ready")
        stored = sem("stored")

        bc0 = 10336
        loads = []

        def col(name, n, p=P, off=[0]):
            o = off[0]
            off[0] += n
            loads.append((cols[0:p, o:o + n], A[name], n, p))
            return cols[0:p, o:o + n]

        c_s1b = col("L1_gnn_s1_b", 16)
        c_b1b = col("L1_gnn_b1_b", 16)
        c_bq = col("L1_gnn_bq", 16)
        c_bk = col("L1_gnn_bk", 16)
        c_s2b = col("L1_gnn_s2_b", 16)
        c_b2b = col("L1_gnn_b2_b", 16)
        c_mb1 = col("L1_gnn_m_b1", 16)
        c_bq3 = col("L3_gnn_bq", 16)
        c_bk3 = col("L3_gnn_bk", 16)
        c_bs3 = col("L3_gnn_bskip", 16)
        loads = [(d, (s.rearrange("b (c p) -> p (b c)", p=P) if len(s.shape) == 2 else s.rearrange("(c p) -> p c", p=P)))
                 for d, s, n, p in loads]
        c_g0 = small[:, 0:4]
        loads.append((c_g0, A["L0_ffn_gamma"].rearrange("(c p) -> p c", p=P)))
        c_fb1, c_fb2 = small[0:16, 4:5], small[0:16, 5:6]
        loads.append((c_fb1, A["L1_gnn_f_b1"].unsqueeze(1)))
        loads.append((c_fb2, A["L1_gnn_f_b2"].unsqueeze(1)))
        c_rb1 = small[:, 6:7]
        loads.append((c_rb1, A["L3_ffn_r_b1"].unsqueeze(1)))
        r_rb2 = small[0:1, 7:10]
        loads.append((r_rb2, A["L3_ffn_r_b2"].unsqueeze(0)))
        ba0 = small[:, 10:11]
        loads.append((ba0, A["L0_gnn_ba"].partition_broadcast(P)))
        r_mixb = small[0:1, 12:20]
        loads.append((r_mixb, A["L2_ffn_mixer_b"].unsqueeze(0)))
        et_bc = small[:, 20:84]
        loads.append((et_bc, A["L2_gnn_et_emb"].rearrange("a b -> (a b)").partition_broadcast(P)))
        wg0 = small[:, 84:108].rearrange("p (c e) -> p c e", c=KC)
        loads.append((wg0, A["L0_ffn_w_gating"].rearrange("(c p) e -> p c e", p=P)))
        wg1 = small[:, 108:172].rearrange("p (c e) -> p c e", c=KC)
        loads.append((wg1, A["L1_ffn_w_gating"].rearrange("(c p) e -> p c e", p=P)))
        fw1 = small[0:64, 172:188]
        loads.append((fw1, A["L1_gnn_f_w1"]))
        fw2 = small[0:16, 188:204]
        loads.append((fw2, A["L1_gnn_f_w2"]))
        rw2 = small[:, 204:207]
        loads.append((rw2, A["L3_ffn_r_w2"]))
        mixT = small[:, 208:240].rearrange("p (c e) -> p c e", c=KC)
        wa = small[:, 240:368]
        loads.append((wa, A["L0_gnn_Wa"].rearrange("d a -> (a d)").partition_broadcast(P)))
        r_bw = rows[0:1, 0:1024]
        loads.append((r_bw, A["L0_gnn_bw"].unsqueeze(0)))
        r_bv0 = rows[0:1, 1024:1536]
        loads.append((r_bv0, A["L0_gnn_bv"].unsqueeze(0)))
        BC = {}
        for j, nm in enumerate(("L2_gnn_a_src", "L2_gnn_a_dst", "L2_gnn_ln_gamma", "L2_gnn_ln_beta", "L3_gnn_gamma",
                                "L3_gnn_beta", "L3_gnn_blin")):
            a = A[nm]
            BC[nm] = bc[:, j, :]
            loads.append((bc[:, j, :], (a.rearrange("a b -> (a b)") if len(a.shape) == 2 else a).partition_broadcast(P)))
        early = mask_src[:].rearrange("p c n -> p (c n)")
        BC["L0_gnn_gamma"], BC["L0_gnn_beta"] = early[:, 0:D], early[:, D:2 * D]
        for nm in ("L0_gnn_gamma", "L0_gnn_beta"):
            loads.append((BC[nm], A[nm].partition_broadcast(P)))
        PARAMS = 16 * len(loads)

        UW = 2 * D + H8
        tab_u = dram("tab_u", (N, UW))
        tab_v = dram("tab_v", (N, UW))
        tab_w = dram("tab_w", (N * N, H8))
        tab_h = dram("tab_h", (N, D))
        tab_es = dram("tab_es", (N, H8))
        tab_ed = dram("tab_ed", (N, H8))
        tab_m2 = dram("tab_m2", (N, H8))

        def tiled(t):
            return t.rearrange("(c p) n -> p c n", p=P)

        def mm(o, a, b, start, stop):
            return nc.tensor.matmul(o, a, b, start=start, stop=stop)

        def pe_transpose(pe, tag, src, i=None):
            for c in range(KC):
                b = banks.open(pe, f"{tag}{c}", i)
                for t in range(NT):
                    last = nc.tensor.transpose(b[:, t * P:(t + 1) * P], src[:, t, c * P:(c + 1) * P], ident[:])
                last.then_inc(banks.full_of(f"{tag}{c}"), 1)

        def act_copy(act, name, dst, w=512, i=None):
            b = banks.filled(act, name, i)
            nc.scalar.activation(dst, b[:, 0:w], ACT.Copy).then_inc(banks.free_of(name), 1)

        def act_transposed(act, tag, dst, i=None):
            for c in range(KC):
                act_copy(act, f"{tag}{c}", dst[:, c, :], N, i)

        def pe_rows(pe, name, aT, w, t, bias=None, i=None, col0=0, n=D):
            b = banks.open(pe, name, i)
            for c in range(KC):
                last = mm(b[:, 0:n], aT[:, c, t * P:(t + 1) * P], w[:, c, col0:col0 + n], c == 0,
                          c == KC - 1 and bias is None)
            if bias is not None:
                last = mm(b[:, 0:n], ones[0:1, :], bias, False, True)
            last.then_inc(banks.full_of(name), 1)

        def pe_cols(pe, name, aT, w, col0, i=None):
            b = banks.open(pe, name, i)
            for c in range(KC):
                last = mm(b[:, 0:N], w[:, c, col0:col0 + P], aT[:, c, :], c == 0, c == KC - 1)
            last.then_inc(banks.full_of(name), 1)

        def dve_norm(dve, od, call, src, dst, gamma=None, beta=None):
            od.settle()
            for t in range(NT):
                last = nc.vector.bn_stats(stats[:, t, :], src[:, t, :])
            od.link(last)
            od.settle()
            for t in range(NT):
                last = nc.vector.bn_aggr(mv[:, t, :], stats[:, t, :])
            od.link(last)
            nc.vector.tensor_scalar_add(vare[:], mv[:, :, 1], EPS).then_inc(var_ready, 1)
            dve.wait_ge(std_ready, call + 1)
            od.link(nc.vector.reciprocal(rstd[:], std[:]))
            for t in range(NT):
                last = nc.vector.tensor_scalar(dst[:, t, :], src[:, t, :], mv[:, t, 0:1], rstd[:, t:t + 1],
                                               ALU.subtract, ALU.mult)
            if gamma is not None:
                od.link(last)
                for t in range(NT):
                    last = nc.vector.tensor_tensor(dst[:, t, :], dst[:, t, :], gamma, ALU.mult)
            if beta is not None:
                od.link(last)
                for t in range(NT):
                    last = nc.vector.tensor_tensor(dst[:, t, :], dst[:, t, :], beta, ALU.add)
            last.then_inc(xn_ready, 1)

        def act_norm(act, call):
            act.wait_ge(var_ready, call + 1)
            nc.scalar.activation(std[:], vare[:], ACT.Sqrt).then_inc(std_ready, 1)

        def dve_softmax_logits(dve, od, name, e, call):
            b = banks.filled(dve, name)[:, 0:NT * e].rearrange("p (t e) -> p t e", t=NT)
            pr, mx = g3(0, e), gate[:, 1, 0:NT]
            od.link(nc.vector.tensor_reduce(mx, b, AX, ALU.max))
            nc.vector.tensor_tensor(g3(2, e), b, mx.unsqueeze(2).broadcast_to([P, NT, e]),
                                    ALU.subtract).then_inc(banks.free_of(name), 1)
            dve.wait_ge(gate_exp, call + 1)
            od.link(nc.vector.tensor_reduce(gate[:, 1, 8:8 + NT], pr, AX, ALU.add))
            od.link(nc.vector.reciprocal(gate[:, 1, 16:16 + NT], gate[:, 1, 8:8 + NT]))
            od.link(nc.vector.tensor_tensor(pr, pr, gate[:, 1, 16:16 + NT].unsqueeze(2).broadcast_to([P, NT, e]), ALU.mult))

        def act_softmax_logits(act, name, e):
            banks.drained(act, name)
            nc.scalar.activation(g3(0, e), g3(2, e), ACT.Exp).then_inc(gate_exp, 1)

        def g3(j, e):
            return gate[:, j, 0:NT * e].rearrange("p (t e) -> p t e", t=NT)

        def dve_top1(od, pr, e, g, onehot, tmp):
            od.link(nc.vector.tensor_reduce(g, pr, AX, ALU.max))
            od.link(nc.vector.tensor_tensor(tmp, pr, g.unsqueeze(2).broadcast_to([P, NT, e]), ALU.is_equal))
            back = iota_back[:, 0:e].unsqueeze(1).broadcast_to([P, NT, e])
            od.link(nc.vector.tensor_tensor(tmp, tmp, back, ALU.mult))
            first = gate[:, 3, 0:NT]
            od.link(nc.vector.tensor_reduce(first, tmp, AX, ALU.min))
            od.link(nc.vector.tensor_tensor(onehot, back, first.unsqueeze(2).broadcast_to([P, NT, e]), ALU.is_equal))

        def pe_logits(pe, name, aT, w, e, bias=None):
            b = banks.open(pe, name)
            for t in range(NT):
                for c in range(KC):
                    last = mm(b[:, t * e:(t + 1) * e], aT[:, c, t * P:(t + 1) * P], w[:, c, :], c == 0,
                              c == KC - 1 and bias is None)
                if bias is not None:
                    last = mm(b[:, t * e:(t + 1) * e], ones[0:1, :], bias, False, True)
            last.then_inc(banks.full_of(name), 1)

        probs = view(AW - 4 * NT * N, 2, NT, N)
        probsT = view(AW - 2 * NT * N, 2, NT, N)
        amax = sb("amax", [P, 2, NT])
        asum = sb("asum", [P, 2, NT])

        def dve_att_scores(dve, od, tag, u, g, par, scale, mask, i):
            for t in range(NT):
                b = banks.filled(dve, f"{tag}s{t}", i)
                if mask is not None:
                    last = nc.vector.scalar_tensor_tensor(out=probs[:, par, t, :], in0=b[:, 0:N], scalar=scale,
                                                          in1=mask[:, t, :], op0=ALU.mult, op1=ALU.add)
                else:
                    last = nc.vector.tensor_scalar(probs[:, par, t, :], b[:, 0:N], scale, None, ALU.mult)
                last.then_inc(banks.free_of(f"{tag}s{t}"), 1)
            for t in range(NT):
                banks.drained(dve, f"{tag}s{t}", i)
            od.link(nc.vector.tensor_reduce(amax[:, par, :], probs[:, par, :, :], AX, ALU.max))
            nc.vector.tensor_scalar(amax[:, par, :], amax[:, par, :], -1.0, None, ALU.mult).then_inc(t_ready, 1)

        def act_att_exp(act, u, par):
            act.wait_ge(t_ready, u + 1)
            for t in range(NT):
                last = nc.scalar.activation(probs[:, par, t, :], probs[:, par, t, :], ACT.Exp, bias=amax[:, par, t:t + 1])
            last.then_inc(e_done, 1)

        def dve_att_probs(dve, od, u, par, count):
            dve.wait_ge(e_done, u + 1)
            pv = probs[:, par, :, :]
            if count is not None:
                od.link(nc.vector.tensor_tensor(pv, pv, count[:], ALU.mult))
            od.link(nc.vector.tensor_reduce(asum[:, par, :], pv, AX, ALU.add))
            od.link(nc.vector.tensor_scalar_max(asum[:, par, :], asum[:, par, :], 1.0e-30))
            od.link(nc.vector.reciprocal(asum[:, par, :], asum[:, par, :]))
            nc.vector.tensor_tensor(pv, pv, asum[:, par, :].unsqueeze(2).broadcast_to([P, NT, N]),
                                    ALU.mult).then_inc(p_ready, 1)

        def pe_att_transpose(pe, tag, u, par, i):
            pe.wait_ge(p_ready, u + 1)
            for c in range(NT):
                b = banks.open(pe, f"{tag}p{c}", i)
                for t in range(NT):
                    last = nc.tensor.transpose(b[:, t * P:(t + 1) * P], probs[:, par, t, c * P:(c + 1) * P], ident[:])
                last.then_inc(banks.full_of(f"{tag}p{c}"), 1)

        def act_att_transposed(act, tag, par, i):
            for c in range(NT):
                act_copy(act, f"{tag}p{c}", probsT[:, par, c, :], N, i)

        seg_max = view(4864, H8, N)
        w_edge = view(7936, ET, H8)
        neg = view(9568, 2, N)
        seg_node = view(9568 + 2 * N + 2 * D, NT, H8)
        ust = view(0, NT, UW)
        vst = view(NT * UW, NT, UW)
        zb = view(0, ZB, UW)
        hotb = arena[:, ZB * UW:ZB * UW + 2 * N].bitcast(BF16).rearrange("p (b k n) -> p b k n", b=2, k=2)
        w_row = view(ZB * UW + 2 * N, UNROLL, H8)
        masked = view(2 * NT * UW, 4 * N)
        prod0 = view(2 * NT * UW + 4 * N, 2 * D)
        wm = view(0, NT, N * H8)
        ost = view(NT * N * H8, NT, D)
        pw = view(NT * N * H8 + NT * D, 2, NT, N)
        pwT = [xT, xT2]
        wa99 = small[:, 368:496]
        go = view(0, RB, D)
        gm = view(RB * D, RB, H8)
        ex = view(RB * D + 40, RB, H8)
        msg = view(RB * D + 80, RB, 2, 264)
        hot = view(RB * D + 80 + RB * 528, RB, N)

        def dve_segment_max(t, b):
            for h in range(H8):
                last = nc.vector.scalar_tensor_tensor(out=seg_max[:, h, :], in0=neg[:, b, :],
                                                      scalar=w_edge[:, bass.ds(t, 1), h], in1=seg_max[:, h, :],
                                                      op0=ALU.add, op1=ALU.max)
            return last

        def pe_segment_max(pe, tag):
            for j in range(6):
                b = banks.open(pe, f"{tag}m{j}")
                for q in range(4):
                    c, h = (4 * j + q) // H8, (4 * j + q) % H8
                    last = nc.tensor.transpose(b[:, q * P:(q + 1) * P], seg_max[:, h, c * P:(c + 1) * P], ident[:])
                last.then_inc(banks.full_of(f"{tag}m{j}"), 1)

        def dve_segment_node(dve, tag):
            for j in range(6):
                b = banks.filled(dve, f"{tag}m{j}")
                flat = seg_node[:].rearrange("p c h -> p (c h)")[:, 4 * j:4 * j + 4]
                nc.vector.tensor_reduce(flat, b.rearrange("p (q l) -> p q l", q=4), AX,
                                        ALU.max).then_inc(banks.free_of(f"{tag}m{j}"), 1)

        def pool_gather(o, table, column, **more):
            return nc.gpsimd.indirect_dma_start(o, None, table, bass.IndirectOffsetOnAxis(ap=column.bitcast(U32), axis=0), **more)

        def pool_scatter_rows(pool, op, table, maxima):
            with op.loop(ET // RB, RB) as i:
                for b in range(RB):
                    t = RB * i + b
                    pool.wait_ge(msg_free, t + 1)
                    op.link(nc.gpsimd.tensor_copy(idx[:, b, :], sd_i[:, bass.ds(t, 1), :].rearrange("p a k -> p (a k)")))
                    pool.nop(nofuse=True)
                    pool_gather(gm[:, b, :], maxima, idx[:, b, 1:2]).then_inc(cols_landed[b], 16)
                    pool_gather(go[:, b, :], table, idx[:, b, 0:1]).then_inc(rows_landed[b], 16)

        def dve_scatter_rows(dve, od, key, landed_before):
            with od.loop(ET // RB, RB) as i:
                for k in range(RB + 1):
                    if k < RB:
                        b, t = k, RB * i + k
                        dve.wait_ge(cols_landed[b], 16 * (i + 1) + landed_before)
                        nc.vector.tensor_tensor(gm[:, b, :], w_edge[:, bass.ds(t, 1), :].rearrange("p a h -> p (a h)"),
                                                gm[:, b, :], ALU.subtract).then_inc(diff_ready, 1)
                        dve.wait_ge(msg_used, t + 1)
                        nc.vector.tensor_scalar(hot[:, b, :], iota[:], key[:, bass.ds(t, 1)], None, ALU.is_equal)
                    if k >= 1:
                        b, t = k - 1, RB * i + k - 1
                        dve.wait_ge(ex_done, t + 1)
                        nc.vector.tensor_copy(msg[:, b, :, 256:264], ex[:, b, :].unsqueeze(1).broadcast_to([P, 2, H8]))
                        dve.wait_ge(rows_landed[b], 16 * (i + 1) + landed_before)
                        for hf in range(2):
                            last = nc.vector.tensor_tensor(
                                msg[:, b, hf, 0:256].rearrange("p (h d) -> p h d", h=4),
                                go[:, b, hf * 256:hf * 256 + 256].rearrange("p (h d) -> p h d", h=4),
                                ex[:, b, hf * 4:hf * 4 + 4].unsqueeze(2).broadcast_to([P, 4, HD]), ALU.mult)
                        od.link(last)
                        nc.vector.memset(gate[:, 15, 0:1], 0.0).then_inc(msg_free, 1)
                        nc.vector.memset(gate[:, 15, 3:4], 0.0).then_inc(msg_ready, 1)

        def act_scatter_rows(act):
            with act.Fori(0, ET // RB) as i:
                for b in range(RB):
                    act.wait_ge(diff_ready, RB * i + b + 1)
                    nc.scalar.activation(ex[:, b, :], gm[:, b, :], ACT.Exp).then_inc(ex_done, 1)

        def pe_scatter_rows(pe, tag):
            bk = [[banks.open(pe, f"{tag}a{c}{hf}") for hf in range(2)] for c in range(NT)]
            for c in range(NT):
                for hf in range(2):
                    last = mm(bk[c][hf][:, 0:264], zeros[:, 0:P], zeros[:, 0:264], True, False)
            last.then_inc(msg_used, RB)
            with pe.Fori(0, ET // RB) as i:
                for b in range(RB):
                    pe.wait_ge(msg_ready, RB * i + b + 1)
                    for c in range(NT):
                        for hf in range(2):
                            last = mm(bk[c][hf][:, 0:264], hot[:, b, c * P:(c + 1) * P], msg[:, b, hf, :], False, False)
                    last.then_inc(msg_used, 1)
            for c in range(NT):
                for hf in range(2):
                    mm(bk[c][hf][:, 0:264], zeros[:, 0:P], zeros[:, 0:264], False, True).then_inc(
                        banks.full_of(f"{tag}a{c}{hf}"), 1)

        def dve_scatter_sums(dve, od, tag, tiny, add):
            for c in range(NT):
                for hf in range(2):
                    b = banks.filled(dve, f"{tag}a{c}{hf}")
                    den = gate[:, 4, 8 * (2 * c + hf):8 * (2 * c + hf) + 8]
                    od.link(nc.vector.tensor_scalar(den, b[:, 256:264], tiny, None, ALU.add if add else ALU.max))
                    od.link(nc.vector.reciprocal(den, den))
                    nc.vector.tensor_tensor(
                        xn2[:, c, hf * 256:hf * 256 + 256].rearrange("p (h d) -> p h d", h=4),
                        b[:, 0:256].rearrange("p (h d) -> p h d", h=4),
                        den[:, hf * 4:hf * 4 + 4].unsqueeze(2).broadcast_to([P, 4, HD]),
                        ALU.mult).then_inc(banks.free_of(f"{tag}a{c}{hf}"), 1)
            for c in range(NT):
                for hf in range(2):
                    banks.drained(dve, f"{tag}a{c}{hf}")

        layers = {"sp": [], "act": [], "dve": [], "pe": [], "pool": []}

        def on(engine):
            def add(f):
                layers[engine].append(f)
                return f
            return add

        NORM = dict(l0=0, l0b=1, f0=2, f0b=3, l1=4, blk=5, f1=13, l2=14, l2b=15, f2=16, l3=17, l3b=18, f3=19)

        @on("sp")
        def _(sp, o):
            sp.dma_start(x[:], tiled(A["x"])).then_inc(x_loaded, 16)
            for dst, nm in ((src_i, "src"), (dst_i, "dst"), (typ_i, "edge_type_8"), (ew, "edge_weight")):
                sp.dma_start(dst[:], A[nm].rearrange("(p t) -> p t", p=P)).then_inc(edges_loaded, 16)

        @on("act")
        def _(act, o):
            for dst, src in loads:
                act.dma_start(dst, src).then_inc(params, 16)

        @on("pool")
        def _(pool, op):
            nc.gpsimd.memset(ident[:], 0.0)
            nc.gpsimd.memset(ones[:], 1.0)
            nc.gpsimd.memset(zeros[:], 0.0)
            nc.gpsimd.iota(iota[:], pattern=[[1, N]], base=0, channel_multiplier=0, allow_small_or_imprecise_dtypes=True)
            op.link(nc.gpsimd.iota(iota_back[:], pattern=[[1, 16]], base=-64, channel_multiplier=0,
                                   allow_small_or_imprecise_dtypes=True))
            nc.gpsimd.affine_select(out=ident[:], in_=ident[:], compare_op=ALU.not_equal, fill=1.0, base=0,
                                    pattern=[[-1, P]], channel_multiplier=1)
            nc.gpsimd.affine_select(out=tri[:], in_=ones[:], compare_op=ALU.is_gt, fill=0.0, base=0,
                                    pattern=[[1, P]], channel_multiplier=-1).then_inc(consts_ready, 1)

        @on("dve")
        def _(dve, od):
            dve.wait_ge(edges_loaded, 64)
            dve.wait_ge(consts_ready, 1)
            nc.vector.tensor_copy(src_f[:], src_i[:])
            nc.vector.tensor_copy(typ_f[:], typ_i[:])
            od.link(nc.vector.tensor_copy(dst_f[:], dst_i[:]))
            od.link(nc.vector.scalar_tensor_tensor(out=sel0[:], in0=src_f[:], scalar=float(N), in1=dst_f[:], op0=ALU.mult, op1=ALU.add))
            nc.vector.tensor_copy(sd_i[:, :, 0], src_i[:])
            nc.vector.tensor_copy(sd_i[:, :, 1], dst_i[:])
            nc.vector.tensor_copy(sd_i[:, :, 2], sel0[:]).then_inc(mask_done, 1)

        sel0 = prod0[:, 0:ET]

        @on("sp")
        def _(sp, o):
            Ww = A["L0_gnn_Ww"].rearrange("(r c p) (q n) -> r q p c n", r=2, p=P, q=2)
            for r in range(2):
                for q in range(2):
                    ring.load(sp, banks, 2 * r + q, [(ring.slot(2 * r + q), Ww[r, q])])
                    ring.last[2 * r + q] = (f"l0uv{r}{q}2",)
            ring.load(sp, banks, 4, [(ring.slot(4), A["L0_gnn_Wv"].rearrange("(c p) n -> p c n", p=P))])
            ring.last[4] = ("l0o2",)

        filled = sem("filled")

        def l0_store_tables(sp):
            sp.wait_ge(masked_ready, 1)
            flat_w = tab_w.rearrange("(p a) h -> p (a h)", p=P)
            for j in range(6):
                    sp.dma_start(flat_w[:, j * 4 * N:(j + 1) * 4 * N], masked).then_inc(filled, 16)
            sp.wait_ge(step_ready, 1)
            sp.dma_start(tiled(tab_u), ust[:]).then_inc(tables_stored, 16)
            sp.dma_start(tiled(tab_v), vst[:]).then_inc(tables_stored, 16)

        def store_maxima(sp, n, table):
            sp.wait_ge(max_ready, n)
            sp.dma_start(tiled(table), seg_node[:]).then_inc(max_stored, 16)

        @on("pe")
        def _(pe, o):
            pe.wait_ge(params, PARAMS)
            pe.wait_ge(xn_ready, NORM["l0"] + 1)
            pe_transpose(pe, "l0x", xn)
            for c in range(KC):
                banks.drained(pe, f"l0x{c}")
            for r in range(2):
                for q in range(2):
                    w = ring.get(pe, 2 * r + q)
                    for t in range(NT):
                        pe_rows(pe, f"l0uv{r}{q}{t}", xT, w, t, r_bw[:, q * 512:q * 512 + 512] if r else None)
            w = ring.get(pe, 4)
            for t in range(NT):
                pe_rows(pe, f"l0o{t}", xT, w, t, r_bv0)
            bk = [banks.open(pe, f"cnt{c}") for c in range(NT)]
            for c in range(NT):
                last = mm(bk[c][:, 0:N], zeros[:, 0:P], zeros[:, 0:N], True, False)
            last.then_inc(hot_used, 2)
            with pe.Fori(0, ET // 2) as i:
                for b in range(2):
                    pe.wait_ge(hot_ready, 2 * i + b + 1)
                    for c in range(NT):
                        last = mm(bk[c][:, 0:N], hotb[:, b, 0, c * P:(c + 1) * P], hotb[:, b, 1, :], False, False)
                    last.then_inc(hot_used, 1)
            for c in range(NT):
                mm(bk[c][:, 0:N], zeros[:, 0:P], zeros[:, 0:N], False, True).then_inc(banks.full_of(f"cnt{c}"), 1)
            for c in range(NT):
                banks.drained(pe, f"cnt{c}")
            for c in range(NT):
                b = banks.open(pe, f"cntT{c}")
                for t in range(NT):
                    last = nc.tensor.transpose(b[:, t * P:(t + 1) * P], cnt_src[:, t, c * P:(c + 1) * P], ident[:])
                last.then_inc(banks.full_of(f"cntT{c}"), 1)
            for h in range(H8 + 1):
                if h < H8:
                    pe.wait_ge(exp_done, h + 1)
                    for c in range(NT):
                        b = banks.open(pe, f"l0p{h}{c}")
                        for t in range(NT):
                            last = nc.tensor.transpose(b[:, t * P:(t + 1) * P], pw[:, h % 2, t, c * P:(c + 1) * P], ident[:])
                        last.then_inc(banks.full_of(f"l0p{h}{c}"), 1)
                if h >= 1:
                    g = h - 1
                    for c in range(NT):
                        banks.drained(pe, f"l0p{g}{c}")
                    b = banks.open(pe, f"l0y{g}")
                    for t in range(NT):
                        for c in range(NT):
                            last = mm(b[:, t * HD:(t + 1) * HD], pwT[g % 2][:, c, t * P:(t + 1) * P],
                                      ost[:, c, g * HD:(g + 1) * HD], c == 0, c == NT - 1)
                    last.then_inc(banks.full_of(f"l0y{g}"), 1)

        @on("act")
        def _(act, o):
            act_norm(act, NORM["l0"])
            act_transposed(act, "l0x", xT)
            for r in range(2):
                for q in range(2):
                    for t in range(NT):
                        act_copy(act, f"l0uv{r}{q}{t}", (vst if r else ust)[:, t, q * 512:q * 512 + 512])
            for t in range(NT):
                act_copy(act, f"l0o{t}", ost[:, t, :])
            with act.Fori(0, ET // UNROLL) as i:
                for b in range(UNROLL):
                    z = b % ZB
                    act.wait_ge(cols_landed[z], 16 * (UNROLL // ZB * i + b // ZB + 1))
                    nc.scalar.activation(zb[:, z, 0:2 * D], zb[:, z, 0:2 * D], ACT.Relu).then_inc(relu_done, 1)
            act.wait_ge(neg_max, 1)
            for h in range(H8 + 1):
                if h < H8:
                    if h >= 2:
                        banks.filled(act, f"l0p{h - 2}{NT - 1}")
                    for t in range(NT):
                        last = nc.scalar.activation(pw[:, h % 2, t, :], wm[:, t, :].rearrange("p (j h) -> p h j", h=H8)[:, h, :],
                                                    ACT.Exp, bias=gate[:, 5, t * H8 + h:t * H8 + h + 1],
                                                    accum_out=gate[:, 9, h * NT + t:h * NT + t + 1])
                    last.then_inc(exp_done, 1)
                if h >= 1:
                    for c in range(NT):
                        act_copy(act, f"l0p{h - 1}{c}", pwT[(h - 1) % 2][:, c, :], N)
            act.wait_ge(elu_in, 1)
            nc.scalar.activation(xn2b[:], xn2b[:], ACT.Exp).then_inc(elu_exp, 1)
            act_norm(act, NORM["l0b"])

        xn2b = view(0, NT, D)

        @on("pool")
        def _(pool, op):
            nc.gpsimd.memset(masked, MASKED).then_inc(masked_ready, 1)
            pool.wait_ge(tables_stored, 32)
            pool.wait_ge(mask_done, 1)

            def first_rows(i, b, first):
                if not first:
                    pool.wait_ge(w_landed[b], 16 * i)
                op.link(nc.gpsimd.tensor_copy(idx[:, b, :], sd_i[:, bass.ds(UNROLL * i + b, 1), :].rearrange("p a k -> p (a k)")))
                pool.nop(nofuse=True)
                pool_gather(zb[:, b % ZB, :], tab_u, idx[:, b, 0:1]).then_inc(rows_landed[b % ZB], 16)

            def second_rows(i, b):
                pool.wait_ge(rows_landed[b % ZB], 16 * (UNROLL // ZB * i + b // ZB + 1))
                pool.nop(nofuse=True)
                pool_gather(zb[:, b % ZB, :], tab_v, idx[:, b, 1:2], compute_op=ALU.add).then_inc(cols_landed[b % ZB], 16)

            def store_scores(i, b, first=False):
                if b >= 1:
                    pool.wait_ge(w_landed[b - 1], 16 * (i + 1))
                elif not first:
                    pool.wait_ge(w_landed[UNROLL - 1], 16 * i)
                pool.wait_ge(w_ready, UNROLL * i + b + 1)
                pool.nop(nofuse=True)
                nc.gpsimd.indirect_dma_start(tab_w, bass.IndirectOffsetOnAxis(ap=idx[:, b, 2:3].bitcast(U32), axis=0),
                                             w_row[:, b, :], None).then_inc(w_landed[b], 16)

            def tiles(i, first):
                for b in range(UNROLL):
                    if b >= ZB:
                        store_scores(i, b - ZB, first)
                    elif not first:
                        store_scores(i - 1, b + UNROLL - ZB)
                    first_rows(i, b, first)
                    if b >= 1:
                        second_rows(i, b - 1)
                second_rows(i, UNROLL - 1)

            pool.wait_ge(filled, 96)
            tiles(0, True)
            with op.loop(ET // UNROLL - 1, UNROLL) as i:
                tiles(i + 1, False)
            for b in range(UNROLL - ZB, UNROLL):
                store_scores(ET // UNROLL - 1, b)

        @on("dve")
        def _(dve, od):
            dve.wait_ge(x_loaded, 16)
            dve_norm(dve, od, NORM["l0"], x, xn)
            dve.wait_ge(params, PARAMS)
            wa_bc = wa.unsqueeze(1).broadcast_to([P, H8, P])
            od.link(nc.vector.tensor_scalar(wa99, wa, 1.0 - 0.01, None, ALU.mult))
            for r, tab in ((0, ust), (1, vst)):
                for t in range(NT):
                    for q in range(2):
                        banks.drained(dve, f"l0uv{r}{q}{t}")
                    od.link(nc.vector.tensor_tensor(prod0.rearrange("p (h d) -> p h d", h=H8),
                                                    tab[:, t, 0:2 * D].rearrange("p (h d) -> p h d", h=H8), wa_bc, ALU.mult))
                    lin = tab[:, t, 2 * D:UW]
                    od.link(nc.vector.tensor_reduce(lin, prod0.rearrange("p (h d) -> p h d", h=H8), AX, ALU.add))
                    od.link(nc.vector.tensor_scalar(lin, lin, 0.01, ba0 if r else 0.0, ALU.mult, ALU.add))
            nc.vector.memset(gate[:, 15, 1:2], 0.0).then_inc(step_ready, 1)
            dve.wait_ge(tables_stored, 32)
            def score_tiles(i, last):
                for b in range(UNROLL):
                    t = UNROLL * i + b
                    dve.wait_ge(hot_used, t + 1)
                    nc.vector.tensor_scalar(hotb[:, b % 2, 0, :], iota[:], src_f[:, bass.ds(t, 1)], None, ALU.is_equal)
                    nc.vector.tensor_scalar(hotb[:, b % 2, 1, :], iota[:], dst_f[:, bass.ds(t, 1)], None,
                                            ALU.is_equal).then_inc(hot_ready, 1)
                    dve.wait_ge(relu_done, t + 1)
                    if last is not None:
                        dve.wait_ge(w_landed[b], 16 * (last + 1))
                    z3 = zb[:, b % ZB, 0:2 * D].rearrange("p (h d) -> p h d", h=H8)
                    od.link(nc.vector.tensor_tensor(z3, z3, wa99.unsqueeze(1).broadcast_to([P, H8, P]), ALU.mult))
                    od.link(nc.vector.tensor_reduce(w_row[:, b, :], z3, AX, ALU.add))
                    nc.vector.tensor_tensor(w_row[:, b, :], w_row[:, b, :], zb[:, b % ZB, 2 * D:UW], ALU.add).then_inc(w_ready, 1)

            score_tiles(0, None)
            with od.loop(ET // UNROLL - 1, 2 * UNROLL) as i:
                score_tiles(i + 1, i)
            for c in range(NT):
                b = banks.filled(dve, f"cnt{c}")
                nc.vector.tensor_copy(cnt_src[:, c, :], b[:, 0:N]).then_inc(banks.free_of(f"cnt{c}"), 1)
            for c in range(NT):
                b = banks.filled(dve, f"cntT{c}")
                nc.vector.tensor_copy(cnt_dst[:, c, :], b[:, 0:N]).then_inc(banks.free_of(f"cntT{c}"), 1)
            dve.wait_ge(w_loaded, 16)
            top, keep = gate[:, 4, 0:NT * H8], gate[:, 6, 0:NT * H8]
            for t in range(NT):
                last = nc.vector.tensor_reduce(top[:, t * H8:(t + 1) * H8], wm[:, t, :].rearrange("p (j h) -> p h j", h=H8), AX, ALU.max)
            od.link(last)
            nc.vector.tensor_scalar(keep, top, 0.5 * MASKED, None, ALU.is_gt)
            nc.vector.tensor_scalar(gate[:, 5, 0:NT * H8], top, -1.0, None, ALU.mult).then_inc(neg_max, 1)
            for h in range(H8):
                dve.wait_ge(exp_done, h + 1)
                s3 = gate[:, 9, h * NT:(h + 1) * NT]
                od.link(nc.vector.reciprocal(s3, s3))
                od.link(nc.vector.tensor_tensor(s3, s3, keep.rearrange("p (t h) -> p h t", h=H8)[:, h, :], ALU.mult))
                b = banks.filled(dve, f"l0y{h}")
                nc.vector.tensor_tensor(xn2[:, :, h * HD:(h + 1) * HD], b[:, 0:NT * HD].rearrange("p (t d) -> p t d", t=NT),
                                        s3.unsqueeze(2).broadcast_to([P, NT, HD]), ALU.mult).then_inc(banks.free_of(f"l0y{h}"), 1)
            for h in range(H8):
                banks.drained(dve, f"l0y{h}")
            nc.vector.tensor_scalar(xn2b[:], xn2[:], 0.0, None, ALU.min).then_inc(elu_in, 1)
            dve.wait_ge(elu_exp, 1)
            od.link(nc.vector.scalar_tensor_tensor(out=flat(xn2), in0=flat(xn2), scalar=0.0, in1=flat(xn2b), op0=ALU.max,
                                                   op1=ALU.add))
            od.link(nc.vector.scalar_tensor_tensor(out=flat(xn2), in0=flat(xn2), scalar=-1.0, in1=flat(xn), op0=ALU.add,
                                                   op1=ALU.add))
            dve_norm(dve, od, NORM["l0b"], xn2, xn2, BC["L0_gnn_gamma"], BC["L0_gnn_beta"])
            dve.wait_ge(xn_ready, NORM["l0b"] + 1)
            od.link(nc.vector.tensor_tensor(x[:], x[:], xn2[:], ALU.add))

        def flat(a):
            return a[:].rearrange("p t n -> p (t n)")

        @on("sp")
        def _(sp, o):
            l0_store_tables(sp)

        E0, E1 = A["L0_ffn_w1"].shape[0], A["L1_ffn_w1"].shape[0]
        HE = A["L0_ffn_w1"].shape[2]
        FC = HE // P
        CAP1 = max(min(N, int(N * 2 * 2.0 / E1)), 4)
        hid = view(0, 2 * FC, N).rearrange("p (b f) n -> p b f n", b=2)
        acc = view(4 * N, NT, D)

        def w1_of(s):
            return ring.slot(s).rearrange("p c n -> p (c n)").rearrange("p (e c h) -> p e c h", e=2, c=KC)

        def w2_of(s):
            return ring.slot(s).rearrange("p (e f) n -> p e f n", e=2)

        def load_pair(sp, w1, w2, e, s1, s2):
            ring.load(sp, banks, s1, [(w1_of(s1), w1[e:e + 2].rearrange("e (c p) h -> p e c h", p=P))])
            ring.load(sp, banks, s2, [(w2_of(s2), w2[e:e + 2].rearrange("e (f p) n -> p e f n", p=P))])

        def pe_expert_up(pe, tag, e, aT, s1, i=None):
            if e % 2 == 0:
                ring.get(pe, s1, i)
            for f in range(FC):
                b = banks.open(pe, f"{tag}h{e}{f}", i)
                for c in range(KC):
                    last = mm(b[:, 0:N], w1_of(s1)[:, e % 2, c, f * P:(f + 1) * P], aT[:, c, :], c == 0, c == KC - 1)
                last.then_inc(banks.full_of(f"{tag}h{e}{f}"), 1)

        def pe_expert_down(pe, tag, e, s2, i=None):
            if e % 2 == 0:
                ring.get(pe, s2, i)
            for f in range(FC):
                banks.drained(pe, f"{tag}h{e}{f}", i)
            for t in range(NT):
                b = banks.open(pe, f"{tag}e{e}{t}", i)
                for f in range(FC):
                    last = mm(b, hid[:, e % 2, f, t * P:(t + 1) * P], w2_of(s2)[:, e % 2, f, :], f == 0, f == FC - 1)
                last.then_inc(banks.full_of(f"{tag}e{e}{t}"), 1)

        def act_expert(act, tag, e, func, i=None):
            for f in range(FC):
                name = f"{tag}h{e}{f}"
                b = banks.filled(act, name, i)
                nc.scalar.activation(hid[:, e % 2, f, :], b[:, 0:N], func).then_inc(banks.free_of(name), 1)

        def dve_expert(dve, tag, e, weight, i=None):
            for t in range(NT):
                name = f"{tag}e{e}{t}"
                if e > 0:
                    banks.drained(dve, f"{tag}e{e - 1}{t}", i)
                b = banks.filled(dve, name, i)
                nc.vector.scalar_tensor_tensor(out=acc[:, t, :], in0=b, scalar=weight(t), in1=acc[:, t, :], op0=ALU.mult,
                                               op1=ALU.add).then_inc(banks.free_of(name), 1)

        F0_SLOTS = [(5, 6), (7, 0), (1, 2)]

        @on("sp")
        def _(sp, o):
            for j, (s1, s2) in enumerate(F0_SLOTS):
                load_pair(sp, A["L0_ffn_w1"], A["L0_ffn_w2"], 2 * j, s1, s2)
                ring.last[s1] = (f"f0h{2 * j + 1}{FC - 1}",)
                ring.last[s2] = (f"f0e{2 * j + 1}{NT - 1}",)
            for b in range(UNROLL):
                sp.wait_ge(w_landed[b], 16 * (ET // UNROLL))
            sp.wait_ge(hot_used, ET + 2)
            sp.dma_start(wm[:], tab_w.rearrange("(t p j) h -> p t (j h)", t=NT, p=P)).then_inc(w_loaded, 16)

        @on("pe")
        def _(pe, o):
            pe.wait_ge(xn_ready, NORM["f0"] + 1)
            pe_transpose(pe, "f0x", xn)
            for c in range(KC):
                banks.drained(pe, f"f0x{c}")
            pe_logits(pe, "f0g", xT, wg0, E0)
            pe.wait_ge(xn_ready, NORM["f0b"] + 1)
            pe_transpose(pe, "f0y", xn2)
            for c in range(KC):
                banks.drained(pe, f"f0y{c}")
            for e in range(E0 + 1):
                if e < E0:
                    pe_expert_up(pe, "f0", e, xT2, F0_SLOTS[e // 2][0])
                if e >= 1:
                    pe_expert_down(pe, "f0", e - 1, F0_SLOTS[(e - 1) // 2][1])

        @on("act")
        def _(act, o):
            act_norm(act, NORM["f0"])
            act_transposed(act, "f0x", xT)
            act_norm(act, NORM["f0b"])
            for c in range(KC):
                b = banks.filled(act, f"f0y{c}")
                nc.scalar.activation(xT2[:, c, :], b[:, 0:N], ACT.Copy, scale=c_g0[:, c:c + 1]).then_inc(
                    banks.free_of(f"f0y{c}"), 1)
            act_softmax_logits(act, "f0g", E0)
            for e in range(E0):
                act_expert(act, "f0", e, ACT.Gelu)

        @on("dve")
        def _(dve, od):
            dve_norm(dve, od, NORM["f0"], x, xn)
            dve.wait_ge(xn_ready, NORM["f0"] + 1)
            dve_norm(dve, od, NORM["f0b"], xn, xn2)
            dve_softmax_logits(dve, od, "f0g", E0, 0)
            pr, one, wo1, comb = g3(0, E0), g3(4, E0), g3(5, E0), g3(6, E0)
            g1, g2 = gate[:, 1, 24:24 + NT], gate[:, 1, 32:32 + NT]
            dve_top1(od, pr, E0, g1, one, g3(2, E0))
            od.link(nc.vector.tensor_scalar(wo1, one, -1.0, 1.0, ALU.mult, ALU.add))
            od.link(nc.vector.tensor_tensor(wo1, wo1, pr, ALU.mult))
            od.link(nc.vector.tensor_reduce(g2, wo1, AX, ALU.max))
            od.link(nc.vector.scalar_tensor_tensor(out=g2, in0=g2, scalar=1e-9, in1=g1, op0=ALU.add, op1=ALU.add))
            od.link(nc.vector.reciprocal(g2, g2))
            od.link(nc.vector.tensor_tensor(g1, g1, g2, ALU.mult))
            od.link(nc.vector.tensor_tensor(comb, one, g1.unsqueeze(2).broadcast_to([P, NT, E0]), ALU.mult))
            od.link(nc.vector.memset(acc[:], 0.0))
            for e in range(E0):
                dve_expert(dve, "f0", e, lambda t: comb[:, t, e:e + 1])
            for t in range(NT):
                banks.drained(dve, f"f0e{E0 - 1}{t}")
            od.link(nc.vector.tensor_tensor(x[:], x[:], acc[:], ALU.add))

        BLK, CDIM = A["L1_gnn_s1_w"].shape[0], A["L1_gnn_s1_w"].shape[1]
        NF = A["L1_gnn_f_w1"].shape[0] // 2
        HA = D // P
        TWO_PI_HI, TWO_PI_MID = 6.28125, 0.0019353071795864769
        ROUND = 12582912.0
        noise = view(11400, N)
        ph = view(11800, N)
        turns = view(12200, N)
        condT = view(0, N)
        mod = view(N, 2, N)
        qT = view(3 * N, HA, N)
        kT = view(3 * N + 1536, HA, N)
        vrow = view(3 * N + 3072, NT, D)
        modw = view(3 * N + 4608, 4, D)
        oT = qT
        blk_in = sem("blk_in")
        noise_in = sem("noise_in")
        L1W = ("wq", "wk", "wv", "wo", "m_w1", "m_w2")

        def block_of(name, i):
            a = A["L1_gnn_" + name]
            return a[i] if isinstance(i, int) else a[bass.ds(i, 1)].rearrange("a k n -> (a k) n")

        def load_block_rows(sp, i):
            for j, nm in enumerate(("s1_w", "b1_w", "s2_w", "b2_w")):
                sp.dma_start(modw[0:CDIM, j, :], block_of(nm, i)).then_inc(blk_in, 16)
            for j, nm in enumerate(("bv", "bo", "m_b2")):
                a = A["L1_gnn_" + nm]
                sp.dma_start(blk_rows[0:1, j, :], a[bass.ds(i, 1), :]).then_inc(blk_in, 16)

        L1_LAST = ("l1q3", "l1k3", "l1v2", "l1w2", "l1u3", "l1d2")

        @on("sp")
        def _(sp, o):
            sp.wait_ge(xn_ready, NORM["f0"] + 1)
            sp.dma_start(noise[0:2 * NF, :], A["node_vec1"].rearrange("n a -> (a n)").partition_broadcast(2 * NF)).then_inc(noise_in, 16)
            for s, nm in enumerate(L1W):
                ring.load(sp, banks, s, [(ring.slot(s), block_of(nm, 0).rearrange("(c p) n -> p c n", p=P))])
            sp.wait_ge(xn_ready, NORM["l1"] + 1)
            load_block_rows(sp, 0)
            with sp.Fori(0, BLK - 1) as i:
                for s, nm in enumerate(L1W):
                    ring.load(sp, banks, s, [(ring.slot(s), block_of(nm, i + 1).rearrange("(c p) n -> p c n", p=P))],
                              used=(L1_LAST[s], i))
                banks.filled(sp, "l1d2", i)
                load_block_rows(sp, i + 1)
            for s in range(6):
                ring.last[s] = (L1_LAST[s], BLK - 1)

        @on("pe")
        def _(pe, o):
            pe.wait_ge(pe_col, 1)
            b = banks.open(pe, "cond1")
            mm(b[0:CDIM, 0:N], fw1, ph[0:2 * NF, :], True, True).then_inc(banks.full_of("cond1"), 1)
            banks.drained(pe, "cond1")
            b = banks.open(pe, "cond2")
            mm(b[0:CDIM, 0:N], fw2, turns[0:CDIM, :], True, True).then_inc(banks.full_of("cond2"), 1)
            banks.drained(pe, "cond2")

            def modulated(k, i):
                for c in range(KC):
                    for j, nm in ((2 * k, f"l1s{k}{c}"), (2 * k + 1, f"l1b{k}{c}")):
                        b = banks.open(pe, nm, i)
                        mm(b[:, 0:N], modw[0:CDIM, j, c * P:(c + 1) * P], condT[0:CDIM, :], True, True).then_inc(
                            banks.full_of(nm), 1)
                    if c == 0:
                        pe.wait_ge(xn_ready, NORM["blk"] + 2 * i + k + 1)
                    b = banks.open(pe, f"l1x{k}{c}", i)
                    for t in range(NT):
                        last = nc.tensor.transpose(b[:, t * P:(t + 1) * P], xn[:, t, c * P:(c + 1) * P], ident[:])
                    last.then_inc(banks.full_of(f"l1x{k}{c}"), 1)
                for c in range(KC):
                    banks.drained(pe, f"l1b{k}{c}", i)

            def head_scores(h, i):
                for t in range(NT):
                    b = banks.open(pe, f"l1h{h}s{t}", i)
                    mm(b[:, 0:N], qT[:, h, t * P:(t + 1) * P], kT[:, h, :], True, True).then_inc(
                        banks.full_of(f"l1h{h}s{t}"), 1)

            def head_values(h, i):
                pe_att_transpose(pe, f"l1h{h}", HA * i + h, h % 2, i)
                for c in range(NT):
                    banks.drained(pe, f"l1h{h}p{c}", i)
                b = banks.open(pe, f"l1o{h}", i)
                for c in range(NT):
                    last = mm(b[:, 0:N], vrow[:, c, h * P:(h + 1) * P], probsT[:, h % 2, c, :], c == 0, c == NT - 1)
                last.then_inc(banks.full_of(f"l1o{h}"), 1)

            with banks.loop(BLK, 73), pe.Fori(0, BLK) as i:
                pe.wait_ge(blk_in, 16 * 7 * (i + 1))
                modulated(0, i)
                for s, nm in ((0, "q"), (1, "k")):
                    w = ring.get(pe, s, i)
                    for h in range(HA):
                        pe_cols(pe, f"l1{nm}{h}", xT, w, h * P, i)
                w = ring.get(pe, 2, i)
                for t in range(NT):
                    pe_rows(pe, f"l1v{t}", xT, w, t, blk_rows[0:1, 0, :], i)
                for h in range(HA):
                    banks.drained(pe, f"l1q{h}", i)
                    banks.drained(pe, f"l1k{h}", i)
                for t in range(NT):
                    banks.drained(pe, f"l1v{t}", i)
                for h in range(HA + 1):
                    if h < HA:
                        head_scores(h, i)
                    if h >= 1:
                        head_values(h - 1, i)
                for h in range(HA):
                    banks.drained(pe, f"l1o{h}", i)
                w = ring.get(pe, 3, i)
                for t in range(NT):
                    pe_rows(pe, f"l1w{t}", oT, w, t, blk_rows[0:1, 1, :], i)
                modulated(1, i)
                w = ring.get(pe, 4, i)
                for c in range(KC):
                    pe_cols(pe, f"l1u{c}", xT, w, c * P, i)
                for c in range(KC):
                    banks.drained(pe, f"l1u{c}", i)
                w = ring.get(pe, 5, i)
                for t in range(NT):
                    pe_rows(pe, f"l1d{t}", kT, w, t, blk_rows[0:1, 2, :], i)
            ring.after_loop(range(6), BLK)

        @on("act")
        def _(act, o):
            act.wait_ge(step_ready, 2)
            nc.scalar.activation(ph[0:2 * NF, :], ph[0:2 * NF, :], ACT.Sin).then_inc(pe_col, 1)
            b = banks.filled(act, "cond1")
            nc.scalar.activation(turns[0:CDIM, :], b[0:CDIM, 0:N], ACT.Silu, bias=c_fb1).then_inc(banks.free_of("cond1"), 1)
            b = banks.filled(act, "cond2")
            nc.scalar.activation(condT[0:CDIM, :], b[0:CDIM, 0:N], ACT.Identity, bias=c_fb2).then_inc(banks.free_of("cond2"), 1)
            act_norm(act, NORM["l1"])

            def biased(name, dst, table, c, i, func=ACT.Identity):
                b = banks.filled(act, name, i)
                nc.scalar.activation(dst, b[:, 0:N], func, bias=table[:, bass.ds(KC * i + c, 1)]).then_inc(
                    banks.free_of(name), 1)

            with act.Fori(0, BLK) as i:
                for k, table in ((0, c_s1b), (1, c_s2b)):
                    if k == 0:
                        act_norm(act, NORM["blk"] + 2 * i)
                    for c in range(KC):
                        if c >= 2:
                            banks.drained(act, f"l1x{k}{c - 2}", i)
                        biased(f"l1s{k}{c}", mod[:, c % 2, :], table, c, i)
                    if k == 0:
                        for nm, dst, tb in (("q", qT, c_bq), ("k", kT, c_bk)):
                            for h in range(HA):
                                biased(f"l1{nm}{h}", dst[:, h, :], tb, h, i)
                        for t in range(NT):
                            act_copy(act, f"l1v{t}", vrow[:, t, :], D, i)
                        for h in range(HA + 1):
                            if h < HA:
                                act_att_exp(act, HA * i + h, h % 2)
                            if h >= 1:
                                act_att_transposed(act, f"l1h{h - 1}", (h - 1) % 2, i)
                                act_copy(act, f"l1o{h - 1}", oT[:, h - 1, :], N, i)
                        act_norm(act, NORM["blk"] + 2 * i + 1)
                    else:
                        for c in range(KC):
                            biased(f"l1u{c}", kT[:, c, :], c_mb1, c, i, ACT.Relu)

        @on("dve")
        def _(dve, od):
            nc.vector.tensor_scalar(mask_src[:], cnt_src[:], 0.5, MASKED, ALU.is_lt, ALU.mult)
            nc.vector.tensor_scalar(mask_dst[:], cnt_dst[:], 0.5, MASKED, ALU.is_lt, ALU.mult)
            dve.wait_ge(noise_in, 16)
            dve.wait_ge(consts_ready, 2)
            fr = gate[0:2 * NF, 7, 0:1]
            od.link(nc.vector.tensor_scalar(fr, fr, float(2.0 * 3.141592653589793 / 16), None, ALU.mult))
            z, tn = ph[0:2 * NF, :], turns[0:2 * NF, :]
            od.link(nc.vector.tensor_scalar(z, noise[0:2 * NF, :], fr, None, ALU.mult))
            od.link(nc.vector.tensor_scalar(tn, z, 0.15915494309189535, ROUND, ALU.mult, ALU.add))
            od.link(nc.vector.tensor_scalar(tn, tn, -ROUND, None, ALU.add))
            od.link(nc.vector.scalar_tensor_tensor(out=z, in0=tn, scalar=-TWO_PI_HI, in1=z, op0=ALU.mult, op1=ALU.add))
            od.link(nc.vector.scalar_tensor_tensor(out=z, in0=tn, scalar=-TWO_PI_MID, in1=z, op0=ALU.mult, op1=ALU.add))
            od.link(nc.vector.tensor_scalar(z, z, 3.1415925, -3.1415925, ALU.min, ALU.max))
            zc = ph[NF:2 * NF, :]
            od.link(nc.vector.scalar_tensor_tensor(out=zc, in0=zc, scalar=-1.0, in1=zc, op0=ALU.mult, op1=ALU.max))
            nc.vector.tensor_scalar(zc, zc, -1.0, 1.5707963267948966, ALU.mult, ALU.add).then_inc(step_ready, 1)
            for tb in (c_s1b, c_s2b):
                od.link(nc.vector.tensor_scalar(tb, tb, 1.0, None, ALU.add))
            dve_norm(dve, od, NORM["l1"], x, xn2)
            dve.wait_ge(xn_ready, NORM["l1"] + 1)

            def modulated(k, table, i):
                for c in range(KC):
                    banks.drained(dve, f"l1s{k}{c}", i)
                    b = banks.filled(dve, f"l1x{k}{c}", i)
                    nc.vector.tensor_tensor(xT[:, c, :], b[:, 0:N], mod[:, c % 2, :], ALU.mult).then_inc(
                        banks.free_of(f"l1x{k}{c}"), 1)
                    banks.drained(dve, f"l1x{k}{c}", i)
                    b = banks.filled(dve, f"l1b{k}{c}", i)
                    nc.vector.scalar_tensor_tensor(out=xT[:, c, :], in0=b[:, 0:N], scalar=table[:, bass.ds(KC * i + c, 1)],
                                                   in1=xT[:, c, :], op0=ALU.add, op1=ALU.add).then_inc(
                        banks.free_of(f"l1b{k}{c}"), 1)

            def add_rows(tag, i):
                for t in range(NT):
                    b = banks.filled(dve, f"{tag}{t}", i)
                    nc.vector.tensor_tensor(xn2[:, t, :], xn2[:, t, :], b, ALU.add).then_inc(banks.free_of(f"{tag}{t}"), 1)
                for t in range(NT):
                    banks.drained(dve, f"{tag}{t}", i)

            with od.loop(BLK, 26) as i:
                dve_norm(dve, od, NORM["blk"] + 2 * i, xn2, xn)
                modulated(0, c_b1b, i)
                for h in range(HA + 1):
                    if h < HA:
                        dve_att_scores(dve, od, f"l1h{h}", HA * i + h, h, h % 2, float(P) ** -0.5, mask_src, i)
                    if h >= 1:
                        dve_att_probs(dve, od, HA * i + h - 1, (h - 1) % 2, cnt_src)
                add_rows("l1w", i)
                dve_norm(dve, od, NORM["blk"] + 2 * i + 1, xn2, xn)
                modulated(1, c_b2b, i)
                add_rows("l1d", i)
            od.link(nc.vector.tensor_tensor(x[:], x[:], xn2[:], ALU.add))

        @on("pool")
        def _(pool, op):
            fr = gate[0:2 * NF, 7, 0:1]
            nc.gpsimd.iota(fr[0:NF, :], pattern=[[0, 1]], base=1, channel_multiplier=1, allow_small_or_imprecise_dtypes=True)
            nc.gpsimd.iota(gate[NF:2 * NF, 7, 0:1], pattern=[[0, 1]], base=1, channel_multiplier=1,
                           allow_small_or_imprecise_dtypes=True).then_inc(consts_ready, 1)

        HALF = E1 // 2

        @on("sp")
        def _(sp, o):
            for i in range(2):
                for j in range(HALF // 2):
                    load_pair(sp, A["L1_ffn_w1"], A["L1_ffn_w2"], HALF * i + 2 * j, 2 * j, 2 * j + 1)
                    ring.last[2 * j] = (f"f1h{2 * j + 1}{FC - 1}", i)
                    ring.last[2 * j + 1] = (f"f1e{2 * j + 1}{NT - 1}", i)

        @on("pe")
        def _(pe, o):
            pe.wait_ge(xn_ready, NORM["f1"] + 1)
            pe_transpose(pe, "f1x", xn)
            for c in range(KC):
                banks.drained(pe, f"f1x{c}")
            pe_logits(pe, "f1g", xT, wg1, E1)

            def before(name, mask, total):
                b = banks.open(pe, name)
                for t in range(NT):
                    ks = range(NT) if total else range(t + 1)
                    for k in ks:
                        last = mm(b[:, t * E1:(t + 1) * E1], tri[:] if k == t and not total else ones[:], mask[:, k, :],
                                  k == 0, k == ks[-1])
                last.then_inc(banks.full_of(name), 1)

            pe.wait_ge(step_ready, 3)
            before("f1p1", g3(4, E1), False)
            before("f1p2", g3(5, E1), False)
            pe.wait_ge(step_ready, 4)
            before("f1n1", g3(4, E1), True)
            with banks.loop(2, HALF * (FC + NT)), pe.Fori(0, 2) as i:
                for e in range(HALF + 1):
                    if e < HALF:
                        pe_expert_up(pe, "f1", e, xT, e // 2 * 2, i)
                    if e >= 1:
                        pe_expert_down(pe, "f1", e - 1, (e - 1) // 2 * 2 + 1, i)
            ring.after_loop(range(8), 2)

        @on("act")
        def _(act, o):
            act_norm(act, NORM["f1"])
            act_transposed(act, "f1x", xT)
            act_softmax_logits(act, "f1g", E1)
            with act.Fori(0, 2) as i:
                for e in range(HALF):
                    act_expert(act, "f1", e, ACT.Relu, i)

        @on("dve")
        def _(dve, od):
            dve_norm(dve, od, NORM["f1"], x, xn)
            dve_softmax_logits(dve, od, "f1g", E1, 1)
            pr, m1, m2, rest, tmp = g3(0, E1), g3(4, E1), g3(5, E1), g3(6, E1), g3(2, E1)
            g1, g2, dn = gate[:, 1, 24:24 + NT], gate[:, 1, 32:32 + NT], gate[:, 1, 40:40 + NT]
            dve_top1(od, pr, E1, g1, m1, tmp)
            od.link(nc.vector.tensor_scalar(rest, m1, -1.0, 1.0, ALU.mult, ALU.add))
            od.link(nc.vector.tensor_tensor(rest, rest, pr, ALU.mult))
            dve_top1(od, rest, E1, g2, m2, tmp)
            nc.vector.memset(gate[:, 15, 4:5], 0.0).then_inc(step_ready, 1)
            od.link(nc.vector.scalar_tensor_tensor(out=dn, in0=g1, scalar=1e-9, in1=g2, op0=ALU.add, op1=ALU.add))
            od.link(nc.vector.reciprocal(dn, dn))
            nc.vector.tensor_tensor(g1, g1, dn, ALU.mult)
            od.link(nc.vector.tensor_tensor(g2, g2, dn, ALU.mult))

            def bank3(name):
                return banks.filled(dve, name)[:, 0:NT * E1].rearrange("p (t e) -> p t e", t=NT)

            p1, p2 = g3(8, E1), g3(9, E1)
            nc.vector.tensor_scalar(p1, bank3("f1p1"), float(CAP1), None, ALU.is_lt).then_inc(banks.free_of("f1p1"), 1)
            nc.vector.tensor_copy(p2, bank3("f1p2")).then_inc(banks.free_of("f1p2"), 1)
            banks.drained(dve, "f1p2")
            od.link(nc.vector.tensor_tensor(m1, m1, p1, ALU.mult))
            nc.vector.memset(gate[:, 15, 4:5], 0.0).then_inc(step_ready, 1)
            nc.vector.tensor_tensor(p2, p2, bank3("f1n1"), ALU.add).then_inc(banks.free_of("f1n1"), 1)
            banks.drained(dve, "f1n1")
            od.link(nc.vector.tensor_scalar(p2, p2, float(CAP1), None, ALU.is_lt))
            od.link(nc.vector.tensor_tensor(m2, m2, p2, ALU.mult))
            nc.vector.tensor_tensor(m1, m1, g1.unsqueeze(2).broadcast_to([P, NT, E1]), ALU.mult)
            od.link(nc.vector.tensor_tensor(m2, m2, g2.unsqueeze(2).broadcast_to([P, NT, E1]), ALU.mult))
            od.link(nc.vector.tensor_tensor(m1, m1, m2, ALU.add))
            od.link(nc.vector.memset(acc[:], 0.0))
            with dve.Fori(0, 2) as i:
                for e in range(HALF):
                    dve_expert(dve, "f1", e, lambda t: m1[:, t, bass.ds(HALF * i + e, 1)], i)
                for t in range(NT):
                    banks.drained(dve, f"f1e{HALF - 1}{t}", i)
            for t in range(NT):
                banks.drained(dve, f"f1e{HALF - 1}{t}", 1)
            od.link(nc.vector.tensor_tensor(x[:], x[:], acc[:], ALU.add))

        hrows = view(0, NT, D)
        prod = view(NT * D, NT, D)
        wT = view(2 * NT * D, KC, D)
        es_n, ed_n = view(11400, NT, H8), view(11430, NT, H8)
        es_b, ed_b = view(11500, RB, H8), view(11540, RB, H8)
        fac = view(10336, ET, H8)
        sel8 = view(11600, ET, H8)
        BEFORE = 16 * (ET // ZB)
        TYPES = A["L2_gnn_et_emb"].shape[0]

        @on("sp")
        def _(sp, o):
            ring.load(sp, banks, 0, [(ring.slot(0), A["L2_gnn_W"].rearrange("(c p) n -> p c n", p=P))])
            ring.last[0] = ("l2t3",)
            sp.wait_ge(step_ready, 5)
            sp.dma_start(tiled(tab_h), hrows[:]).then_inc(tables_stored, 16)
            sp.dma_start(tiled(tab_es), es_n[:]).then_inc(tables_stored, 16)
            sp.dma_start(tiled(tab_ed), ed_n[:]).then_inc(tables_stored, 16)

        def pe_weight_transpose(pe, tag, w, i=None):
            for c in range(KC):
                b = banks.open(pe, f"{tag}{c}", i)
                for q in range(KC):
                    last = nc.tensor.transpose(b[:, q * P:(q + 1) * P], w[:, q, c * P:(c + 1) * P], ident[:])
                last.then_inc(banks.full_of(f"{tag}{c}"), 1)

        @on("pe")
        def _(pe, o):
            pe_weight_transpose(pe, "l2t", ring.get(pe, 0))
            pe.wait_ge(xn_ready, NORM["l2"] + 1)
            pe_transpose(pe, "l2x", xn)
            for c in range(KC):
                banks.drained(pe, f"l2t{c}")
                banks.drained(pe, f"l2x{c}")
            for t in range(NT):
                pe_rows(pe, f"l2r{t}", xT, wT, t)
            pe.wait_ge(scores_max, 1)
            pe_segment_max(pe, "l2")
            pe_scatter_rows(pe, "l2")

        @on("act")
        def _(act, o):
            act.wait_ge(var_ready, NORM["l2"] + 1)
            for c in range(KC):
                act_copy(act, f"l2t{c}", wT[:, c, :])
            act_norm(act, NORM["l2"])
            act_transposed(act, "l2x", xT)
            for t in range(NT):
                act_copy(act, f"l2r{t}", hrows[:, t, :])
            act_scatter_rows(act)
            act_norm(act, NORM["l2b"])

        @on("pool")
        def _(pool, op):
            pool.wait_ge(tables_stored, 80)
            with op.loop(ET // RB, RB) as i:
                for b in range(RB):
                    t = RB * i + b
                    pool.wait_ge(edge_free, t + 1)
                    op.link(nc.gpsimd.tensor_copy(idx[:, b, :], sd_i[:, bass.ds(t, 1), :].rearrange("p a k -> p (a k)")))
                    pool.nop(nofuse=True)
                    pool_gather(es_b[:, b, :], tab_es, idx[:, b, 0:1]).then_inc(rows_landed[b], 16)
                    pool_gather(ed_b[:, b, :], tab_ed, idx[:, b, 1:2]).then_inc(cols_landed[b], 16)
            pool.wait_ge(max_stored, 16)
            pool_scatter_rows(pool, op, tab_h, tab_m2)

        @on("dve")
        def _(dve, od):
            dve_norm(dve, od, NORM["l2"], x, xn)
            for t in range(NT):
                banks.drained(dve, f"l2r{t}")
            for vec, dst in ((BC["L2_gnn_a_src"], es_n), (BC["L2_gnn_a_dst"], ed_n)):
                for t in range(NT):
                    last = nc.vector.tensor_tensor(prod[:, t, :], hrows[:, t, :], vec, ALU.mult)
                od.link(last)
                od.link(nc.vector.tensor_reduce(dst[:].rearrange("p c h -> p (c h)"),
                                                prod[:].rearrange("p c (h d) -> p (c h) d", d=HD), AX, ALU.add))
            nc.vector.memset(gate[:, 15, 5:6], 0.0).then_inc(step_ready, 1)
            nc.vector.memset(gate[:, 15, 2:3], 0.0).then_inc(edge_free, RB)
            et3 = et_bc.rearrange("p (y h) -> p y h", h=H8)
            od.link(nc.vector.memset(fac[:], 1.0))
            for y in range(TYPES):
                od.link(nc.vector.scalar_tensor_tensor(
                    out=sel8[:], in0=typ_f[:].unsqueeze(2).broadcast_to([P, ET, H8]), scalar=float(y),
                    in1=et3[:, y:y + 1, :].broadcast_to([P, ET, H8]), op0=ALU.is_equal, op1=ALU.mult))
                od.link(nc.vector.tensor_tensor(fac[:], fac[:], sel8[:], ALU.add))
            od.link(nc.vector.tensor_tensor(fac[:], fac[:], ew[:].unsqueeze(2).broadcast_to([P, ET, H8]), ALU.mult))
            od.link(nc.vector.memset(seg_max[:], 0.0))
            with od.loop(ET // RB, 4 * RB) as i:
                for b in range(RB):
                    t = RB * i + b
                    dve.wait_ge(rows_landed[b], 16 * (i + 1) + BEFORE)
                    dve.wait_ge(cols_landed[b], 16 * (i + 1) + BEFORE)
                    nc.vector.tensor_scalar(neg[:, b % 2, :], iota[:], dst_f[:, bass.ds(t, 1)], MASKED, ALU.not_equal, ALU.mult)
                    we = w_edge[:, bass.ds(t, 1), :].rearrange("p a h -> p (a h)")
                    od.link(nc.vector.tensor_tensor(es_b[:, b, :], es_b[:, b, :], ed_b[:, b, :], ALU.add))
                    od.link(nc.vector.scalar_tensor_tensor(out=es_b[:, b, :], in0=es_b[:, b, :], scalar=0.2, in1=es_b[:, b, :],
                                                           op0=ALU.mult, op1=ALU.max))
                    od.link(nc.vector.tensor_tensor(we, es_b[:, b, :], fac[:, bass.ds(t, 1), :].rearrange("p a h -> p (a h)"),
                                                    ALU.mult))
                    od.link(dve_segment_max(t, b % 2))
                    nc.vector.memset(gate[:, 15, 20:21], 0.0).then_inc(edge_free, 1)
            nc.vector.memset(gate[:, 15, 0:1], 0.0).then_inc(scores_max, 1)
            dve_segment_node(dve, "l2")
            for j in range(6):
                banks.drained(dve, f"l2m{j}")
            nc.vector.memset(gate[:, 15, 1:2], 0.0).then_inc(max_ready, 1)
            nc.vector.memset(gate[:, 15, 2:3], 0.0).then_inc(msg_free, RB)
            dve_scatter_rows(dve, od, dst_f, BEFORE + 16 * (ET // RB))
            dve_scatter_sums(dve, od, "l2", 1.0e-10, True)
            od.link(nc.vector.tensor_tensor(xn2[:], xn2[:], xn[:], ALU.add))
            dve_norm(dve, od, NORM["l2b"], xn2, xn2, BC["L2_gnn_ln_gamma"], BC["L2_gnn_ln_beta"])
            dve.wait_ge(xn_ready, NORM["l2b"] + 1)
            od.link(nc.vector.tensor_tensor(x[:], x[:], xn2[:], ALU.add))

        K2 = A["L2_ffn_expert_weights"].shape[0]
        wTs = [view(0, KC, D), view(KC * D, KC, D)]
        coefT = view(2 * KC * D, N)
        acc2 = view(2 * KC * D + N, NT, D)
        mixw = xT2[0:K2, :, :].rearrange("p c n -> p (c n)")[:, 0:D]
        mixb = xT2[0:K2, :, :].rearrange("p c n -> p (c n)")[:, D:2 * D]
        mix_in = sem("mix_in")
        Q2 = K2 // 2

        @on("sp")
        def _(sp, o):
            sp.dma_start(mixw, A["L2_ffn_mixer_w"]).then_inc(mix_in, 16)
            sp.dma_start(mixb, A["L2_ffn_expert_biases"]).then_inc(mix_in, 16)
            for i in range(2):
                for e in range(Q2):
                    s = e + 1
                    ring.load(sp, banks, s, [(ring.slot(s), A["L2_ffn_expert_weights"][Q2 * i + e].rearrange("(c p) n -> p c n", p=P))])
                    ring.last[s] = (f"f2t{e}{KC - 1}", i)
                if i == 0:
                    store_maxima(sp, 1, tab_m2)

        @on("pe")
        def _(pe, o):
            pe.wait_ge(mix_in, 32)
            b = banks.open(pe, "f2m")
            for c in range(KC):
                last = nc.tensor.transpose(b[:, c * K2:(c + 1) * K2], mixw[:, c * P:(c + 1) * P], ident[0:K2, 0:K2])
            last.then_inc(banks.full_of("f2m"), 1)
            pe.wait_ge(xn_ready, NORM["f2"] + 1)
            pe_transpose(pe, "f2x", xn)
            banks.drained(pe, "f2m")
            for c in range(KC):
                banks.drained(pe, f"f2x{c}")
            pe_logits(pe, "f2g", xT, mixT, K2, r_mixb)
            pe.wait_ge(step_ready, 6)
            b = banks.open(pe, "f2c")
            for t in range(NT):
                last = nc.tensor.transpose(b[0:K2, t * P:(t + 1) * P], g3(0, K2)[:, t, :], ident[:])
            last.then_inc(banks.full_of("f2c"), 1)
            banks.drained(pe, "f2c")
            for t in range(NT):
                b = banks.open(pe, f"f2b{t}")
                mm(b, coefT[0:K2, t * P:(t + 1) * P], mixb, True, True).then_inc(banks.full_of(f"f2b{t}"), 1)
            with banks.loop(2, Q2 * (KC + NT)), pe.Fori(0, 2) as i:
                for e in range(Q2 + 1):
                    if e < Q2:
                        pe_weight_transpose(pe, f"f2t{e}", ring.get(pe, e + 1, i), i)
                    if e >= 1:
                        for c in range(KC):
                            banks.drained(pe, f"f2t{e - 1}{c}", i)
                        for t in range(NT):
                            pe_rows(pe, f"f2y{e - 1}{t}", xT, wTs[(e - 1) % 2], t, None, i)
            ring.after_loop(range(1, Q2 + 1), 2)

        @on("act")
        def _(act, o):
            act_copy(act, "f2m", small[:, 208:240], KC * K2)
            act_norm(act, NORM["f2"])
            act_transposed(act, "f2x", xT)
            act_softmax_logits(act, "f2g", K2)
            b = banks.filled(act, "f2c")
            nc.scalar.activation(coefT[0:K2, :], b[0:K2, 0:N], ACT.Copy).then_inc(banks.free_of("f2c"), 1)
            with act.Fori(0, 2) as i:
                for e in range(Q2):
                    for c in range(KC):
                        act_copy(act, f"f2t{e}{c}", wTs[e % 2][:, c, :], D, i)

        @on("dve")
        def _(dve, od):
            dve_norm(dve, od, NORM["f2"], x, xn)
            dve_softmax_logits(dve, od, "f2g", K2, 2)
            nc.vector.memset(gate[:, 15, 6:7], 0.0).then_inc(step_ready, 1)
            for t in range(NT):
                b = banks.filled(dve, f"f2b{t}")
                nc.vector.tensor_copy(acc2[:, t, :], b).then_inc(banks.free_of(f"f2b{t}"), 1)
            for t in range(NT):
                banks.drained(dve, f"f2b{t}")
            with dve.Fori(0, 2) as i:
                for e in range(Q2):
                    for t in range(NT):
                        name = f"f2y{e}{t}"
                        if e > 0:
                            banks.drained(dve, f"f2y{e - 1}{t}", i)
                        b = banks.filled(dve, name, i)
                        nc.vector.scalar_tensor_tensor(out=acc2[:, t, :], in0=b, scalar=g3(0, K2)[:, t, bass.ds(Q2 * i + e, 1)],
                                                       in1=acc2[:, t, :], op0=ALU.mult, op1=ALU.add).then_inc(
                            banks.free_of(name), 1)
                for t in range(NT):
                    banks.drained(dve, f"f2y{Q2 - 1}{t}", i)
            for t in range(NT):
                banks.drained(dve, f"f2y{Q2 - 1}{t}", 1)
            od.link(nc.vector.tensor_tensor(x[:], x[:], acc2[:], ALU.add))

        H3 = A["L3_gnn_Wq"].shape[1] // D
        U3 = BLK * HA
        q3, k3, v3, xa = view(0, KC, N), view(1536, KC, N), view(3072, NT, D), view(4608, KC, N)
        acc3 = view(6144, NT, D)
        row_in = sem("row_in")

        def head_cols(name, i):
            return A["L3_gnn_" + name][:, bass.ds((H3 - 1 - i) * D, D)].rearrange("(c p) n -> p c n", p=P)

        L3W = (("Wq", 5, "l3q3"), ("Wk", 6, "l3k3"), ("Wv", 7, "l3v2"), ("Wskip", 0, "l3a3"), ("Wlin", 1, "l3l2"))

        def load_head(sp, i, before):
            for nm, s, job in L3W:
                src = (A["L3_gnn_Wlin"][bass.ds((H3 - 1 - i) * D, D), :].rearrange("(c p) n -> p c n", p=P) if nm == "Wlin"
                       else head_cols(nm, i))
                ring.load(sp, banks, s, [(ring.slot(s), src)], used=None if before is None else (job, before))
            if before is not None:
                banks.filled(sp, "l3v2", before)
                sp.nop(nofuse=True)
            sp.dma_start(blk_rows[0:1, 0, :], A["L3_gnn_bv"].unsqueeze(0)[:, bass.ds((H3 - 1 - i) * D, D)]).then_inc(row_in, 16)

        @on("sp")
        def _(sp, o):
            load_head(sp, 0, None)
            with sp.Fori(0, H3 - 1) as i:
                load_head(sp, i + 1, i)
            for nm, s, job in L3W:
                ring.last[s] = (job, H3 - 1)

        @on("pe")
        def _(pe, o):
            pe.wait_ge(xn_ready, NORM["l3"] + 1)
            pe_transpose(pe, "l3x", xn)
            for c in range(KC):
                banks.drained(pe, f"l3x{c}")
            with banks.loop(H3, 24), pe.Fori(0, H3) as i:
                pe.wait_ge(row_in, 16 * (i + 1))
                for nm, s in (("q", 5), ("k", 6)):
                    w = ring.get(pe, s, i)
                    for c in range(KC):
                        pe_cols(pe, f"l3{nm}{c}", xT, w, c * P, i)
                w = ring.get(pe, 7, i)
                for t in range(NT):
                    pe_rows(pe, f"l3v{t}", xT, w, t, blk_rows[0:1, 0, :], i)
                for c in range(KC):
                    banks.drained(pe, f"l3q{c}", i)
                    banks.drained(pe, f"l3k{c}", i)
                for t in range(NT):
                    b = banks.open(pe, f"l3s{t}", i)
                    for c in range(KC):
                        last = mm(b[:, 0:N], q3[:, c, t * P:(t + 1) * P], k3[:, c, :], c == 0, c == KC - 1)
                    last.then_inc(banks.full_of(f"l3s{t}"), 1)
                for t in range(NT):
                    banks.drained(pe, f"l3v{t}", i)
                pe_att_transpose(pe, "l3", U3 + i, 0, i)
                w = ring.get(pe, 0, i)
                for c in range(NT):
                    banks.drained(pe, f"l3p{c}", i)
                for d in range(KC):
                    b = banks.open(pe, f"l3a{d}", i)
                    for c in range(NT):
                        mm(b[:, 0:N], v3[:, c, d * P:(d + 1) * P], probsT[:, 0, c, :], c == 0, False)
                    for c in range(KC):
                        last = mm(b[:, 0:N], w[:, c, d * P:(d + 1) * P], xT[:, c, :], False, c == KC - 1)
                    last.then_inc(banks.full_of(f"l3a{d}"), 1)
                w = ring.get(pe, 1, i)
                for d in range(KC):
                    banks.drained(pe, f"l3a{d}", i)
                for t in range(NT):
                    pe_rows(pe, f"l3l{t}", xa, w, t, None, i)
            ring.after_loop((5, 6, 7, 0, 1), H3)
            for t in range(NT):
                b = banks.open(pe, f"l3f{t}")
                for c in range(KC):
                    last = nc.tensor.transpose(b[:, c * P:(c + 1) * P], xa[:, c, t * P:(t + 1) * P], ident[:])
                last.then_inc(banks.full_of(f"l3f{t}"), 1)

        @on("act")
        def _(act, o):
            act_norm(act, NORM["l3"])
            act_transposed(act, "l3x", xT)

            def biased(name, dst, table, c, i):
                b = banks.filled(act, name, i)
                nc.scalar.activation(dst, b[:, 0:N], ACT.Identity, bias=table[:, bass.ds((H3 - 1 - i) * KC + c, 1)]).then_inc(
                    banks.free_of(name), 1)

            with act.Fori(0, H3) as i:
                for c in range(KC):
                    biased(f"l3q{c}", q3[:, c, :], c_bq3, c, i)
                for c in range(KC):
                    biased(f"l3k{c}", k3[:, c, :], c_bk3, c, i)
                for t in range(NT):
                    act_copy(act, f"l3v{t}", v3[:, t, :], D, i)
                act_att_exp(act, U3 + i, 0)
                act_att_transposed(act, "l3", 0, i)
                for d in range(KC):
                    biased(f"l3a{d}", xa[:, d, :], c_bs3, d, i)
            act_norm(act, NORM["l3b"])

        @on("dve")
        def _(dve, od):
            dve_norm(dve, od, NORM["l3"], x, xn)
            for t in range(NT):
                last = nc.vector.tensor_copy(acc3[:, t, :], BC["L3_gnn_blin"])
            od.link(last)
            with od.loop(H3, 5) as i:
                dve_att_scores(dve, od, "l3", U3 + i, 0, 0, float(D) ** -0.5, mask_dst, i)
                dve_att_probs(dve, od, U3 + i, 0, cnt_dst)
                for t in range(NT):
                    b = banks.filled(dve, f"l3l{t}", i)
                    nc.vector.tensor_tensor(acc3[:, t, :], acc3[:, t, :], b, ALU.add).then_inc(banks.free_of(f"l3l{t}"), 1)
                for t in range(NT):
                    banks.drained(dve, f"l3l{t}", i)
            for t in range(NT):
                banks.drained(dve, f"l3l{t}", H3 - 1)
                b = banks.filled(dve, f"l3f{t}")
                nc.vector.tensor_tensor(acc3[:, t, :], acc3[:, t, :], b, ALU.add).then_inc(banks.free_of(f"l3f{t}"), 1)
            for t in range(NT):
                banks.drained(dve, f"l3f{t}")
            dve_norm(dve, od, NORM["l3b"], acc3, acc3, BC["L3_gnn_gamma"], BC["L3_gnn_beta"])
            dve.wait_ge(xn_ready, NORM["l3b"] + 1)
            od.link(nc.vector.tensor_tensor(x[:], x[:], acc3[:], ALU.add))

        OPTS = 3
        H = 8
        DK = D // H
        U4 = U3 + H3
        q4, k4, v4, o4 = view(0, KC, N), view(1536, KC, N), view(3072, NT, D), view(4608, KC, N)
        route = sb("route", [P, 32])
        kv_in = sems("kv_in", 2)
        q_in, o_in = sem("q_in"), sem("o_in")
        route_i = sb("route_i", [1, 1], I32)
        q_slot, k_slot, v_slot, o_slot, r_slot = 2, 3, 4, 5, 6

        @on("sp")
        def _(sp, o):
            ring.load(sp, banks, r_slot, [(ring.slot(r_slot)[:, :, 0:P], A["L3_ffn_r_w1"].rearrange("(c p) n -> p c n", p=P))])
            sp.wait_ge(step_ready, 8)
            chosen = sp.alloc_register("chosen")
            sp.reg_load(chosen, route_i[0:1, 0:1])
            for s_ in (q_slot, k_slot, v_slot, o_slot):
                if ring.last[s_] is not None:
                    banks.filled(sp, *ring.last[s_])
            for i in range(OPTS):
                with sp.If_eq(chosen, i):
                    sp.dma_start(ring.slot(q_slot), A[f"L3_ffn_wq{i}"].rearrange("(c p) n -> p c n", p=P)).then_inc(q_in, 16)
                    for nm, s_, j in (("wk", k_slot, 0), ("wv", v_slot, 1)):
                        w = A[f"L3_ffn_{nm}{i}"]
                        rep = H // (w.shape[1] // DK)
                        for h in range(H):
                            sp.dma_start(ring.slot(s_)[:, :, h * DK:(h + 1) * DK],
                                         w[:, h // rep * DK:(h // rep + 1) * DK].rearrange("(c p) n -> p c n", p=P)).then_inc(
                                kv_in[j], 16)
                    sp.dma_start(ring.slot(o_slot), A[f"L3_ffn_wo{i}"].rearrange("(c p) n -> p c n", p=P)).then_inc(o_in, 16)

        @on("pe")
        def _(pe, o):
            pe.wait_ge(xn_ready, NORM["f3"] + 1)
            pe_transpose(pe, "f3x", xn)
            rw1 = ring.get(pe, r_slot)
            for c in range(KC):
                banks.drained(pe, f"f3x{c}")
            pe.wait_ge(step_ready, 7)
            b = banks.open(pe, "f3r")
            for c in range(KC):
                last = mm(b[:, 0:1], rw1[:, c, 0:P], route[:, c:c + 1], c == 0, c == KC - 1)
            last.then_inc(banks.full_of("f3r"), 1)
            banks.drained(pe, "f3r")
            b = banks.open(pe, "f3g")
            mm(b[0:1, 0:OPTS], route[:, 4:5], rw2, True, False)
            mm(b[0:1, 0:OPTS], ones[0:1, 0:1], r_rb2, False, True).then_inc(banks.full_of("f3g"), 1)
            def scores(h, i):
                r = slice(DK * (h % 2), DK * (h % 2) + DK)
                for t in range(NT):
                    b = banks.open(pe, f"f3h{h}s{t}", i)
                    mm(b[:, 0:N], q4[r, h // 2, t * P:(t + 1) * P], k4[r, h // 2, :], True, True).then_inc(
                        banks.full_of(f"f3h{h}s{t}"), 1)

            def values(h, i):
                pe_att_transpose(pe, f"f3h{h}", U4 + H * i + h, h % 2, i)
                for c in range(NT):
                    banks.drained(pe, f"f3h{h}p{c}", i)
                b = banks.open(pe, f"f3o{h}", i)
                for c in range(NT):
                    last = mm(b[:, 0:N], v4[:, c, h // 2 * P:(h // 2 + 1) * P], probsT[:, h % 2, c, :], c == 0, c == NT - 1)
                last.then_inc(banks.full_of(f"f3o{h}"), 1)

            i = 0
            w = ring.slot(q_slot)
            pe.wait_ge(q_in, 16)
            for c in range(KC):
                pe_cols(pe, f"f3q{c}", xT, w, c * P, i)
            pe.wait_ge(kv_in[0], 16 * H * (i + 1))
            for c in range(KC):
                pe_cols(pe, f"f3k{c}", xT, ring.slot(k_slot), c * P, i)
            pe.wait_ge(kv_in[1], 16 * H * (i + 1))
            for t in range(NT):
                pe_rows(pe, f"f3v{t}", xT, ring.slot(v_slot), t, None, i)
            for c in range(KC):
                banks.drained(pe, f"f3q{c}", i)
                banks.drained(pe, f"f3k{c}", i)
            for t in range(NT):
                banks.drained(pe, f"f3v{t}", i)
            for h in range(H + 1):
                if h < H:
                    scores(h, i)
                if h >= 1:
                    values(h - 1, i)
            for h in range(H):
                banks.drained(pe, f"f3o{h}", i)
            w = ring.slot(o_slot)
            pe.wait_ge(o_in, 16)
            for t in range(NT):
                pe_rows(pe, f"f3y{t}", o4, w, t, None, i)

        @on("act")
        def _(act, o):
            act_norm(act, NORM["f3"])
            act_transposed(act, "f3x", xT)
            b = banks.filled(act, "f3r")
            nc.scalar.activation(route[:, 4:5], b[:, 0:1], ACT.Relu, bias=c_rb1).then_inc(banks.free_of("f3r"), 1)
            banks.drained(act, "f3g")
            nc.scalar.activation(route[0:1, 12:15], route[0:1, 8:11], ACT.Exp).then_inc(gate_exp, 1)
            i = 0
            for c in range(KC):
                act_copy(act, f"f3q{c}", q4[:, c, :], N, i)
            for c in range(KC):
                act_copy(act, f"f3k{c}", k4[:, c, :], N, i)
            for t in range(NT):
                act_copy(act, f"f3v{t}", v4[:, t, :], D, i)
            for h in range(H + 1):
                if h < H:
                    act_att_exp(act, U4 + H * i + h, h % 2)
                if h >= 1:
                    g = h - 1
                    act_att_transposed(act, f"f3h{g}", g % 2, i)
                    r = slice(DK * (g % 2), DK * (g % 2) + DK)
                    b = banks.filled(act, f"f3o{g}", i)
                    nc.scalar.activation(o4[r, g // 2, :], b[r, 0:N], ACT.Copy).then_inc(banks.free_of(f"f3o{g}"), 1)

        @on("dve")
        def _(dve, od):
            dve_norm(dve, od, NORM["f3"], x, xn)
            for c in range(KC):
                banks.drained(dve, f"f3x{c}")
            od.link(nc.vector.tensor_reduce(route[:, 0:4], xT[:], AX, ALU.add))
            nc.vector.tensor_scalar(route[:, 0:4], route[:, 0:4], 1.0 / N, None, ALU.mult).then_inc(step_ready, 1)
            b = banks.filled(dve, "f3g")[0:1, 0:OPTS]
            od.link(nc.vector.tensor_reduce(route[0:1, 5:6], b, AX, ALU.max))
            nc.vector.tensor_scalar(route[0:1, 8:11], b, route[0:1, 5:6], None, ALU.subtract).then_inc(banks.free_of("f3g"), 1)
            dve.wait_ge(gate_exp, 4)
            od.link(nc.vector.tensor_reduce(route[0:1, 5:6], route[0:1, 12:15], AX, ALU.add))
            od.link(nc.vector.reciprocal(route[0:1, 5:6], route[0:1, 5:6]))
            od.link(nc.vector.tensor_scalar(route[0:1, 12:15], route[0:1, 12:15], route[0:1, 5:6], None, ALU.mult))
            od.link(nc.vector.tensor_reduce(route[0:1, 6:7], route[0:1, 12:15], AX, ALU.max))
            od.link(nc.vector.tensor_scalar(route[0:1, 16:19], route[0:1, 12:15], route[0:1, 6:7], None, ALU.is_equal))
            od.link(nc.vector.tensor_tensor(route[0:1, 16:19], route[0:1, 16:19], iota_back[0:1, 0:OPTS], ALU.mult))
            od.link(nc.vector.tensor_reduce(route[0:1, 6:7], route[0:1, 16:19], AX, ALU.min))
            nc.vector.tensor_scalar(route_i[:], route[0:1, 6:7], 64.0, None, ALU.add).then_inc(step_ready, 1)
            for h in range(H + 1):
                if h < H:
                    dve_att_scores(dve, od, f"f3h{h}", 0, h, h % 2, float(DK) ** -0.5, None, 0)
                if h >= 1:
                    dve_att_probs(dve, od, U4 + h - 1, (h - 1) % 2, None)
            for t in range(NT):
                b = banks.filled(dve, f"f3y{t}")
                nc.vector.tensor_tensor(x[:, t, :], x[:, t, :], b, ALU.add).then_inc(banks.free_of(f"f3y{t}"), 1)
            for t in range(NT):
                banks.drained(dve, f"f3y{t}")

        block = ctx.enter_context(nc.Block())

        @block.tensor
        def _(pe):
            for f in layers["pe"]:
                f(pe, None)

        @block.scalar
        def _(act):
            o = Order(act, act_order)
            for f in layers["act"]:
                f(act, o)

        @block.vector
        def _(dve):
            od = Order(dve, dve_order)
            for f in layers["dve"]:
                f(dve, od)
            nc.vector.memset(gate[:, 15, 0:1], 0.0).then_inc(out_ready, 1)

        @block.gpsimd
        def _(pool):
            op = Order(pool, pool_order)
            for f in layers["pool"]:
                f(pool, op)

        @block.sync
        def _(sp):
            for f in layers["sp"]:
                f(sp, None)
            sp.wait_ge(out_ready, 1)
            sp.dma_start(tiled(out), x[:]).then_inc(stored, 16)
            sp.wait_ge(stored, 16)


INPUTS = ["x", "src", "dst", "edge_type_8", "edge_weight", "node_vec1"] + ["L0_gnn_" + n for n in (
    "Wv bv Ww bw Wa ba gamma beta").split()] + ["L0_ffn_" + n for n in "w_gating gamma w1 w2".split()] + [
    "L1_gnn_" + n for n in (
        "f_w1 f_b1 f_w2 f_b2 s1_w s1_b b1_w b1_b wq bq wk bk wv bv wo bo s2_w s2_b b2_w b2_b m_w1 m_b1 m_w2 m_b2").split()] + [
    "L1_ffn_" + n for n in "w_gating w1 w2".split()] + [
    "L2_gnn_" + n for n in "W a_src a_dst et_emb ln_gamma ln_beta".split()] + [
    "L2_ffn_" + n for n in "expert_weights expert_biases mixer_w mixer_b".split()] + [
    "L3_gnn_" + n for n in "Wq bq Wk bk Wv bv Wskip bskip Wlin blin gamma beta".split()] + [
    "L3_ffn_" + n for n in "r_w1 r_b1 r_w2 r_b2 wq0 wk0 wv0 wo0 wq1 wk1 wv1 wo1 wq2 wk2 wv2 wo2".split()]


def kernel(**inputs):
    import numpy as _np
    import concourse.bacc as _bacc
    from concourse import mybir as _mybir
    from concourse.bass_utils import run_bass_kernel_spmd as _run

    nc = _bacc.Bacc("TRN2", target_bir_lowering=False, num_devices=1)
    arrays, aps = {}, {}
    for name in INPUTS:
        a = _np.ascontiguousarray(inputs[name])
        arrays[f"in_{name}"] = a
        aps[name] = nc.dram_tensor(f"in_{name}", a.shape, _mybir.dt.from_np(a.dtype), kind="ExternalInput").ap()
    out = nc.dram_tensor("out_x", (N, D), F32, kind="ExternalOutput").ap()
    with nc.allow_non_contiguous_dma("bias columns and weight tiles are loaded in the layout that the engines read"):
        gnn_ffn_program(nc, aps, out)
    r = _run(nc, [arrays], core_ids=[0])
    return r.results[0]["out_x"]
```

```python
from contextlib import ExitStack, contextmanager

import concourse.bass as bass
from concourse import mybir

P = 128
N = 384
NT = N // P
D = 512
KC = D // P
E = 12288
ET = E // P
H8 = 8
HD = D // H8
EPS = 1e-5
MASKED = -1.0e30
SLOTS = 8
NB = 8
UNROLL = 8
ZB = 8
LEAD = 3
LAG = 6
RB = 4
F32 = mybir.dt.float32
BF16 = mybir.dt.bfloat16
F16 = mybir.dt.float16
I32 = mybir.dt.int32
U32 = mybir.dt.uint32
ALU = mybir.AluOpType
ACT = mybir.ActivationFunctionType
AX = mybir.AxisListType.X


class Banks:

    def __init__(self, psum, full, free):
        self.psum, self.full, self.free = psum, full, free
        self.uses, self.at, self.jobs, self.per = [0] * NB, 0, {}, None

    def open(self, pe, name, i=None):
        b = self.at
        self.at = (b + 1) % NB
        before, coef = self.uses[b], (self.per[b] if self.per else 0)
        self.uses[b] += 1
        self.jobs[name] = (b, before, coef)
        if before > 0:
            pe.wait_ge(self.free[b], before + i * coef if coef else before)
        return self.psum[:, b, :]

    @contextmanager
    def loop(self, trips, jobs, first=0):
        self.at = first
        start = list(self.uses)
        self.per = [sum((first + j) % NB == b for j in range(jobs)) for b in range(NB)]
        yield
        done = [u - s for u, s in zip(self.uses, start)]
        assert done == self.per, (sum(done), jobs)
        self.uses = [s + trips * k for s, k in zip(start, self.per)]
        self.per = None

    def count(self, name, i):
        b, before, coef = self.jobs[name]
        return b, (before + 1 + i * coef if coef and i is not None else before + 1)

    def full_of(self, name):
        return self.full[self.jobs[name][0]]

    def free_of(self, name):
        return self.free[self.jobs[name][0]]

    def filled(self, eng, name, i=None):
        b, n = self.count(name, i)
        eng.wait_ge(self.full[b], n)
        return self.psum[:, b, :]

    def drained(self, eng, name, i=None):
        b, n = self.count(name, i)
        eng.wait_ge(self.free[b], n)

    def all_drained(self, eng, names, i=None):
        for name in {self.jobs[name][0]: name for name in names}.values():
            self.drained(eng, name, i)


class Order:

    def __init__(self, eng, sem):
        self.eng, self.sem, self.n, self.more, self.looping = eng, sem, 0, 0, False

    def link(self, ins):
        self.n += 1
        ins.then_inc(self.sem, 1)
        self.eng.wait_ge(self.sem, self.n + self.more)

    def settle(self):
        if self.looping:
            self.eng.nop(nofuse=True)

    @contextmanager
    def loop(self, trips, per):
        start, self.looping = self.n, True
        with self.eng.Fori(0, trips) as i:
            self.more = i * per
            yield i
        assert self.n - start == per, (self.n - start, per)
        self.n, self.more, self.looping = start + trips * per, 0, False


class Ring:

    def __init__(self, slots, arrived):
        self.slots, self.arrived = slots, arrived
        self.got, self.per = [0] * SLOTS, None
        self.last = [None] * SLOTS

    def slot(self, s):
        return self.slots[:, s, :, :]

    def get(self, pe, s, i=None):
        self.got[s] += 1
        n = 16 * self.got[s]
        pe.wait_ge(self.arrived[s], n if i is None else n + i * 16)
        return self.slot(s)

    def after_loop(self, slots, trips):
        for s in slots:
            self.got[s] += trips - 1

    def load(self, sp, banks, s, pairs, used=None, i=None):
        job = used if used is not None else self.last[s]
        if job is not None:
            banks.filled(sp, *job)
            if used is not None:
                sp.nop(nofuse=True)
        assert len(pairs) == 1
        for dst, src in pairs:
            sp.dma_start(dst, src).then_inc(self.arrived[s], 16)


def gnn_ffn_program(nc, A, out):
    ctx = ExitStack()
    with ctx:
        def sb(name, shape, dt=F32):
            return ctx.enter_context(nc.sbuf_tensor(name, shape, dt))

        def sem(name):
            return ctx.enter_context(nc.semaphore(name))

        def sems(name, n):
            return [sem(f"{name}{i}") for i in range(n)]

        def dram(name, shape):
            return nc.dram_tensor(name, shape, F32, kind="Internal").ap()

        psum = ctx.enter_context(nc.psum_tensor("psum", [P, NB, 512], F32))
        banks = Banks(psum, sems("bank_full", NB), sems("bank_free", NB))
        ring = Ring(sb("ring", [P, SLOTS, KC, D]), sems("slot_arrived", SLOTS))

        x = sb("x", [P, NT, D])
        xn = sb("xn", [P, NT, D])
        xT = sb("xT", [P, KC, N])
        xn2 = sb("xn2", [P, NT, D])
        xT2 = sb("xT2", [P, KC, N])
        cnt_src = sb("cnt_src", [P, NT, N])
        cnt_dst = sb("cnt_dst", [P, NT, N])
        mask_src = sb("mask_src", [P, NT, N])
        mask_dst = sb("mask_dst", [P, NT, N])
        ident = sb("ident", [P, P])
        tri = sb("tri", [P, P])
        ones = sb("ones", [P, P])
        zeros = sb("zeros", [P, 512])
        iota = sb("iota", [P, N])
        iota_back = sb("iota_back", [P, 16])
        sd_i = sb("sd_i", [P, ET, 3], I32)
        rec = sb("rec", [P, ET, 4])
        src_f, dst_f, typ_f, ew = (rec[:, :, k] for k in range(4))
        pos = sb("pos", [P, ET], I32)
        pos_col = sb("pos_col", [P, 1], I32)
        rec_row = sb("rec_row", [P, 4])
        node_id = sb("node_id", [P, NT])
        stats = sb("stats", [P, NT, 6])
        mv = sb("mv", [P, NT, 2])
        vare = sb("vare", [P, NT])
        std = sb("std", [P, NT])
        rstd = sb("rstd", [P, NT])
        gate = sb("gate", [P, 16, 64])
        idx = sb("idx", [P, UNROLL, 3], I32)

        cols = sb("cols", [P, 160])
        rows = sb("rows", [1, 1536])
        bc = sb("bc", [P, 7, D])
        small = sb("small", [P, 512])
        AW = 13400
        arena = sb("arena", [P, AW])

        def view(off, *shape):
            n = 1
            for s in shape:
                n *= s
            assert off + n <= AW, (off, n)
            v = arena[:, off:off + n]
            if len(shape) == 2:
                v = v.rearrange("p (a b) -> p a b", a=shape[0])
            elif len(shape) == 3:
                v = v.rearrange("p (a b c) -> p a b c", a=shape[0], b=shape[1])
            return v

        params = sem("params")
        x_loaded = sem("x_loaded")
        edges_loaded = sem("edges_loaded")
        consts_ready = sem("consts_ready")
        pool_order = sem("pool_order")
        dve_order = sem("dve_order")
        act_order = sem("act_order")
        var_ready = sem("var_ready")
        std_ready = sem("std_ready")
        xn_ready = sem("xn_ready")
        hot_ready = sem("hot_ready")
        hot_used = sem("hot_used")
        source_hot = sem("source_hot")
        rank_ready = sem("rank_ready")
        rank_read = sem("rank_read")
        base_ready = sem("base_ready")
        base_copied = sem("base_copied")
        pos_ready = sem("pos_ready")
        u_ready = sem("u_ready")
        records_landed = sem("records_landed")
        sorted_loaded = sem("sorted_loaded")
        factor_ready = sem("factor_ready")
        cols_ready = sem("cols_ready")
        nodes_ready = sem("nodes_ready")
        lanes_ready = sem("lanes_ready")
        indices_ready = sem("indices_ready")
        gate_exp = sem("gate_exp")
        tables_stored = sem("tables_stored")
        rows_landed = sems("rows_landed", ZB)
        cols_landed = sems("cols_landed", ZB)
        w_landed = sems("w_landed", UNROLL)
        w_loaded = sems("w_loaded", NT)
        masked_ready = sem("masked_ready")
        neg_max = sem("neg_max")
        exp_done = sem("exp_done")
        relu_done = sem("relu_done")
        w_ready = sem("w_ready")
        diff_ready = sem("diff_ready")
        ex_done = sem("ex_done")
        msg_free = sem("msg_free")
        msg_ready = sem("msg_ready")
        msg_used = sem("msg_used")
        elu_in = sem("elu_in")
        elu_exp = sem("elu_exp")
        t_ready = sem("t_ready")
        e_done = sem("e_done")
        p_ready = sem("p_ready")
        step_ready = sem("step_ready")
        pe_col = sem("pe_col")
        out_ready = sem("out_ready")
        stored = sem("stored")

        loads = []

        def col(name, n, p=P, off=[0]):
            o = off[0]
            off[0] += n
            loads.append((cols[0:p, o:o + n], A[name], n, p))
            return cols[0:p, o:o + n]

        c_s1b = col("L1_gnn_s1_b", 16)
        c_b1b = col("L1_gnn_b1_b", 16)
        c_bq = col("L1_gnn_bq", 16)
        c_bk = col("L1_gnn_bk", 16)
        c_s2b = col("L1_gnn_s2_b", 16)
        c_b2b = col("L1_gnn_b2_b", 16)
        c_mb1 = col("L1_gnn_m_b1", 16)
        c_bq3 = col("L3_gnn_bq", 16)
        c_bk3 = col("L3_gnn_bk", 16)
        c_bs3 = col("L3_gnn_bskip", 16)
        loads = [(d, (s.rearrange("b (c p) -> p (b c)", p=P) if len(s.shape) == 2 else s.rearrange("(c p) -> p c", p=P)))
                 for d, s, n, p in loads]
        c_g0 = small[:, 0:4]
        loads.append((c_g0, A["L0_ffn_gamma"].rearrange("(c p) -> p c", p=P)))
        c_fb1, c_fb2 = small[0:16, 4:5], small[0:16, 5:6]
        loads.append((c_fb1, A["L1_gnn_f_b1"].unsqueeze(1)))
        loads.append((c_fb2, A["L1_gnn_f_b2"].unsqueeze(1)))
        c_rb1 = small[:, 6:7]
        loads.append((c_rb1, A["L3_ffn_r_b1"].unsqueeze(1)))
        r_rb2 = small[0:1, 7:10]
        loads.append((r_rb2, A["L3_ffn_r_b2"].unsqueeze(0)))
        ba0 = small[:, 10:11]
        loads.append((ba0, A["L0_gnn_ba"].partition_broadcast(P)))
        r_mixb = small[0:1, 12:20]
        loads.append((r_mixb, A["L2_ffn_mixer_b"].unsqueeze(0)))
        et_bc = small[:, 20:84]
        loads.append((et_bc, A["L2_gnn_et_emb"].rearrange("a b -> (a b)").partition_broadcast(P)))
        wg0 = small[:, 84:108].rearrange("p (c e) -> p c e", c=KC)
        loads.append((wg0, A["L0_ffn_w_gating"].rearrange("(c p) e -> p c e", p=P)))
        wg1 = small[:, 108:172].rearrange("p (c e) -> p c e", c=KC)
        loads.append((wg1, A["L1_ffn_w_gating"].rearrange("(c p) e -> p c e", p=P)))
        fw1 = small[0:64, 172:188]
        loads.append((fw1, A["L1_gnn_f_w1"]))
        fw2 = small[0:16, 188:204]
        loads.append((fw2, A["L1_gnn_f_w2"]))
        rw2 = small[:, 204:207]
        loads.append((rw2, A["L3_ffn_r_w2"]))
        mixT = small[:, 208:240].rearrange("p (c e) -> p c e", c=KC)
        wa = small[:, 240:368]
        loads.append((wa, A["L0_gnn_Wa"].rearrange("d a -> (a d)").partition_broadcast(P)))
        r_bw = rows[0:1, 0:1024]
        loads.append((r_bw, A["L0_gnn_bw"].unsqueeze(0)))
        r_bv0 = rows[0:1, 1024:1536]
        loads.append((r_bv0, A["L0_gnn_bv"].unsqueeze(0)))
        BC = {}
        for j, nm in enumerate(("L2_gnn_a_src", "L2_gnn_a_dst", "L2_gnn_ln_gamma", "L2_gnn_ln_beta", "L3_gnn_gamma",
                                "L3_gnn_beta", "L3_gnn_blin")):
            a = A[nm]
            BC[nm] = bc[:, j, :]
            loads.append((bc[:, j, :], (a.rearrange("a b -> (a b)") if len(a.shape) == 2 else a).partition_broadcast(P)))
        early = mask_src[:].rearrange("p c n -> p (c n)")
        BC["L0_gnn_gamma"], BC["L0_gnn_beta"] = early[:, 0:D], early[:, D:2 * D]
        for nm in ("L0_gnn_gamma", "L0_gnn_beta"):
            loads.append((BC[nm], A[nm].partition_broadcast(P)))
        PARAMS = 16 * len(loads)

        UW = 2 * D + H8
        tab_u = dram("tab_u", (N, UW))
        tab_v = dram("tab_v", (N, UW))
        tab_w = dram("tab_w", (N * N, H8))
        tab_h = dram("tab_h", (N, D))
        tab_sorted = dram("tab_sorted", (E, 4))

        def tiled(t):
            return t.rearrange("(c p) n -> p c n", p=P)

        def mm(o, a, b, start, stop):
            return nc.tensor.matmul(o, a, b, start=start, stop=stop)

        def pe_transpose(pe, tag, src, i=None):
            for c in range(KC):
                b = banks.open(pe, f"{tag}{c}", i)
                for t in range(NT):
                    last = nc.tensor.transpose(b[:, t * P:(t + 1) * P], src[:, t, c * P:(c + 1) * P], ident[:])
                last.then_inc(banks.full_of(f"{tag}{c}"), 1)

        def act_copy(act, name, dst, w=512, i=None):
            b = banks.filled(act, name, i)
            nc.scalar.activation(dst, b[:, 0:w], ACT.Copy).then_inc(banks.free_of(name), 1)

        def act_transposed(act, tag, dst, i=None):
            for c in range(KC):
                act_copy(act, f"{tag}{c}", dst[:, c, :], N, i)

        def pe_rows(pe, name, aT, w, t, bias=None, i=None, col0=0, n=D):
            b = banks.open(pe, name, i)
            for c in range(KC):
                last = mm(b[:, 0:n], aT[:, c, t * P:(t + 1) * P], w[:, c, col0:col0 + n], c == 0,
                          c == KC - 1 and bias is None)
            if bias is not None:
                last = mm(b[:, 0:n], ones[0:1, :], bias, False, True)
            last.then_inc(banks.full_of(name), 1)

        def pe_cols(pe, name, aT, w, col0, i=None):
            b = banks.open(pe, name, i)
            for c in range(KC):
                last = mm(b[:, 0:N], w[:, c, col0:col0 + P], aT[:, c, :], c == 0, c == KC - 1)
            last.then_inc(banks.full_of(name), 1)

        def dve_norm(dve, od, call, src, dst, gamma=None, beta=None, measured=False):
            if not measured:
                od.settle()
                for t in range(NT):
                    last = nc.vector.bn_stats(stats[:, t, :], src[:, t, :])
                od.link(last)
            od.settle()
            for t in range(NT):
                last = nc.vector.bn_aggr(mv[:, t, :], stats[:, t, :])
            od.link(last)
            nc.vector.tensor_scalar_add(vare[:], mv[:, :, 1], EPS).then_inc(var_ready, 1)
            dve.wait_ge(std_ready, call + 1)
            od.link(nc.vector.reciprocal(rstd[:], std[:]))
            for t in range(NT):
                last = nc.vector.tensor_scalar(dst[:, t, :], src[:, t, :], mv[:, t, 0:1], rstd[:, t:t + 1],
                                               ALU.subtract, ALU.mult)
            if gamma is not None:
                od.link(last)
                for t in range(NT):
                    last = nc.vector.tensor_tensor(dst[:, t, :], dst[:, t, :], gamma, ALU.mult)
            if beta is not None:
                od.link(last)
                for t in range(NT):
                    last = nc.vector.tensor_tensor(dst[:, t, :], dst[:, t, :], beta, ALU.add)
            last.then_inc(xn_ready, 1)

        def act_norm(act, call):
            act.wait_ge(var_ready, call + 1)
            nc.scalar.activation(std[:], vare[:], ACT.Sqrt).then_inc(std_ready, 1)

        def dve_softmax_logits(dve, od, name, e, call):
            b = banks.filled(dve, name)[:, 0:NT * e].rearrange("p (t e) -> p t e", t=NT)
            pr, mx = g3(0, e), gate[:, 1, 0:NT]
            od.link(nc.vector.tensor_reduce(mx, b, AX, ALU.max))
            nc.vector.tensor_tensor(g3(2, e), b, mx.unsqueeze(2).broadcast_to([P, NT, e]),
                                    ALU.subtract).then_inc(banks.free_of(name), 1)
            dve.wait_ge(gate_exp, call + 1)
            od.link(nc.vector.tensor_reduce(gate[:, 1, 8:8 + NT], pr, AX, ALU.add))
            od.link(nc.vector.reciprocal(gate[:, 1, 16:16 + NT], gate[:, 1, 8:8 + NT]))
            od.link(nc.vector.tensor_tensor(pr, pr, gate[:, 1, 16:16 + NT].unsqueeze(2).broadcast_to([P, NT, e]), ALU.mult))

        def act_softmax_logits(act, name, e):
            banks.drained(act, name)
            nc.scalar.activation(g3(0, e), g3(2, e), ACT.Exp).then_inc(gate_exp, 1)

        def g3(j, e):
            return gate[:, j, 0:NT * e].rearrange("p (t e) -> p t e", t=NT)

        def dve_top1(od, pr, e, g, onehot, tmp):
            od.link(nc.vector.tensor_reduce(g, pr, AX, ALU.max))
            od.link(nc.vector.tensor_tensor(tmp, pr, g.unsqueeze(2).broadcast_to([P, NT, e]), ALU.is_equal))
            back = iota_back[:, 0:e].unsqueeze(1).broadcast_to([P, NT, e])
            od.link(nc.vector.tensor_tensor(tmp, tmp, back, ALU.mult))
            first = gate[:, 3, 0:NT]
            od.link(nc.vector.tensor_reduce(first, tmp, AX, ALU.min))
            od.link(nc.vector.tensor_tensor(onehot, back, first.unsqueeze(2).broadcast_to([P, NT, e]), ALU.is_equal))

        def pe_logits(pe, name, aT, w, e, bias=None):
            b = banks.open(pe, name)
            for t in range(NT):
                for c in range(KC):
                    last = mm(b[:, t * e:(t + 1) * e], aT[:, c, t * P:(t + 1) * P], w[:, c, :], c == 0,
                              c == KC - 1 and bias is None)
                if bias is not None:
                    last = mm(b[:, t * e:(t + 1) * e], ones[0:1, :], bias, False, True)
            last.then_inc(banks.full_of(name), 1)

        SPARE = 6
        spare = ring.slot(SPARE).rearrange("p c n -> p (c n)")
        two_probs, two_divide = view(AW - 4 * NT * N, 2, NT, N), view(AW - 4 * NT * N - 2 * NT * P, 2, NT, P)
        probs = [two_probs[:, 0], two_probs[:, 1], spare[:, 0:NT * N].rearrange("p (t n) -> p t n", t=NT)]
        divide = [two_divide[:, 0], two_divide[:, 1],
                  spare[:, NT * N:NT * (N + P)].rearrange("p (t n) -> p t n", t=NT)]
        probsT = view(AW - 2 * NT * N, 2, NT, N)
        amax = sb("amax", [P, 3, NT])
        asum = sb("asum", [P, 3, NT])

        def dve_att_scores(dve, od, tag, par, scale, mask, i):
            for t in range(NT):
                b = banks.filled(dve, f"{tag}s{t}", i)
                nc.vector.scalar_tensor_tensor(out=probs[par][:, t, :], in0=b[:, 0:N], scalar=scale, in1=mask[:, t, :],
                                               op0=ALU.mult, op1=ALU.add).then_inc(banks.free_of(f"{tag}s{t}"), 1)
            for t in range(NT):
                banks.drained(dve, f"{tag}s{t}", i)
            od.link(nc.vector.tensor_reduce(amax[:, par, :], probs[par], AX, ALU.max))
            nc.vector.tensor_scalar(amax[:, par, :], amax[:, par, :], -1.0, None, ALU.mult).then_inc(t_ready, 1)

        def dve_att_max(dve, od, tag, par, scale):
            for t in range(NT):
                last = nc.vector.tensor_reduce(amax[:, par, t:t + 1], banks.filled(dve, f"{tag}s{t}")[:, 0:N], AX, ALU.max)
            od.link(last)
            nc.vector.tensor_scalar(amax[:, par, :], amax[:, par, :], -scale, None, ALU.mult).then_inc(t_ready, 1)

        def act_att_exp(act, u, par):
            act.wait_ge(t_ready, u + 1)
            for t in range(NT):
                last = nc.scalar.activation(probs[par][:, t, :], probs[par][:, t, :], ACT.Exp, bias=amax[:, par, t:t + 1])
            last.then_inc(e_done, 1)

        def act_att_exp_scores(act, tag, u, par, scale):
            act.wait_ge(t_ready, u + 1)
            for t in range(NT):
                b = banks.filled(act, f"{tag}s{t}")
                nc.scalar.activation(probs[par][:, t, :], b[:, 0:N], ACT.Exp, bias=amax[:, par, t:t + 1], scale=scale,
                                     accum_out=asum[:, par, t:t + 1]).then_inc(banks.free_of(f"{tag}s{t}"), 1)

        def dve_att_probs(dve, od, u, par, count, tag=None):
            if count is None:
                for t in range(NT):
                    banks.drained(dve, f"{tag}s{t}")
            else:
                dve.wait_ge(e_done, u + 1)
                for t in range(NT):
                    last = nc.vector.scalar_tensor_tensor(out=probs[par][:, t, :], in0=probs[par][:, t, :], scalar=1.0,
                                                          in1=count[:, t, :], op0=ALU.mult, op1=ALU.mult,
                                                          accum_out=asum[:, par, t:t + 1])
                od.link(last)
                od.link(nc.vector.tensor_scalar_max(asum[:, par, :], asum[:, par, :], 1.0e-30))
            od.link(nc.vector.reciprocal(asum[:, par, :], asum[:, par, :]))
            nc.vector.tensor_tensor(divide[par], ident[:].unsqueeze(1).broadcast_to([P, NT, P]),
                                    asum[:, par, :].unsqueeze(2).broadcast_to([P, NT, P]), ALU.mult).then_inc(p_ready, 1)

        def pe_att_transpose(pe, tag, u, par, i=None):
            pe.wait_ge(p_ready, u + 1)
            for c in range(NT):
                b = banks.open(pe, f"{tag}p{c}", i)
                for t in range(NT):
                    last = mm(b[:, t * P:(t + 1) * P], probs[par][:, t, c * P:(c + 1) * P], divide[par][:, t, :], True, True)
                last.then_inc(banks.full_of(f"{tag}p{c}"), 1)

        def act_att_transposed(act, tag, par, i=None):
            for c in range(NT):
                act_copy(act, f"{tag}p{c}", probsT[:, par, c, :], N, i)

        ust = view(0, NT, UW)
        vst = view(NT * UW, NT, UW)
        zb = view(0, ZB, UW)
        hotb = arena[:, ZB * UW:ZB * UW + 2 * N].bitcast(BF16).rearrange("p (b k n) -> p b k n", b=2, k=2)
        w_row = view(ZB * UW + 2 * N, UNROLL, H8)
        masked = view(2 * NT * UW, 4 * N)
        prod0 = view(2 * NT * UW + 4 * N, 2 * D)
        wm = view(0, NT, N * H8)
        ost = view(NT * N * H8, NT, D)
        pw = view(NT * N * H8 + NT * D, 2, NT, N)
        pwT = [xT, xT2]
        wa99 = small[:, 368:496]
        go = view(0, RB, D)
        MW = D // 2 + H8 // 2
        msg = view(RB * D + 80, RB, 2, MW)
        hot = view(RB * D + 80 + RB * 528, RB, N)

        def pool_gather(o, table, column, **more):
            return nc.gpsimd.indirect_dma_start(o, None, table, bass.IndirectOffsetOnAxis(ap=column.bitcast(U32), axis=0), **more)

        def pool_scatter_rows(pool, op, table):
            with op.loop(ET // RB, RB) as i:
                for b in range(RB):
                    t = RB * i + b
                    pool.wait_ge(msg_free, t + 1)
                    op.link(nc.gpsimd.tensor_copy(idx[:, b, :], sd_i[:, bass.ds(t, 1), :].rearrange("p a k -> p (a k)")))
                    pool.nop(nofuse=True)
                    pool_gather(go[:, b, :], table, idx[:, b, 0:1]).then_inc(rows_landed[b], 16)

        def dve_scatter_rows(dve, od, key, weight, landed_before):
            with od.loop(ET // RB, RB) as i:
                for b in range(RB):
                    t = RB * i + b
                    dve.wait_ge(msg_used, t + 1)
                    nc.vector.tensor_scalar(hot[:, b, :], iota[:], key[:, bass.ds(t, 1)], None, ALU.is_equal)
                    p = weight[:, bass.ds(t, 1), :]
                    nc.vector.tensor_copy(msg[:, b, :, 256:MW], p.rearrange("p a (f h) -> p (a f) h", f=2))
                    dve.wait_ge(rows_landed[b], 16 * (i + 1) + landed_before)
                    for hf in range(2):
                        last = nc.vector.tensor_tensor(
                            msg[:, b, hf, 0:256].rearrange("p (h d) -> p h d", h=4),
                            go[:, b, hf * 256:hf * 256 + 256].rearrange("p (h d) -> p h d", h=4),
                            p[:, :, hf * 4:hf * 4 + 4].rearrange("p a h -> p (a h)").unsqueeze(2).broadcast_to([P, 4, HD]),
                            ALU.mult)
                    od.link(last)
                    nc.vector.memset(gate[:, 15, 0:1], 0.0).then_inc(msg_free, 1)
                    nc.vector.memset(gate[:, 15, 3:4], 0.0).then_inc(msg_ready, 1)

        def pe_scatter_rows(pe, tag):
            bk = [[banks.open(pe, f"{tag}a{c}{hf}") for hf in range(2)] for c in range(NT)]
            for c in range(NT):
                for hf in range(2):
                    last = mm(bk[c][hf][:, 0:MW], zeros[:, 0:P], zeros[:, 0:MW], True, False)
            last.then_inc(msg_used, RB)
            with pe.Fori(0, ET // RB) as i:
                for b in range(RB):
                    pe.wait_ge(msg_ready, RB * i + b + 1)
                    for c in range(NT):
                        for hf in range(2):
                            last = mm(bk[c][hf][:, 0:MW], hot[:, b, c * P:(c + 1) * P], msg[:, b, hf, :], False, False)
                    last.then_inc(msg_used, 1)
            for c in range(NT):
                for hf in range(2):
                    mm(bk[c][hf][:, 0:MW], zeros[:, 0:P], zeros[:, 0:MW], False, True).then_inc(
                        banks.full_of(f"{tag}a{c}{hf}"), 1)

        def dve_scatter_sums(dve, od, tag, tiny, add):
            for c in range(NT):
                for hf in range(2):
                    b = banks.filled(dve, f"{tag}a{c}{hf}")
                    den = gate[:, 4, 4 * (2 * c + hf):4 * (2 * c + hf) + 4]
                    od.link(nc.vector.tensor_scalar(den, b[:, 256:MW], tiny, None, ALU.add if add else ALU.max))
                    od.link(nc.vector.reciprocal(den, den))
                    nc.vector.tensor_tensor(
                        xn2[:, c, hf * 256:hf * 256 + 256].rearrange("p (h d) -> p h d", h=4),
                        b[:, 0:256].rearrange("p (h d) -> p h d", h=4),
                        den.unsqueeze(2).broadcast_to([P, 4, HD]),
                        ALU.mult).then_inc(banks.free_of(f"{tag}a{c}{hf}"), 1)
            for c in range(NT):
                for hf in range(2):
                    banks.drained(dve, f"{tag}a{c}{hf}")

        layers = {"sp": [], "act": [], "dve": [], "pe": [], "pool": []}

        def on(engine):
            def add(f):
                layers[engine].append(f)
                return f
            return add

        NORM = dict(l0=0, l0b=1, f0=2, f0b=3, l1=4, blk=5, f1=13, l2=14, l2b=15, f2=16, l3=17, l3b=18, f3=19)

        @on("sp")
        def _(sp, o):
            sp.dma_start(x[:], tiled(A["x"])).then_inc(x_loaded, 16)
            for dst, nm in ((src_i, "src"), (dst_i, "dst"), (typ_i, "edge_type_8"), (ew_in, "edge_weight")):
                sp.dma_start(dst, A[nm].rearrange("(p t) -> p t", p=P)).then_inc(edges_loaded, 16)

        @on("act")
        def _(act, o):
            for dst, src in loads:
                act.dma_start(dst, src).then_inc(params, 16)

        @on("pool")
        def _(pool, op):
            nc.gpsimd.memset(ident[:], 0.0)
            nc.gpsimd.memset(ones[:], 1.0)
            nc.gpsimd.memset(zeros[:], 0.0)
            nc.gpsimd.iota(iota[:], pattern=[[1, N]], base=0, channel_multiplier=0, allow_small_or_imprecise_dtypes=True)
            op.link(nc.gpsimd.iota(iota_back[:], pattern=[[1, 16]], base=-64, channel_multiplier=0,
                                   allow_small_or_imprecise_dtypes=True))
            nc.gpsimd.affine_select(out=ident[:], in_=ident[:], compare_op=ALU.not_equal, fill=1.0, base=0,
                                    pattern=[[-1, P]], channel_multiplier=1)
            nc.gpsimd.iota(node_id[:], pattern=[[P, NT]], base=0, channel_multiplier=1, allow_small_or_imprecise_dtypes=True)
            nc.gpsimd.affine_select(out=tri[:], in_=ones[:], compare_op=ALU.is_gt, fill=0.0, base=0,
                                    pattern=[[1, P]], channel_multiplier=-1).then_inc(consts_ready, 1)

        @on("dve")
        def _(dve, od):
            dve.wait_ge(edges_loaded, 64)
            dve.wait_ge(consts_ready, 1)
            nc.vector.tensor_copy(src_f, src_i)
            nc.vector.tensor_copy(typ_f, typ_i)
            nc.vector.tensor_copy(ew, ew_in)
            nc.vector.tensor_copy(tri_b, tri[:])
            nc.vector.memset(ones_b, 1.0)
            od.link(nc.vector.tensor_copy(dst_f, dst_i))
            od.link(nc.vector.scalar_tensor_tensor(out=sel0[:], in0=src_f, scalar=float(N), in1=dst_f, op0=ALU.mult, op1=ALU.add))
            nc.vector.tensor_copy(sd_i[:, :, 0], src_i)
            nc.vector.tensor_copy(sd_i[:, :, 1], dst_i)
            nc.vector.tensor_copy(sd_i[:, :, 2], sel0[:]).then_inc(indices_ready, 1)

        sel0 = prod0[:, 0:ET]
        sort0 = NT * N * H8 + NT * D
        src_i, dst_i, typ_i = (arena[:, sort0 + k * ET:sort0 + (k + 1) * ET].bitcast(I32) for k in range(3))
        ew_in = view(sort0 + 3 * ET, ET)
        later = arena[:, 0:2 * N].bitcast(BF16).rearrange("p (b n) -> p b n", b=RB)
        first_pos = view(sort0 + 4 * ET + N, 2, N)
        tri_b, ones_b = (arena[:, sort0 + 4 * ET + 3 * N + k * 64:sort0 + 4 * ET + 3 * N + (k + 1) * 64].bitcast(BF16)
                         for k in range(2))
        ranked = view(sort0 + 4 * ET + 3 * N + 128, N)
        pos_f = view(sort0 + 4 * ET + 4 * N + 128, UNROLL)
        apart0 = sort0 + 4 * ET + 4 * N + 128 + UNROLL
        apart = arena[:, apart0:apart0 + N].bitcast(BF16).rearrange("p (b n) -> p b n", b=2)

        @on("sp")
        def _(sp, o):
            Ww = A["L0_gnn_Ww"].rearrange("(r c p) (q n) -> r q p c n", r=2, p=P, q=2)
            for r in range(2):
                for q in range(2):
                    ring.load(sp, banks, 2 * r + q, [(ring.slot(2 * r + q), Ww[r, q])])
                    ring.last[2 * r + q] = (f"l0uv{r}{q}2",)
            ring.load(sp, banks, 4, [(ring.slot(4), A["L0_gnn_Wv"].rearrange("(c p) n -> p c n", p=P))])
            ring.last[4] = ("l0o2",)

        filled = sem("filled")

        def l0_store_tables(sp):
            sp.wait_ge(masked_ready, 1)
            flat_w = tab_w.rearrange("(p a) h -> p (a h)", p=P)
            for j in range(6):
                    sp.dma_start(flat_w[:, j * 4 * N:(j + 1) * 4 * N], masked).then_inc(filled, 16)
            sp.wait_ge(u_ready, 1)
            sp.dma_start(tiled(tab_u), ust[:]).then_inc(tables_stored, 16)
            sp.wait_ge(step_ready, 1)
            sp.dma_start(tiled(tab_v), vst[:]).then_inc(tables_stored, 16)

        @on("pe")
        def _(pe, o):
            pe.wait_ge(consts_ready, 1)
            b = banks.open(pe, "hist")
            mm(b[:, 0:N], zeros[:, 0:P], zeros[:, 0:N], True, False).then_inc(hot_used, RB)
            with pe.Fori(0, ET // RB) as i:
                for k in range(RB):
                    pe.wait_ge(hot_ready, RB * i + k + 1)
                    mm(b[:, 0:N], ones_b, later[:, k, :], False, False).then_inc(hot_used, 1)
            mm(b[:, 0:N], zeros[:, 0:P], zeros[:, 0:N], False, True).then_inc(banks.full_of("hist"), 1)
            pe.wait_ge(params, PARAMS)
            pe.wait_ge(xn_ready, NORM["l0"] + 1)
            pe_transpose(pe, "l0x", xn)
            for c in range(KC):
                banks.drained(pe, f"l0x{c}")
            for r in range(2):
                for q in range(2):
                    w = ring.get(pe, 2 * r + q)
                    for t in range(NT):
                        pe_rows(pe, f"l0uv{r}{q}{t}", xT, w, t, r_bw[:, q * 512:q * 512 + 512] if r else None)
            w = ring.get(pe, 4)
            for t in range(NT):
                pe_rows(pe, f"l0o{t}", xT, w, t, r_bv0)
            bk = [banks.open(pe, f"cnt{c}") for c in range(NT)]
            for c in range(NT):
                last = mm(bk[c][:, 0:N], zeros[:, 0:P], zeros[:, 0:N], True, False)
            rank, base = banks.open(pe, "rank"), banks.open(pe, "base")
            banks.drained(pe, "hist")
            with pe.Fori(0, ET // 2) as i:
                for b in range(2):
                    pe.wait_ge(hot_ready, 2 * i + b + 1 + ET)
                    pe.wait_ge(base_copied, 2 * i + b + 1)
                    mm(rank[:, 0:N], ident[:], first_pos[:, b, :], True, False)
                    mm(rank[:, 0:N], tri_b, hotb[:, b, 1, :], False, True).then_inc(rank_ready, 1)
                    mm(base[:, 0:N], ident[:], first_pos[:, b, :], True, False)
                    mm(base[:, 0:N], ones_b, hotb[:, b, 1, :], False, True).then_inc(base_ready, 1)
                    pe.wait_ge(source_hot, 2 * i + b + 1)
                    for c in range(NT):
                        last = mm(bk[c][:, 0:N], hotb[:, b, 0, c * P:(c + 1) * P], hotb[:, b, 1, :], False, False)
                    last.then_inc(hot_used, 1)
            for c in range(NT):
                mm(bk[c][:, 0:N], zeros[:, 0:P], zeros[:, 0:N], False, True).then_inc(banks.full_of(f"cnt{c}"), 1)
            pe.wait_ge(rank_read, ET)
            pe.wait_ge(base_copied, ET + 1)
            for nm, b in (("rank", rank), ("base", base)):
                mm(b[:, 0:N], zeros[:, 0:P], zeros[:, 0:N], True, True).then_inc(banks.full_of(nm), 1)
            for c in range(NT):
                banks.drained(pe, f"cnt{c}")
            for c in range(NT):
                b = banks.open(pe, f"cntT{c}")
                for t in range(NT):
                    last = nc.tensor.transpose(b[:, t * P:(t + 1) * P], cnt_src[:, t, c * P:(c + 1) * P], ident[:])
                last.then_inc(banks.full_of(f"cntT{c}"), 1)
            for h in range(H8 + 1):
                if h < H8:
                    pe.wait_ge(exp_done, h + 1)
                    for c in range(NT):
                        b = banks.open(pe, f"l0p{h}{c}")
                        for t in range(NT):
                            last = nc.tensor.transpose(b[:, t * P:(t + 1) * P], pw[:, h % 2, t, c * P:(c + 1) * P], ident[:])
                        last.then_inc(banks.full_of(f"l0p{h}{c}"), 1)
                if h >= 1:
                    g = h - 1
                    for c in range(NT):
                        banks.drained(pe, f"l0p{g}{c}")
                    b = banks.open(pe, f"l0y{g}")
                    for t in range(NT):
                        for c in range(NT):
                            last = mm(b[:, t * HD:(t + 1) * HD], pwT[g % 2][:, c, t * P:(t + 1) * P],
                                      ost[:, c, g * HD:(g + 1) * HD], c == 0, c == NT - 1)
                    last.then_inc(banks.full_of(f"l0y{g}"), 1)

        @on("act")
        def _(act, o):
            act_norm(act, NORM["l0"])
            b = banks.filled(act, "hist")
            nc.scalar.activation(first_pos[:, 0, 0:N // 2], b[:, 0:N // 2], ACT.Copy).then_inc(base_copied, 1)
            nc.scalar.activation(first_pos[:, 0, N // 2:N], b[:, N // 2:N], ACT.Copy).then_inc(banks.free_of("hist"), 1)
            act_transposed(act, "l0x", xT)
            for r in range(2):
                for q in range(2):
                    for t in range(NT):
                        act_copy(act, f"l0uv{r}{q}{t}", (vst if r else ust)[:, t, q * 512:q * 512 + 512])
            for t in range(NT):
                act_copy(act, f"l0o{t}", ost[:, t, :])
            act.wait_ge(tables_stored, 32)
            with o.loop(ET // UNROLL, UNROLL) as i:
                for b in range(UNROLL):
                    act.wait_ge(hot_used, UNROLL * i + b + ET + RB - 1)
                    o.link(nc.scalar.activation(apart[:, b % 2, :], iota[:], ACT.Square, bias=src_f[:, bass.ds(UNROLL * i + b, 1)], scale=-1.0))
                    nc.scalar.activation(hotb[:, b % 2, 0, :], apart[:, b % 2, :], ACT.Relu, bias=ones[:, 0:1], scale=-1.0).then_inc(
                        source_hot, 1)
                    z = b % ZB
                    act.wait_ge(cols_landed[z], 16 * (UNROLL // ZB * i + b // ZB + 1))
                    nc.scalar.activation(zb[:, z, 0:2 * D], zb[:, z, 0:2 * D], ACT.Relu).then_inc(relu_done, 1)
                    act.wait_ge(base_ready, UNROLL * i + b + 1)
                    nc.scalar.activation(first_pos[:, 1 - b % 2, :], psum[:, banks.jobs["base"][0], 0:N],
                                         ACT.Copy).then_inc(base_copied, 1)
            act.wait_ge(neg_max, 1)
            for h in range(H8 + 1):
                if h < H8:
                    if h >= 2:
                        banks.filled(act, f"l0p{h - 2}{NT - 1}")
                    for t in range(NT):
                        last = nc.scalar.activation(pw[:, h % 2, t, :], wm[:, t, :].rearrange("p (j h) -> p h j", h=H8)[:, h, :],
                                                    ACT.Exp, bias=gate[:, 5, t * H8 + h:t * H8 + h + 1],
                                                    accum_out=gate[:, 9, h * NT + t:h * NT + t + 1])
                    last.then_inc(exp_done, 1)
                if h >= 1:
                    for c in range(NT):
                        act_copy(act, f"l0p{h - 1}{c}", pwT[(h - 1) % 2][:, c, :], N)
            act.wait_ge(elu_in, 1)
            nc.scalar.activation(xn2b[:], xn2b[:], ACT.Exp).then_inc(elu_exp, 1)
            act_norm(act, NORM["l0b"])

        xn2b = view(0, NT, D)

        @on("pool")
        def _(pool, op):
            nc.gpsimd.memset(masked, MASKED).then_inc(masked_ready, 1)
            pool.wait_ge(tables_stored, 32)
            pool.wait_ge(indices_ready, 1)

            def first_rows(i, b, first):
                if not first:
                    pool.wait_ge(w_landed[b], 16 * i)
                op.link(nc.gpsimd.tensor_copy(idx[:, b, :], sd_i[:, bass.ds(UNROLL * i + b, 1), :].rearrange("p a k -> p (a k)")))
                pool.nop(nofuse=True)
                pool_gather(zb[:, b % ZB, :], tab_u, idx[:, b, 0:1]).then_inc(rows_landed[b % ZB], 16)

            def second_rows(i, b):
                pool.wait_ge(rows_landed[b % ZB], 16 * (UNROLL // ZB * i + b // ZB + 1))
                pool.nop(nofuse=True)
                pool_gather(zb[:, b % ZB, :], tab_v, idx[:, b, 1:2], compute_op=ALU.add).then_inc(cols_landed[b % ZB], 16)

            def store_scores(i, b, first=False):
                if b >= 1:
                    pool.wait_ge(w_landed[b - 1], 16 * (i + 1))
                elif not first:
                    pool.wait_ge(w_landed[UNROLL - 1], 16 * i)
                pool.wait_ge(w_ready, UNROLL * i + b + 1)
                pool.nop(nofuse=True)
                nc.gpsimd.indirect_dma_start(tab_w, bass.IndirectOffsetOnAxis(ap=idx[:, b, 2:3].bitcast(U32), axis=0),
                                             w_row[:, b, :], None).then_inc(w_landed[b], 16)

            def tiles(i, first):
                for b in range(UNROLL):
                    if b >= LAG:
                        store_scores(i, b - LAG, first)
                    elif not first:
                        store_scores(i - 1, b + UNROLL - LAG)
                    first_rows(i, b, first)
                    if b >= LEAD:
                        second_rows(i, b - LEAD)
                    elif not first:
                        second_rows(i - 1, b + UNROLL - LEAD)

            pool.wait_ge(filled, 96)
            tiles(0, True)
            with op.loop(ET // UNROLL - 1, UNROLL) as i:
                tiles(i + 1, False)
            for b in range(UNROLL - LEAD, UNROLL):
                second_rows(ET // UNROLL - 1, b)
            for b in range(UNROLL - LAG, UNROLL):
                store_scores(ET // UNROLL - 1, b)

        @on("dve")
        def _(dve, od):
            dve.wait_ge(x_loaded, 16)
            dve_norm(dve, od, NORM["l0"], x, xn)
            with dve.Fori(0, ET // RB) as i:
                for k in range(RB):
                    dve.wait_ge(hot_used, RB * i + k + 1)
                    nc.vector.tensor_scalar(later[:, k, :], iota[:], dst_f[:, bass.ds(RB * i + k, 1)], None,
                                            ALU.is_gt).then_inc(hot_ready, 1)
            dve.wait_ge(params, PARAMS)
            wa_bc = wa.unsqueeze(1).broadcast_to([P, H8, P])
            od.link(nc.vector.tensor_scalar(wa99, wa, 1.0 - 0.01, None, ALU.mult))
            for r, tab in ((0, ust), (1, vst)):
                for t in range(NT):
                    for q in range(2):
                        banks.drained(dve, f"l0uv{r}{q}{t}")
                    od.link(nc.vector.tensor_tensor(prod0.rearrange("p (h d) -> p h d", h=H8),
                                                    tab[:, t, 0:2 * D].rearrange("p (h d) -> p h d", h=H8), wa_bc, ALU.mult))
                    lin = tab[:, t, 2 * D:UW]
                    od.link(nc.vector.tensor_reduce(lin, prod0.rearrange("p (h d) -> p h d", h=H8), AX, ALU.add))
                    od.link(nc.vector.tensor_scalar(lin, lin, 0.01, ba0 if r else 0.0, ALU.mult, ALU.add))
                if r == 0:
                    nc.vector.memset(gate[:, 15, 7:8], 0.0).then_inc(u_ready, 1)
            nc.vector.memset(gate[:, 15, 1:2], 0.0).then_inc(step_ready, 1)
            dve.wait_ge(tables_stored, 32)
            def score_tiles(i, last):
                for b in range(UNROLL):
                    t = UNROLL * i + b
                    dve.wait_ge(hot_used, t + ET + RB - 1)
                    nc.vector.tensor_scalar(hotb[:, b % 2, 1, :], iota[:], dst_f[:, bass.ds(t, 1)], None,
                                            ALU.is_equal).then_inc(hot_ready, 1)
                    dve.wait_ge(relu_done, t + 1)
                    if last is not None:
                        dve.wait_ge(w_landed[b], 16 * (last + 1))
                    z3 = zb[:, b % ZB, 0:2 * D].rearrange("p (h d) -> p h d", h=H8)
                    od.link(nc.vector.tensor_tensor(z3, z3, wa99.unsqueeze(1).broadcast_to([P, H8, P]), ALU.mult))
                    od.link(nc.vector.tensor_reduce(w_row[:, b, :], z3, AX, ALU.add))
                    nc.vector.tensor_tensor(w_row[:, b, :], w_row[:, b, :], zb[:, b % ZB, 2 * D:UW], ALU.add).then_inc(w_ready, 1)
                    dve.wait_ge(rank_ready, t + 1)
                    last_rank = nc.vector.scalar_tensor_tensor(
                        out=ranked, in0=hotb[:, b % 2, 1, :], scalar=1.0, in1=psum[:, banks.jobs["rank"][0], 0:N],
                        op0=ALU.mult, op1=ALU.mult, accum_out=pos_f[:, b:b + 1])
                    last_rank.then_inc(rank_read, 1)
                dve.wait_ge(rank_read, UNROLL * i + UNROLL)
                nc.vector.tensor_copy(pos[:, bass.ds(UNROLL * i, UNROLL)], pos_f)

            score_tiles(0, None)
            with od.loop(ET // UNROLL - 1, 2 * UNROLL) as i:
                score_tiles(i + 1, i)
            nc.vector.memset(gate[:, 15, 10:11], 0.0).then_inc(pos_ready, 1)
            for k, nm in enumerate(("rank", "base")):
                banks.filled(dve, nm)
                nc.vector.memset(gate[:, 15, 8 + k:9 + k], 0.0).then_inc(banks.free_of(nm), 1)
            for c in range(NT):
                b = banks.filled(dve, f"cnt{c}")
                nc.vector.tensor_copy(cnt_src[:, c, :], b[:, 0:N]).then_inc(banks.free_of(f"cnt{c}"), 1)
            for c in range(NT):
                b = banks.filled(dve, f"cntT{c}")
                nc.vector.tensor_copy(cnt_dst[:, c, :], b[:, 0:N]).then_inc(banks.free_of(f"cntT{c}"), 1)
            top, keep = gate[:, 4, 0:NT * H8], gate[:, 6, 0:NT * H8]
            for t in range(NT):
                dve.wait_ge(w_loaded[t], 16)
                last = nc.vector.tensor_reduce(top[:, t * H8:(t + 1) * H8], wm[:, t, :].rearrange("p (j h) -> p h j", h=H8), AX, ALU.max)
            od.link(last)
            nc.vector.tensor_scalar(keep, top, 0.5 * MASKED, None, ALU.is_gt)
            nc.vector.tensor_scalar(gate[:, 5, 0:NT * H8], top, -1.0, None, ALU.mult).then_inc(neg_max, 1)
            for h in range(H8):
                dve.wait_ge(exp_done, h + 1)
                s3 = gate[:, 9, h * NT:(h + 1) * NT]
                od.link(nc.vector.reciprocal(s3, s3))
                od.link(nc.vector.tensor_tensor(s3, s3, keep.rearrange("p (t h) -> p h t", h=H8)[:, h, :], ALU.mult))
                b = banks.filled(dve, f"l0y{h}")
                nc.vector.tensor_tensor(xn2[:, :, h * HD:(h + 1) * HD], b[:, 0:NT * HD].rearrange("p (t d) -> p t d", t=NT),
                                        s3.unsqueeze(2).broadcast_to([P, NT, HD]), ALU.mult).then_inc(banks.free_of(f"l0y{h}"), 1)
            for h in range(H8):
                banks.drained(dve, f"l0y{h}")
            nc.vector.tensor_scalar(xn2b[:], xn2[:], 0.0, None, ALU.min).then_inc(elu_in, 1)
            dve.wait_ge(elu_exp, 1)
            od.link(nc.vector.scalar_tensor_tensor(out=flat(xn2), in0=flat(xn2), scalar=0.0, in1=flat(xn2b), op0=ALU.max,
                                                   op1=ALU.add))
            od.link(nc.vector.scalar_tensor_tensor(out=flat(xn2), in0=flat(xn2), scalar=-1.0, in1=flat(xn), op0=ALU.add,
                                                   op1=ALU.add))
            dve_norm(dve, od, NORM["l0b"], xn2, xn2, BC["L0_gnn_gamma"], BC["L0_gnn_beta"])
            dve.wait_ge(xn_ready, NORM["l0b"] + 1)
            od.link(nc.vector.tensor_tensor(x[:], x[:], xn2[:], ALU.add))

        def flat(a):
            return a[:].rearrange("p t n -> p (t n)")

        @on("sp")
        def _(sp, o):
            l0_store_tables(sp)

        E0, E1 = A["L0_ffn_w1"].shape[0], A["L1_ffn_w1"].shape[0]
        HE = A["L0_ffn_w1"].shape[2]
        FC = HE // P
        CAP1 = max(min(N, int(N * 2 * 2.0 / E1)), 4)
        hid = view(0, 2 * FC, N).rearrange("p (b f) n -> p b f n", b=2)
        acc = view(4 * N, NT, D)

        def w1_of(s):
            return ring.slot(s).rearrange("p c n -> p (c n)").rearrange("p (e c h) -> p e c h", e=2, c=KC)

        def w2_of(s):
            return ring.slot(s).rearrange("p (e f) n -> p e f n", e=2)

        def load_pair(sp, w1, w2, e, s1, s2):
            ring.load(sp, banks, s1, [(w1_of(s1), w1[e:e + 2].rearrange("e (c p) h -> p e c h", p=P))])
            ring.load(sp, banks, s2, [(w2_of(s2), w2[e:e + 2].rearrange("e (f p) n -> p e f n", p=P))])

        def pe_expert_up(pe, tag, e, aT, s1, i=None):
            if e % 2 == 0:
                ring.get(pe, s1, i)
            for f in range(FC):
                b = banks.open(pe, f"{tag}h{e}{f}", i)
                for c in range(KC):
                    last = mm(b[:, 0:N], w1_of(s1)[:, e % 2, c, f * P:(f + 1) * P], aT[:, c, :], c == 0, c == KC - 1)
                last.then_inc(banks.full_of(f"{tag}h{e}{f}"), 1)

        def pe_expert_down(pe, tag, e, s2, i=None):
            if e % 2 == 0:
                ring.get(pe, s2, i)
            for f in range(FC):
                banks.drained(pe, f"{tag}h{e}{f}", i)
            for t in range(NT):
                b = banks.open(pe, f"{tag}e{e}{t}", i)
                for f in range(FC):
                    last = mm(b, hid[:, e % 2, f, t * P:(t + 1) * P], w2_of(s2)[:, e % 2, f, :], f == 0, f == FC - 1)
                last.then_inc(banks.full_of(f"{tag}e{e}{t}"), 1)

        def act_expert(act, tag, e, func, i=None):
            for f in range(FC):
                name = f"{tag}h{e}{f}"
                b = banks.filled(act, name, i)
                nc.scalar.activation(hid[:, e % 2, f, :], b[:, 0:N], func).then_inc(banks.free_of(name), 1)

        def dve_expert(dve, tag, e, weight, i=None):
            for t in range(NT):
                name = f"{tag}e{e}{t}"
                if e > 0:
                    banks.drained(dve, f"{tag}e{e - 1}{t}", i)
                b = banks.filled(dve, name, i)
                nc.vector.scalar_tensor_tensor(out=acc[:, t, :], in0=b, scalar=weight(t), in1=acc[:, t, :], op0=ALU.mult,
                                               op1=ALU.add).then_inc(banks.free_of(name), 1)

        F0_SLOTS = [(5, 6), (7, 0), (1, 2)]

        @on("sp")
        def _(sp, o):
            for j, (s1, s2) in enumerate(F0_SLOTS):
                load_pair(sp, A["L0_ffn_w1"], A["L0_ffn_w2"], 2 * j, s1, s2)
                ring.last[s1] = (f"f0h{2 * j + 1}{FC - 1}",)
                ring.last[s2] = (f"f0e{2 * j + 1}{NT - 1}",)
            for b in range(UNROLL):
                sp.wait_ge(w_landed[b], 16 * (ET // UNROLL))
            sp.wait_ge(rank_read, ET)
            sp.wait_ge(hot_used, 2 * ET + RB)
            for t in range(NT):
                sp.dma_start(wm[:, t, :], tab_w.rearrange("(t p j) h -> t p (j h)", t=NT, p=P)[t]).then_inc(w_loaded[t], 16)

        @on("pe")
        def _(pe, o):
            pe.wait_ge(xn_ready, NORM["f0"] + 1)
            pe_transpose(pe, "f0x", xn)
            for c in range(KC):
                banks.drained(pe, f"f0x{c}")
            pe_logits(pe, "f0g", xT, wg0, E0)
            pe.wait_ge(xn_ready, NORM["f0b"] + 1)
            pe_transpose(pe, "f0y", xn2)
            for c in range(KC):
                banks.drained(pe, f"f0y{c}")
            for e in range(E0 + 1):
                if e < E0:
                    pe_expert_up(pe, "f0", e, xT2, F0_SLOTS[e // 2][0])
                if e >= 1:
                    pe_expert_down(pe, "f0", e - 1, F0_SLOTS[(e - 1) // 2][1])

        @on("act")
        def _(act, o):
            act_norm(act, NORM["f0"])
            act_transposed(act, "f0x", xT)
            act_norm(act, NORM["f0b"])
            for c in range(KC):
                b = banks.filled(act, f"f0y{c}")
                nc.scalar.activation(xT2[:, c, :], b[:, 0:N], ACT.Copy, scale=c_g0[:, c:c + 1]).then_inc(
                    banks.free_of(f"f0y{c}"), 1)
            act_softmax_logits(act, "f0g", E0)
            for e in range(E0):
                act_expert(act, "f0", e, ACT.Gelu)

        @on("dve")
        def _(dve, od):
            dve_norm(dve, od, NORM["f0"], x, xn)
            dve.wait_ge(xn_ready, NORM["f0"] + 1)
            dve_norm(dve, od, NORM["f0b"], xn, xn2)
            dve_softmax_logits(dve, od, "f0g", E0, 0)
            pr, one, wo1, comb = g3(0, E0), g3(4, E0), g3(5, E0), g3(6, E0)
            g1, g2 = gate[:, 1, 24:24 + NT], gate[:, 1, 32:32 + NT]
            dve_top1(od, pr, E0, g1, one, g3(2, E0))
            od.link(nc.vector.tensor_scalar(wo1, one, -1.0, 1.0, ALU.mult, ALU.add))
            od.link(nc.vector.tensor_tensor(wo1, wo1, pr, ALU.mult))
            od.link(nc.vector.tensor_reduce(g2, wo1, AX, ALU.max))
            od.link(nc.vector.scalar_tensor_tensor(out=g2, in0=g2, scalar=1e-9, in1=g1, op0=ALU.add, op1=ALU.add))
            od.link(nc.vector.reciprocal(g2, g2))
            od.link(nc.vector.tensor_tensor(g1, g1, g2, ALU.mult))
            od.link(nc.vector.tensor_tensor(comb, one, g1.unsqueeze(2).broadcast_to([P, NT, E0]), ALU.mult))
            od.link(nc.vector.memset(acc[:], 0.0))
            for e in range(E0):
                dve_expert(dve, "f0", e, lambda t: comb[:, t, e:e + 1])
            for t in range(NT):
                banks.drained(dve, f"f0e{E0 - 1}{t}")
            od.link(nc.vector.tensor_tensor(x[:], x[:], acc[:], ALU.add))

        BLK, CDIM = A["L1_gnn_s1_w"].shape[0], A["L1_gnn_s1_w"].shape[1]
        NF = A["L1_gnn_f_w1"].shape[0] // 2
        HA = D // P
        TWO_PI_HI, TWO_PI_MID = 6.28125, 0.0019353071795864769
        ROUND = 12582912.0
        noise = view(11400, N)
        ph = view(11800, N)
        turns = view(12200, N)
        condT = view(0, N)
        mod = view(N, 2, N)
        qT = view(3 * N, HA, N)
        kT = view(3 * N + 1536, HA, N)
        vrow = view(3 * N + 3072, NT, D)
        modw = view(3 * N + 4608, 4, D)
        oT = qT
        blk_rows = ring.slot(SLOTS - 1)
        blk_in = sem("blk_in")
        noise_in = sem("noise_in")
        L1W = ("wq", "wk", "wv", "wo", "m_w1", "m_w2")

        def block_of(name, i):
            a = A["L1_gnn_" + name]
            return a[i] if isinstance(i, int) else a[bass.ds(i, 1)].rearrange("a k n -> (a k) n")

        def load_block_rows(sp, i):
            for j, nm in enumerate(("s1_w", "b1_w", "s2_w", "b2_w")):
                sp.dma_start(modw[0:CDIM, j, :], block_of(nm, i)).then_inc(blk_in, 16)
            for j, nm in enumerate(("bv", "bo", "m_b2")):
                a = A["L1_gnn_" + nm]
                row = a[i] if isinstance(i, int) else a[bass.ds(i, 1), :].rearrange("a n -> (a n)")
                sp.dma_start(blk_rows[:, j, :], row.partition_broadcast(P)).then_inc(blk_in, 16)

        L1_LAST = ("l1q3", "l1k3", "l1v2", "l1w2", "l1u3", "l1d2")

        @on("sp")
        def _(sp, o):
            sp.wait_ge(xn_ready, NORM["f0"] + 1)
            sp.dma_start(noise[0:2 * NF, :], A["node_vec1"].rearrange("n a -> (a n)").partition_broadcast(2 * NF)).then_inc(noise_in, 16)
            for s, nm in enumerate(L1W):
                ring.load(sp, banks, s, [(ring.slot(s), block_of(nm, 0).rearrange("(c p) n -> p c n", p=P))])
            sp.wait_ge(xn_ready, NORM["l1"] + 1)
            load_block_rows(sp, 0)
            with sp.Fori(0, BLK - 1) as i:
                for s, nm in enumerate(L1W):
                    ring.load(sp, banks, s, [(ring.slot(s), block_of(nm, i + 1).rearrange("(c p) n -> p c n", p=P))],
                              used=(L1_LAST[s], i))
                banks.drained(sp, "l1d2", i)
                load_block_rows(sp, i + 1)
            for s in range(6):
                ring.last[s] = (L1_LAST[s], BLK - 1)

        @on("pe")
        def _(pe, o):
            pe.wait_ge(pe_col, 1)
            b = banks.open(pe, "cond1")
            mm(b[0:CDIM, 0:N], fw1, ph[0:2 * NF, :], True, True).then_inc(banks.full_of("cond1"), 1)
            banks.drained(pe, "cond1")
            b = banks.open(pe, "cond2")
            mm(b[0:CDIM, 0:N], fw2, turns[0:CDIM, :], True, True).then_inc(banks.full_of("cond2"), 1)
            banks.drained(pe, "cond2")

            def modulated(k, i):
                def scale_bias(c):
                    for j, nm in ((2 * k, f"l1s{k}{c}"), (2 * k + 1, f"l1b{k}{c}")):
                        b = banks.open(pe, nm, i)
                        mm(b[:, 0:N], modw[0:CDIM, j, c * P:(c + 1) * P], condT[0:CDIM, :], True, True).then_inc(
                            banks.full_of(nm), 1)

                for c in range(KC - 1):
                    scale_bias(c)
                pe.wait_ge(xn_ready, NORM["blk"] + 2 * i + k + 1)
                for c in range(KC):
                    if c == KC - 1:
                        scale_bias(c)
                    b = banks.open(pe, f"l1x{k}{c}", i)
                    for t in range(NT):
                        last = nc.tensor.transpose(b[:, t * P:(t + 1) * P], xn[:, t, c * P:(c + 1) * P], ident[:])
                    last.then_inc(banks.full_of(f"l1x{k}{c}"), 1)
                for c in range(KC):
                    banks.drained(pe, f"l1b{k}{c}", i)

            def head_scores(h, i):
                for t in range(NT):
                    b = banks.open(pe, f"l1h{h}s{t}", i)
                    mm(b[:, 0:N], qT[:, h, t * P:(t + 1) * P], kT[:, h, :], True, True).then_inc(
                        banks.full_of(f"l1h{h}s{t}"), 1)

            def head_values(h, i):
                pe_att_transpose(pe, f"l1h{h}", HA * i + h, h % 3, i)
                for c in range(NT):
                    banks.drained(pe, f"l1h{h}p{c}", i)
                b = banks.open(pe, f"l1o{h}", i)
                for c in range(NT):
                    last = mm(b[:, 0:N], vrow[:, c, h * P:(h + 1) * P], probsT[:, h % 2, c, :], c == 0, c == NT - 1)
                last.then_inc(banks.full_of(f"l1o{h}"), 1)

            with banks.loop(BLK, 73), pe.Fori(0, BLK) as i:
                pe.wait_ge(blk_in, 16 * 7 * (i + 1))
                modulated(0, i)
                for s, nm in ((0, "q"), (1, "k")):
                    w = ring.get(pe, s, i)
                    for h in range(HA):
                        pe_cols(pe, f"l1{nm}{h}", xT, w, h * P, i)
                for h in range(HA):
                    banks.drained(pe, f"l1q{h}", i)
                    banks.drained(pe, f"l1k{h}", i)
                head_scores(0, i)
                w = ring.get(pe, 2, i)
                for t in range(NT):
                    pe_rows(pe, f"l1v{t}", xT, w, t, None, i)
                head_scores(1, i)
                for h in range(1, HA + 1):
                    if h + 1 < HA:
                        head_scores(h + 1, i)
                    if h == 1:
                        for t in range(NT):
                            banks.drained(pe, f"l1v{t}", i)
                    if h >= 1:
                        head_values(h - 1, i)
                banks.all_drained(pe, [f"l1o{h}" for h in range(HA)], i)
                w = ring.get(pe, 3, i)
                for t in range(NT):
                    pe_rows(pe, f"l1w{t}", oT, w, t, None, i)
                modulated(1, i)
                w = ring.get(pe, 4, i)
                for c in range(KC):
                    pe_cols(pe, f"l1u{c}", xT, w, c * P, i)
                for c in range(KC):
                    banks.drained(pe, f"l1u{c}", i)
                w = ring.get(pe, 5, i)
                for t in range(NT):
                    pe_rows(pe, f"l1d{t}", kT, w, t, None, i)
            ring.after_loop(range(6), BLK)

        @on("act")
        def _(act, o):
            act.wait_ge(step_ready, 2)
            nc.scalar.activation(ph[0:2 * NF, :], ph[0:2 * NF, :], ACT.Sin).then_inc(pe_col, 1)
            b = banks.filled(act, "cond1")
            nc.scalar.activation(turns[0:CDIM, :], b[0:CDIM, 0:N], ACT.Silu, bias=c_fb1).then_inc(banks.free_of("cond1"), 1)
            b = banks.filled(act, "cond2")
            nc.scalar.activation(condT[0:CDIM, :], b[0:CDIM, 0:N], ACT.Identity, bias=c_fb2).then_inc(banks.free_of("cond2"), 1)
            act_norm(act, NORM["l1"])

            def biased(name, dst, table, c, i, func=ACT.Identity):
                b = banks.filled(act, name, i)
                nc.scalar.activation(dst, b[:, 0:N], func, bias=table[:, bass.ds(KC * i + c, 1)]).then_inc(
                    banks.free_of(name), 1)

            with act.Fori(0, BLK) as i:
                for k, table in ((0, c_s1b), (1, c_s2b)):
                    if k == 0:
                        act_norm(act, NORM["blk"] + 2 * i)
                    for c in range(KC):
                        if c >= 2:
                            banks.drained(act, f"l1x{k}{c - 2}", i)
                        biased(f"l1s{k}{c}", mod[:, c % 2, :], table, c, i)
                    if k == 0:
                        for nm, dst, tb in (("q", qT, c_bq), ("k", kT, c_bk)):
                            for h in range(HA):
                                biased(f"l1{nm}{h}", dst[:, h, :], tb, h, i)
                        for h in range(HA + 2):
                            if h < HA:
                                act_att_exp(act, HA * i + h, h % 3)
                            if h >= 2:
                                act_att_transposed(act, f"l1h{h - 2}", (h - 2) % 2, i)
                                act_copy(act, f"l1o{h - 2}", oT[:, h - 2, :], N, i)
                        act_norm(act, NORM["blk"] + 2 * i + 1)
                    else:
                        for c in range(KC):
                            biased(f"l1u{c}", kT[:, c, :], c_mb1, c, i, ACT.Relu)

        @on("dve")
        def _(dve, od):
            nc.vector.tensor_scalar(mask_src[:], cnt_src[:], 0.5, MASKED, ALU.is_lt, ALU.mult)
            nc.vector.tensor_scalar(mask_dst[:], cnt_dst[:], 0.5, MASKED, ALU.is_lt, ALU.mult)
            dve.wait_ge(noise_in, 16)
            dve.wait_ge(consts_ready, 2)
            fr = gate[0:2 * NF, 7, 0:1]
            od.link(nc.vector.tensor_scalar(fr, fr, float(2.0 * 3.141592653589793 / 16), None, ALU.mult))
            z, tn = ph[0:2 * NF, :], turns[0:2 * NF, :]
            od.link(nc.vector.tensor_scalar(z, noise[0:2 * NF, :], fr, None, ALU.mult))
            od.link(nc.vector.tensor_scalar(tn, z, 0.15915494309189535, ROUND, ALU.mult, ALU.add))
            od.link(nc.vector.tensor_scalar(tn, tn, -ROUND, None, ALU.add))
            od.link(nc.vector.scalar_tensor_tensor(out=z, in0=tn, scalar=-TWO_PI_HI, in1=z, op0=ALU.mult, op1=ALU.add))
            od.link(nc.vector.scalar_tensor_tensor(out=z, in0=tn, scalar=-TWO_PI_MID, in1=z, op0=ALU.mult, op1=ALU.add))
            od.link(nc.vector.tensor_scalar(z, z, 3.1415925, -3.1415925, ALU.min, ALU.max))
            zc = ph[NF:2 * NF, :]
            od.link(nc.vector.scalar_tensor_tensor(out=zc, in0=zc, scalar=-1.0, in1=zc, op0=ALU.mult, op1=ALU.max))
            nc.vector.tensor_scalar(zc, zc, -1.0, 1.5707963267948966, ALU.mult, ALU.add).then_inc(step_ready, 1)
            for tb in (c_s1b, c_s2b):
                od.link(nc.vector.tensor_scalar(tb, tb, 1.0, None, ALU.add))
            dve_norm(dve, od, NORM["l1"], x, xn2)
            dve.wait_ge(xn_ready, NORM["l1"] + 1)

            def modulated(k, table, i):
                for c in range(KC):
                    banks.drained(dve, f"l1s{k}{c}", i)
                    b = banks.filled(dve, f"l1x{k}{c}", i)
                    nc.vector.tensor_tensor(xT[:, c, :], b[:, 0:N], mod[:, c % 2, :], ALU.mult).then_inc(
                        banks.free_of(f"l1x{k}{c}"), 1)
                    banks.drained(dve, f"l1x{k}{c}", i)
                    b = banks.filled(dve, f"l1b{k}{c}", i)
                    nc.vector.scalar_tensor_tensor(out=xT[:, c, :], in0=b[:, 0:N], scalar=table[:, bass.ds(KC * i + c, 1)],
                                                   in1=xT[:, c, :], op0=ALU.add, op1=ALU.add).then_inc(
                        banks.free_of(f"l1b{k}{c}"), 1)

            def add_bias(j):
                for t in range(NT):
                    last = nc.vector.tensor_tensor(xn2[:, t, :], xn2[:, t, :], blk_rows[:, j, :], ALU.add)
                od.link(last)

            def biased_rows(tag, dst, bias, i):
                for t in range(NT):
                    b = banks.filled(dve, f"{tag}{t}", i)
                    nc.vector.tensor_tensor(dst[:, t, :], b, bias, ALU.add).then_inc(banks.free_of(f"{tag}{t}"), 1)

            def measure():
                for t in range(NT):
                    last = nc.vector.bn_stats(stats[:, t, :], xn2[:, t, :])
                od.link(last)

            def add_rows(tag, i):
                for t in range(NT):
                    b = banks.filled(dve, f"{tag}{t}", i)
                    nc.vector.tensor_tensor(xn2[:, t, :], xn2[:, t, :], b, ALU.add).then_inc(banks.free_of(f"{tag}{t}"), 1)
                    banks.drained(dve, f"{tag}{t}", i)
                    last = nc.vector.bn_stats(stats[:, t, :], xn2[:, t, :])
                od.link(last)

            measure()
            with od.loop(BLK, 24) as i:
                dve_norm(dve, od, NORM["blk"] + 2 * i, xn2, xn, measured=True)
                modulated(0, c_b1b, i)
                dve.wait_ge(blk_in, 16 * 7 * (i + 1))
                add_bias(1)
                for h in range(HA + 1):
                    if h < HA:
                        dve_att_scores(dve, od, f"l1h{h}", h % 3, float(P) ** -0.5, mask_src, i)
                    if h != 1:
                        g = max(h - 1, 0)
                        dve_att_probs(dve, od, HA * i + g, g % 3, cnt_src)
                    if h == 0:
                        biased_rows("l1v", vrow, blk_rows[:, 0, :], i)
                add_rows("l1w", i)
                dve_norm(dve, od, NORM["blk"] + 2 * i + 1, xn2, xn, measured=True)
                modulated(1, c_b2b, i)
                add_bias(2)
                add_rows("l1d", i)
            od.link(nc.vector.tensor_tensor(x[:], x[:], xn2[:], ALU.add))

        @on("pool")
        def _(pool, op):
            fr = gate[0:2 * NF, 7, 0:1]
            nc.gpsimd.iota(fr[0:NF, :], pattern=[[0, 1]], base=1, channel_multiplier=1, allow_small_or_imprecise_dtypes=True)
            nc.gpsimd.iota(gate[NF:2 * NF, 7, 0:1], pattern=[[0, 1]], base=1, channel_multiplier=1,
                           allow_small_or_imprecise_dtypes=True).then_inc(consts_ready, 1)
            pool.wait_ge(pos_ready, 1)
            pool.wait_ge(consts_ready, 2)

            def store_records(t):
                op.link(nc.gpsimd.tensor_copy(rec_row[:], rec[:, bass.ds(t, 1), :].rearrange("p a k -> p (a k)")))
                op.link(nc.gpsimd.tensor_copy(pos_col[:], pos[:, bass.ds(t, 1)]))
                pool.nop(nofuse=True)
                nc.gpsimd.indirect_dma_start(tab_sorted, bass.IndirectOffsetOnAxis(ap=pos_col[:].bitcast(U32), axis=0),
                                             rec_row[:], None).then_inc(records_landed, 16)

            store_records(0)
            with op.loop(ET - 1, 2) as i:
                pool.wait_ge(records_landed, 16 * (i + 1))
                store_records(i + 1)

        HALF = E1 // 2

        @on("sp")
        def _(sp, o):
            sp.wait_ge(records_landed, 16 * ET)
            sp.dma_start(rec[:], tab_sorted.rearrange("(p t) k -> p t k", p=P)).then_inc(sorted_loaded, 16)
            for i in range(2):
                for j in range(HALF // 2):
                    if i == 0 and j == HALF // 2 - 1:
                        banks.drained(sp, "l1d2", BLK - 1)
                    load_pair(sp, A["L1_ffn_w1"], A["L1_ffn_w2"], HALF * i + 2 * j, 2 * j, 2 * j + 1)
                    ring.last[2 * j] = (f"f1h{2 * j + 1}{FC - 1}", i)
                    ring.last[2 * j + 1] = (f"f1e{2 * j + 1}{NT - 1}", i)

        @on("pe")
        def _(pe, o):
            pe.wait_ge(xn_ready, NORM["f1"] + 1)
            pe_transpose(pe, "f1x", xn)
            for c in range(KC):
                banks.drained(pe, f"f1x{c}")
            pe_logits(pe, "f1g", xT, wg1, E1)

            def before(name, mask, total):
                b = banks.open(pe, name)
                for t in range(NT):
                    ks = range(NT) if total else range(t + 1)
                    for k in ks:
                        last = mm(b[:, t * E1:(t + 1) * E1], tri[:] if k == t and not total else ones[:], mask[:, k, :],
                                  k == 0, k == ks[-1])
                last.then_inc(banks.full_of(name), 1)

            pe.wait_ge(step_ready, 3)
            before("f1p1", g3(4, E1), False)
            before("f1p2", g3(5, E1), False)
            pe.wait_ge(step_ready, 4)
            before("f1n1", g3(4, E1), True)
            with banks.loop(2, HALF * (FC + NT)), pe.Fori(0, 2) as i:
                for e in range(HALF + 1):
                    if e < HALF:
                        pe_expert_up(pe, "f1", e, xT, e // 2 * 2, i)
                    if e >= 1:
                        pe_expert_down(pe, "f1", e - 1, (e - 1) // 2 * 2 + 1, i)
            ring.after_loop(range(8), 2)

        @on("act")
        def _(act, o):
            act_norm(act, NORM["f1"])
            act_transposed(act, "f1x", xT)
            act_softmax_logits(act, "f1g", E1)
            with act.Fori(0, 2) as i:
                for e in range(HALF):
                    act_expert(act, "f1", e, ACT.Relu, i)

        @on("dve")
        def _(dve, od):
            dve_norm(dve, od, NORM["f1"], x, xn)
            dve_softmax_logits(dve, od, "f1g", E1, 1)
            pr, m1, m2, rest, tmp = g3(0, E1), g3(4, E1), g3(5, E1), g3(6, E1), g3(2, E1)
            g1, g2, dn = gate[:, 1, 24:24 + NT], gate[:, 1, 32:32 + NT], gate[:, 1, 40:40 + NT]
            dve_top1(od, pr, E1, g1, m1, tmp)
            od.link(nc.vector.tensor_scalar(rest, m1, -1.0, 1.0, ALU.mult, ALU.add))
            od.link(nc.vector.tensor_tensor(rest, rest, pr, ALU.mult))
            dve_top1(od, rest, E1, g2, m2, tmp)
            nc.vector.memset(gate[:, 15, 4:5], 0.0).then_inc(step_ready, 1)
            od.link(nc.vector.scalar_tensor_tensor(out=dn, in0=g1, scalar=1e-9, in1=g2, op0=ALU.add, op1=ALU.add))
            od.link(nc.vector.reciprocal(dn, dn))
            nc.vector.tensor_tensor(g1, g1, dn, ALU.mult)
            od.link(nc.vector.tensor_tensor(g2, g2, dn, ALU.mult))

            def bank3(name):
                return banks.filled(dve, name)[:, 0:NT * E1].rearrange("p (t e) -> p t e", t=NT)

            p1, p2 = g3(8, E1), g3(9, E1)
            nc.vector.tensor_scalar(p1, bank3("f1p1"), float(CAP1), None, ALU.is_lt).then_inc(banks.free_of("f1p1"), 1)
            nc.vector.tensor_copy(p2, bank3("f1p2")).then_inc(banks.free_of("f1p2"), 1)
            banks.drained(dve, "f1p2")
            od.link(nc.vector.tensor_tensor(m1, m1, p1, ALU.mult))
            nc.vector.memset(gate[:, 15, 4:5], 0.0).then_inc(step_ready, 1)
            nc.vector.tensor_tensor(p2, p2, bank3("f1n1"), ALU.add).then_inc(banks.free_of("f1n1"), 1)
            banks.drained(dve, "f1n1")
            od.link(nc.vector.tensor_scalar(p2, p2, float(CAP1), None, ALU.is_lt))
            od.link(nc.vector.tensor_tensor(m2, m2, p2, ALU.mult))
            nc.vector.tensor_tensor(m1, m1, g1.unsqueeze(2).broadcast_to([P, NT, E1]), ALU.mult)
            od.link(nc.vector.tensor_tensor(m2, m2, g2.unsqueeze(2).broadcast_to([P, NT, E1]), ALU.mult))
            od.link(nc.vector.tensor_tensor(m1, m1, m2, ALU.add))
            od.link(nc.vector.memset(acc[:], 0.0))
            with dve.Fori(0, 2) as i:
                for e in range(HALF):
                    dve_expert(dve, "f1", e, lambda t: m1[:, t, bass.ds(HALF * i + e, 1)], i)
                for t in range(NT):
                    banks.drained(dve, f"f1e{HALF - 1}{t}", i)
            for t in range(NT):
                banks.drained(dve, f"f1e{HALF - 1}{t}", 1)
            od.link(nc.vector.tensor_tensor(x[:], x[:], acc[:], ALU.add))

        hrows = view(0, NT, D)
        prod = view(NT * D, NT, D)
        wT = view(2 * NT * D, KC, D)
        GT = 4
        GU = 8
        node_hot = arena[:, 5120:8192].bitcast(BF16).rearrange("p (b f c e) -> p b f c e", b=2, f=2, c=NT)
        key_rows = arena[:, 8192:9216].bitcast(F16).rearrange("p (b f e) -> p b f e", b=2, f=2)
        w_edge = view(9216, ET, H8)
        fac = view(10336, ET, H8)
        ends_n = view(11104, 2, NT, H8)
        parts = arena[:, 11152:11152 + 3 * NT * H8].bitcast(BF16).rearrange("p (f c k h) -> p f c k h", f=2, c=NT, k=3)
        left = view(11232, 2, NT, H8)
        type_is = view(11300, ET)
        key_cols = view(11400, 2, 2, GT)
        whole_max = view(11424, 2, H8)
        run = view(11460, ET)
        sel8 = view(11600, ET, H8)
        top = view(12368, ET, H8)
        lane_mask = view(3584, 2, 2 * P)
        lane_max = view(NT * D, H8, 2 * P)
        weight = sel8
        BEFORE = 16 * (ET // ZB)
        TYPES = A["L2_gnn_et_emb"].shape[0]

        @on("sp")
        def _(sp, o):
            ring.load(sp, banks, 0, [(ring.slot(0), A["L2_gnn_W"].rearrange("(c p) n -> p c n", p=P))])
            ring.last[0] = ("l2t3",)
            sp.wait_ge(step_ready, 5)
            sp.dma_start(tiled(tab_h), hrows[:]).then_inc(tables_stored, 16)

        def pe_weight_transpose(pe, tag, w, i=None):
            for c in range(KC):
                b = banks.open(pe, f"{tag}{c}", i)
                for q in range(KC):
                    last = nc.tensor.transpose(b[:, q * P:(q + 1) * P], w[:, q, c * P:(c + 1) * P], ident[:])
                last.then_inc(banks.full_of(f"{tag}{c}"), 1)

        @on("pe")
        def _(pe, o):
            pe_weight_transpose(pe, "l2t", ring.get(pe, 0))
            pe.wait_ge(xn_ready, NORM["l2"] + 1)
            pe_transpose(pe, "l2x", xn)
            for c in range(KC):
                banks.drained(pe, f"l2t{c}")
                banks.drained(pe, f"l2x{c}")
            for t in range(NT):
                pe_rows(pe, f"l2r{t}", xT, wT, t)
            pe.wait_ge(step_ready, 5)
            with banks.loop(ET // GT // GU, 3 * GU), pe.Fori(0, ET // GT // GU) as i:
                for k in range(GU + 1):
                    if k < GU:
                        pe.wait_ge(cols_ready, GU * i + k + 1)
                        for f in range(2):
                            b = banks.open(pe, f"l2b{k}{f}", i)
                            for j in range(GT):
                                last = mm(b[:, j * P:(j + 1) * P], key_cols[:, k % 2, f, j:j + 1].broadcast_to([P, P]), ident[:],
                                          True, True)
                            last.then_inc(banks.full_of(f"l2b{k}{f}"), 1)
                    if k >= 1:
                        g = k - 1
                        pe.wait_ge(nodes_ready, GU * i + g + 1)
                        b = banks.open(pe, f"l2e{g}", i)
                        for j in range(GT):
                            for f in range(2):
                                for c in range(NT):
                                    last = mm(b[:, j * 3 * H8:(j + 1) * 3 * H8], node_hot[:, g % 2, f, c, j * P:(j + 1) * P],
                                              parts[:, f, c, :, :].rearrange("p k h -> p (k h)"), f + c == 0, f + c == NT)
                        last.then_inc(banks.full_of(f"l2e{g}"), 1)
            pe.wait_ge(lanes_ready, 1)
            b = banks.open(pe, "l2n")
            for s, t in enumerate((0, ET - 1)):
                last = mm(b[:, s * P:(s + 1) * P], rec[:, t, 1:2].broadcast_to([P, P]), ident[:], True, True)
            last.then_inc(banks.full_of("l2n"), 1)
            for s, t in enumerate((0, ET - 1)):
                for hf in range(2):
                    b = banks.open(pe, f"l2m{s}{hf}")
                    for h in range(4):
                        last = mm(b[:, h * P:(h + 1) * P], top[:, t, 4 * hf + h:4 * hf + h + 1].broadcast_to([P, P]), ident[:],
                                  True, True)
                    last.then_inc(banks.full_of(f"l2m{s}{hf}"), 1)
            pe_scatter_rows(pe, "l2")

        @on("act")
        def _(act, o):
            act.wait_ge(var_ready, NORM["l2"] + 1)
            for c in range(KC):
                act_copy(act, f"l2t{c}", wT[:, c, :])
            act_norm(act, NORM["l2"])
            act_transposed(act, "l2x", xT)
            for t in range(NT):
                act_copy(act, f"l2r{t}", hrows[:, t, :])
            with act.Fori(0, ET // GT // GU) as i:
                for k in range(GU):
                    for f in range(2):
                        b = banks.filled(act, f"l2b{k}{f}", i)
                        nc.scalar.activation(key_rows[:, k % 2, f, :], b, ACT.Copy).then_inc(banks.free_of(f"l2b{k}{f}"), 1)
            act.wait_ge(diff_ready, 1)
            nc.scalar.activation(weight[:], weight[:], ACT.Exp).then_inc(ex_done, 1)
            act_norm(act, NORM["l2b"])

        @on("pool")
        def _(pool, op):
            pool.wait_ge(sorted_loaded, 16)
            pool.wait_ge(step_ready, 4)
            et3 = et_bc.rearrange("p (y h) -> p y h", h=H8)
            op.link(nc.gpsimd.memset(fac[:], 1.0))
            for y in range(TYPES):
                op.link(nc.gpsimd.tensor_scalar(type_is, typ_f, float(y), None, ALU.is_equal))
                op.link(nc.gpsimd.tensor_tensor(sel8[:], type_is.unsqueeze(2).broadcast_to([P, ET, H8]),
                                                et3[:, y:y + 1, :].broadcast_to([P, ET, H8]), ALU.mult))
                op.link(nc.gpsimd.tensor_tensor(fac[:], fac[:], sel8[:], ALU.add))
            nc.gpsimd.tensor_tensor(fac[:], fac[:], ew.unsqueeze(2).broadcast_to([P, ET, H8]), ALU.mult).then_inc(factor_ready, 1)
            pool.wait_ge(tables_stored, 48)
            pool_scatter_rows(pool, op, tab_h)

        @on("dve")
        def _(dve, od):
            dve_norm(dve, od, NORM["l2"], x, xn)
            for t in range(NT):
                banks.drained(dve, f"l2r{t}")
            for f, nm in enumerate(("L2_gnn_a_src", "L2_gnn_a_dst")):
                for t in range(NT):
                    last = nc.vector.tensor_tensor(prod[:, t, :], hrows[:, t, :], BC[nm], ALU.mult)
                od.link(last)
                od.link(nc.vector.tensor_reduce(ends_n[:, f, :, :].rearrange("p c h -> p (c h)"),
                                                prod[:].rearrange("p c (h d) -> p (c h) d", d=HD), AX, ALU.add))
            od.link(nc.vector.tensor_copy(left[:], ends_n[:]))
            for k in range(3):
                od.link(nc.vector.tensor_copy(parts[:, :, :, k, :], left[:]))
                if k < 2:
                    od.link(nc.vector.tensor_tensor(left[:], left[:], parts[:, :, :, k, :], ALU.subtract))
            nc.vector.memset(gate[:, 15, 5:6], 0.0).then_inc(step_ready, 1)
            dve.wait_ge(sorted_loaded, 16)
            nc.vector.tensor_copy(sd_i[:, :, 0], src_f)
            nc.vector.tensor_tensor(run[:, 1:ET], dst_f[:, 1:ET], dst_f[:, 0:ET - 1], ALU.not_equal)
            od.link(nc.vector.memset(run[:, 0:1], 1.0))
            od.link(nc.vector.tensor_scalar(run, run, MASKED, None, ALU.mult))
            with dve.Fori(0, ET // GT // GU) as i:
                for k in range(GU + 2):
                    if k < GU:
                        nc.vector.tensor_copy(key_cols[:, k % 2, :, :],
                                              rec[:, bass.ds(GT * (GU * i + k), GT), 0:2].rearrange("p t f -> p f t")).then_inc(
                            cols_ready, 1)
                    if 1 <= k <= GU:
                        g = k - 1
                        for f in range(2):
                            banks.drained(dve, f"l2b{g}{f}", i)
                            for c in range(NT):
                                last = nc.vector.tensor_scalar(node_hot[:, g % 2, f, c, :], key_rows[:, g % 2, f, :],
                                                               node_id[:, c:c + 1], None, ALU.is_equal)
                        last.then_inc(nodes_ready, 1)
                    if k >= 2:
                        g = k - 2
                        b = banks.filled(dve, f"l2e{g}", i)
                        nc.vector.tensor_reduce(w_edge[:, bass.ds(GT * (GU * i + g), GT), :],
                                                b[:, 0:GT * 3 * H8].rearrange("p (t k h) -> p t h k", t=GT, k=3), AX,
                                                ALU.add).then_inc(banks.free_of(f"l2e{g}"), 1)
            for g in range(GU):
                banks.drained(dve, f"l2e{g}", ET // GT // GU - 1)
            od.link(nc.vector.scalar_tensor_tensor(out=w_edge[:], in0=w_edge[:], scalar=0.2, in1=w_edge[:], op0=ALU.mult, op1=ALU.max))
            dve.wait_ge(factor_ready, 1)
            od.link(nc.vector.tensor_tensor(w_edge[:], w_edge[:], fac[:], ALU.mult))
            for h in range(H8):
                last = nc.vector.tensor_tensor_scan(top[:, :, h], run, w_edge[:, :, h], MASKED, ALU.add, ALU.max)
            od.link(last)
            step = 1
            while step < ET:
                keep = run[:, 0:ET - step]
                od.link(nc.vector.tensor_tensor(keep, dst_f[:, 0:ET - step], dst_f[:, step:ET], ALU.not_equal))
                od.link(nc.vector.tensor_scalar(keep, keep, MASKED, None, ALU.mult))
                od.link(nc.vector.tensor_tensor(sel8[:, 0:ET - step, :], top[:, step:ET, :],
                                                keep.unsqueeze(2).broadcast_to([P, ET - step, H8]), ALU.add))
                od.link(nc.vector.tensor_tensor(top[:, 0:ET - step, :], top[:, 0:ET - step, :], sel8[:, 0:ET - step, :], ALU.max))
                step *= 2
            nc.vector.memset(gate[:, 15, 0:1], 0.0).then_inc(lanes_ready, 1)
            b = banks.filled(dve, "l2n")
            for s, t in enumerate((0, ET - 1)):
                last = nc.vector.tensor_scalar(lane_mask[:, s, :], b[:, 0:2 * P], rec[:, t, 1:2], MASKED, ALU.not_equal, ALU.mult)
            last.then_inc(banks.free_of("l2n"), 1)
            banks.drained(dve, "l2n")
            for s, t in enumerate((0, ET - 1)):
                for q in range(2):
                    for hf in range(2):
                        b = banks.filled(dve, f"l2m{q}{hf}")
                        last = nc.vector.tensor_tensor(lane_max[:, 4 * hf:4 * hf + 4, q * P:(q + 1) * P],
                                                       b.rearrange("p (h l) -> p h l", h=4),
                                                       lane_mask[:, s, q * P:(q + 1) * P].unsqueeze(1).broadcast_to([P, 4, P]),
                                                       ALU.add)
                        if s == 1 and (q, hf) != (1, 1):
                            last.then_inc(banks.free_of(f"l2m{q}{hf}"), 1)
                if s == 1:
                    last.then_inc(banks.free_of("l2m11"), 1)
                    banks.drained(dve, "l2m11")
                else:
                    od.link(last)
                od.link(nc.vector.tensor_reduce(whole_max[:, s, :], lane_max[:], AX, ALU.max))
            for s, t in enumerate((0, ET - 1)):
                od.link(nc.vector.tensor_scalar(run, dst_f, rec[:, t, 1:2], MASKED, ALU.not_equal, ALU.mult))
                od.link(nc.vector.tensor_tensor(sel8[:], run.unsqueeze(2).broadcast_to([P, ET, H8]),
                                                whole_max[:, s:s + 1, :].broadcast_to([P, ET, H8]), ALU.add))
                od.link(nc.vector.scalar_tensor_tensor(out=top[:], in0=sel8[:], scalar=0.0, in1=top[:], op0=ALU.max, op1=ALU.max))
            nc.vector.tensor_tensor(weight[:], w_edge[:], top[:], ALU.subtract).then_inc(diff_ready, 1)
            nc.vector.memset(gate[:, 15, 2:3], 0.0).then_inc(msg_free, RB)
            dve.wait_ge(ex_done, 1)
            dve_scatter_rows(dve, od, dst_f, weight, BEFORE)
            dve_scatter_sums(dve, od, "l2", 1.0e-10, True)
            od.link(nc.vector.tensor_tensor(xn2[:], xn2[:], xn[:], ALU.add))
            dve_norm(dve, od, NORM["l2b"], xn2, xn2, BC["L2_gnn_ln_gamma"], BC["L2_gnn_ln_beta"])
            dve.wait_ge(xn_ready, NORM["l2b"] + 1)
            od.link(nc.vector.tensor_tensor(x[:], x[:], xn2[:], ALU.add))

        K2 = A["L2_ffn_expert_weights"].shape[0]
        wTs = [view(0, KC, D), view(KC * D, KC, D)]
        coefT = view(2 * KC * D, N)
        acc2 = view(2 * KC * D + N, NT, D)
        mixw = xT2[0:K2, :, :].rearrange("p c n -> p (c n)")[:, 0:D]
        mixb = xT2[0:K2, :, :].rearrange("p c n -> p (c n)")[:, D:2 * D]
        mix_in = sem("mix_in")
        Q2 = K2 // 2

        @on("sp")
        def _(sp, o):
            sp.dma_start(mixw, A["L2_ffn_mixer_w"]).then_inc(mix_in, 16)
            sp.dma_start(mixb, A["L2_ffn_expert_biases"]).then_inc(mix_in, 16)
            for i in range(2):
                for e in range(Q2):
                    s = e + 1
                    ring.load(sp, banks, s, [(ring.slot(s), A["L2_ffn_expert_weights"][Q2 * i + e].rearrange("(c p) n -> p c n", p=P))])
                    ring.last[s] = (f"f2t{e}{KC - 1}", i)

        @on("pe")
        def _(pe, o):
            pe.wait_ge(mix_in, 32)
            b = banks.open(pe, "f2m")
            for c in range(KC):
                last = nc.tensor.transpose(b[:, c * K2:(c + 1) * K2], mixw[:, c * P:(c + 1) * P], ident[0:K2, 0:K2])
            last.then_inc(banks.full_of("f2m"), 1)
            pe.wait_ge(xn_ready, NORM["f2"] + 1)
            pe_transpose(pe, "f2x", xn)
            banks.drained(pe, "f2m")
            for c in range(KC):
                banks.drained(pe, f"f2x{c}")
            pe_logits(pe, "f2g", xT, mixT, K2, r_mixb)
            pe.wait_ge(step_ready, 6)
            b = banks.open(pe, "f2c")
            for t in range(NT):
                last = nc.tensor.transpose(b[0:K2, t * P:(t + 1) * P], g3(0, K2)[:, t, :], ident[:])
            last.then_inc(banks.full_of("f2c"), 1)
            banks.drained(pe, "f2c")
            for t in range(NT):
                b = banks.open(pe, f"f2b{t}")
                mm(b, coefT[0:K2, t * P:(t + 1) * P], mixb, True, True).then_inc(banks.full_of(f"f2b{t}"), 1)
            with banks.loop(2, Q2 * (KC + NT)), pe.Fori(0, 2) as i:
                for e in range(Q2 + 1):
                    if e < Q2:
                        pe_weight_transpose(pe, f"f2t{e}", ring.get(pe, e + 1, i), i)
                    if e >= 1:
                        for c in range(KC):
                            banks.drained(pe, f"f2t{e - 1}{c}", i)
                        for t in range(NT):
                            pe_rows(pe, f"f2y{e - 1}{t}", xT, wTs[(e - 1) % 2], t, None, i)
            ring.after_loop(range(1, Q2 + 1), 2)

        @on("act")
        def _(act, o):
            act_copy(act, "f2m", small[:, 208:240], KC * K2)
            act_norm(act, NORM["f2"])
            act_transposed(act, "f2x", xT)
            act_softmax_logits(act, "f2g", K2)
            b = banks.filled(act, "f2c")
            nc.scalar.activation(coefT[0:K2, :], b[0:K2, 0:N], ACT.Copy).then_inc(banks.free_of("f2c"), 1)
            with act.Fori(0, 2) as i:
                for e in range(Q2):
                    for c in range(KC):
                        act_copy(act, f"f2t{e}{c}", wTs[e % 2][:, c, :], D, i)

        @on("dve")
        def _(dve, od):
            dve_norm(dve, od, NORM["f2"], x, xn)
            dve_softmax_logits(dve, od, "f2g", K2, 2)
            nc.vector.memset(gate[:, 15, 6:7], 0.0).then_inc(step_ready, 1)
            for t in range(NT):
                b = banks.filled(dve, f"f2b{t}")
                nc.vector.tensor_copy(acc2[:, t, :], b).then_inc(banks.free_of(f"f2b{t}"), 1)
            for t in range(NT):
                banks.drained(dve, f"f2b{t}")
            with dve.Fori(0, 2) as i:
                for e in range(Q2):
                    for t in range(NT):
                        name = f"f2y{e}{t}"
                        if e > 0:
                            banks.drained(dve, f"f2y{e - 1}{t}", i)
                        b = banks.filled(dve, name, i)
                        nc.vector.scalar_tensor_tensor(out=acc2[:, t, :], in0=b, scalar=g3(0, K2)[:, t, bass.ds(Q2 * i + e, 1)],
                                                       in1=acc2[:, t, :], op0=ALU.mult, op1=ALU.add).then_inc(
                            banks.free_of(name), 1)
                for t in range(NT):
                    banks.drained(dve, f"f2y{Q2 - 1}{t}", i)
            for t in range(NT):
                banks.drained(dve, f"f2y{Q2 - 1}{t}", 1)
            od.link(nc.vector.tensor_tensor(x[:], x[:], acc2[:], ALU.add))

        H3 = A["L3_gnn_Wq"].shape[1] // D
        U3 = BLK * HA
        q3, k3, v3, xa = view(0, KC, N), view(1536, KC, N), view(3072, NT, D), view(4608, KC, N)
        acc3 = view(6144, NT, D)
        row_in = sem("row_in")
        v_bias = xT2[:].rearrange("p c n -> p (c n)")[:, 0:D]

        def head_cols(name, i):
            return A["L3_gnn_" + name][:, bass.ds((H3 - 1 - i) * D, D)].rearrange("(c p) n -> p c n", p=P)

        L3W = (("Wq", 5, "l3q3"), ("Wk", 6, "l3k3"), ("Wv", 7, "l3v2"), ("Wskip", 0, "l3a3"), ("Wlin", 1, "l3l2"))

        def load_head(sp, i, before):
            for nm, s, job in L3W:
                src = (A["L3_gnn_Wlin"][bass.ds((H3 - 1 - i) * D, D), :].rearrange("(c p) n -> p c n", p=P) if nm == "Wlin"
                       else head_cols(nm, i))
                ring.load(sp, banks, s, [(ring.slot(s), src)], used=None if before is None else (job, before))
            if before is not None:
                banks.drained(sp, "l3v2", before)
                sp.nop(nofuse=True)
            else:
                banks.filled(sp, f"f2b{NT - 1}")
            sp.dma_start(v_bias, A["L3_gnn_bv"][bass.ds((H3 - 1 - i) * D, D)].partition_broadcast(P)).then_inc(row_in, 16)

        @on("sp")
        def _(sp, o):
            load_head(sp, 0, None)
            with sp.Fori(0, H3 - 1) as i:
                load_head(sp, i + 1, i)
            for nm, s, job in L3W:
                ring.last[s] = (job, H3 - 1)

        @on("pe")
        def _(pe, o):
            pe.wait_ge(xn_ready, NORM["l3"] + 1)
            pe_transpose(pe, "l3x", xn)
            for c in range(KC):
                banks.drained(pe, f"l3x{c}")
            with banks.loop(H3, 24), pe.Fori(0, H3) as i:
                for nm, s in (("q", 5), ("k", 6)):
                    w = ring.get(pe, s, i)
                    for c in range(KC):
                        pe_cols(pe, f"l3{nm}{c}", xT, w, c * P, i)
                for c in range(KC):
                    banks.drained(pe, f"l3q{c}", i)
                    banks.drained(pe, f"l3k{c}", i)
                for t in range(NT):
                    b = banks.open(pe, f"l3s{t}", i)
                    for c in range(KC):
                        last = mm(b[:, 0:N], q3[:, c, t * P:(t + 1) * P], k3[:, c, :], c == 0, c == KC - 1)
                    last.then_inc(banks.full_of(f"l3s{t}"), 1)
                w = ring.get(pe, 7, i)
                for t in range(NT):
                    pe_rows(pe, f"l3v{t}", xT, w, t, None, i)
                w = ring.get(pe, 0, i)
                bk = [banks.open(pe, f"l3a{d}", i) for d in range(KC)]
                for d in range(KC):
                    for c in range(KC):
                        mm(bk[d][:, 0:N], w[:, c, d * P:(d + 1) * P], xT[:, c, :], c == 0, False)
                pe_att_transpose(pe, "l3", U3 + i, 0, i)
                for t in range(NT):
                    banks.drained(pe, f"l3v{t}", i)
                for c in range(NT):
                    banks.drained(pe, f"l3p{c}", i)
                for d in range(KC):
                    for c in range(NT):
                        last = mm(bk[d][:, 0:N], v3[:, c, d * P:(d + 1) * P], probsT[:, 0, c, :], False, c == NT - 1)
                    last.then_inc(banks.full_of(f"l3a{d}"), 1)
                w = ring.get(pe, 1, i)
                for d in range(KC):
                    banks.drained(pe, f"l3a{d}", i)
                for t in range(NT):
                    pe_rows(pe, f"l3l{t}", xa, w, t, None, i)
            ring.after_loop((5, 6, 7, 0, 1), H3)
            for t in range(NT):
                b = banks.open(pe, f"l3f{t}")
                for c in range(KC):
                    last = nc.tensor.transpose(b[:, c * P:(c + 1) * P], xa[:, c, t * P:(t + 1) * P], ident[:])
                last.then_inc(banks.full_of(f"l3f{t}"), 1)

        @on("act")
        def _(act, o):
            act_norm(act, NORM["l3"])
            act_transposed(act, "l3x", xT)

            def biased(name, dst, table, c, i):
                b = banks.filled(act, name, i)
                nc.scalar.activation(dst, b[:, 0:N], ACT.Identity, bias=table[:, bass.ds((H3 - 1 - i) * KC + c, 1)]).then_inc(
                    banks.free_of(name), 1)

            with act.Fori(0, H3) as i:
                for c in range(KC):
                    biased(f"l3q{c}", q3[:, c, :], c_bq3, c, i)
                for c in range(KC):
                    biased(f"l3k{c}", k3[:, c, :], c_bk3, c, i)
                act_att_exp(act, U3 + i, 0)
                act_att_transposed(act, "l3", 0, i)
                for d in range(KC):
                    biased(f"l3a{d}", xa[:, d, :], c_bs3, d, i)
            act_norm(act, NORM["l3b"])

        @on("dve")
        def _(dve, od):
            dve_norm(dve, od, NORM["l3"], x, xn)
            for t in range(NT):
                last = nc.vector.tensor_copy(acc3[:, t, :], BC["L3_gnn_blin"])
            od.link(last)
            with od.loop(H3, 4) as i:
                dve_att_scores(dve, od, "l3", 0, float(D) ** -0.5, mask_dst, i)
                dve_att_probs(dve, od, U3 + i, 0, cnt_dst)
                dve.wait_ge(row_in, 16 * (i + 1))
                for t in range(NT):
                    b = banks.filled(dve, f"l3v{t}", i)
                    nc.vector.tensor_tensor(v3[:, t, :], b, v_bias, ALU.add).then_inc(banks.free_of(f"l3v{t}"), 1)
                for t in range(NT):
                    b = banks.filled(dve, f"l3l{t}", i)
                    nc.vector.tensor_tensor(acc3[:, t, :], acc3[:, t, :], b, ALU.add).then_inc(banks.free_of(f"l3l{t}"), 1)
                for t in range(NT):
                    banks.drained(dve, f"l3l{t}", i)
            for t in range(NT):
                banks.drained(dve, f"l3l{t}", H3 - 1)
                b = banks.filled(dve, f"l3f{t}")
                nc.vector.tensor_tensor(acc3[:, t, :], acc3[:, t, :], b, ALU.add).then_inc(banks.free_of(f"l3f{t}"), 1)
            for t in range(NT):
                banks.drained(dve, f"l3f{t}")
            dve_norm(dve, od, NORM["l3b"], acc3, acc3, BC["L3_gnn_gamma"], BC["L3_gnn_beta"])
            dve.wait_ge(xn_ready, NORM["l3b"] + 1)
            od.link(nc.vector.tensor_tensor(x[:], x[:], acc3[:], ALU.add))

        OPTS = 3
        H = 8
        DK = D // H
        U4 = U3 + H3
        q4, k4, v4, o4 = view(0, KC, N), view(1536, KC, N), view(3072, NT, D), view(4608, KC, N)
        route = sb("route", [P, 32])
        kv_in = sems("kv_in", 2)
        q_in, o_in = sem("q_in"), sem("o_in")
        route_i = sb("route_i", [1, 1], I32)
        q_slot, k_slot, v_slot, o_slot, r_slot = 2, 3, 4, 5, 7

        @on("sp")
        def _(sp, o):
            ring.load(sp, banks, r_slot, [(ring.slot(r_slot)[:, :, 0:P], A["L3_ffn_r_w1"].rearrange("(c p) n -> p c n", p=P))])
            sp.wait_ge(step_ready, 8)
            chosen = sp.alloc_register("chosen")
            sp.reg_load(chosen, route_i[0:1, 0:1])
            for s_ in (q_slot, k_slot, v_slot, o_slot):
                if ring.last[s_] is not None:
                    banks.filled(sp, *ring.last[s_])
            for i in range(OPTS):
                with sp.If_eq(chosen, i):
                    sp.dma_start(ring.slot(q_slot), A[f"L3_ffn_wq{i}"].rearrange("(c p) n -> p c n", p=P)).then_inc(q_in, 16)
                    for nm, s_, j in (("wk", k_slot, 0), ("wv", v_slot, 1)):
                        w = A[f"L3_ffn_{nm}{i}"]
                        rep = H // (w.shape[1] // DK)
                        for h in range(H):
                            sp.dma_start(ring.slot(s_)[:, :, h * DK:(h + 1) * DK],
                                         w[:, h // rep * DK:(h // rep + 1) * DK].rearrange("(c p) n -> p c n", p=P)).then_inc(
                                kv_in[j], 16)
                    sp.dma_start(ring.slot(o_slot), A[f"L3_ffn_wo{i}"].rearrange("(c p) n -> p c n", p=P)).then_inc(o_in, 16)

        @on("pe")
        def _(pe, o):
            pe.wait_ge(xn_ready, NORM["f3"] + 1)
            pe_transpose(pe, "f3x", xn)
            rw1 = ring.get(pe, r_slot)
            for c in range(KC):
                banks.drained(pe, f"f3x{c}")
            pe.wait_ge(step_ready, 7)
            b = banks.open(pe, "f3r")
            for c in range(KC):
                last = mm(b[:, 0:1], rw1[:, c, 0:P], route[:, c:c + 1], c == 0, c == KC - 1)
            last.then_inc(banks.full_of("f3r"), 1)
            banks.drained(pe, "f3r")
            b = banks.open(pe, "f3g")
            mm(b[0:1, 0:OPTS], route[:, 4:5], rw2, True, False)
            mm(b[0:1, 0:OPTS], ones[0:1, 0:1], r_rb2, False, True).then_inc(banks.full_of("f3g"), 1)
            def scores(h):
                r = slice(DK * (h % 2), DK * (h % 2) + DK)
                for t in range(NT):
                    b = banks.open(pe, f"f3h{h}s{t}")
                    mm(b[:, 0:N], q4[r, h // 2, t * P:(t + 1) * P], k4[r, h // 2, :], True, True).then_inc(
                        banks.full_of(f"f3h{h}s{t}"), 1)

            def values(h):
                pe_att_transpose(pe, f"f3h{h}", U4 + h, h % 3)
                for c in range(NT):
                    banks.drained(pe, f"f3h{h}p{c}")
                b = banks.open(pe, f"f3o{h}")
                for c in range(NT):
                    last = mm(b[:, 0:N], v4[:, c, h // 2 * P:(h // 2 + 1) * P], probsT[:, h % 2, c, :], c == 0, c == NT - 1)
                last.then_inc(banks.full_of(f"f3o{h}"), 1)

            w = ring.slot(q_slot)
            pe.wait_ge(q_in, 16)
            for c in range(KC):
                pe_cols(pe, f"f3q{c}", xT, w, c * P)
            pe.wait_ge(kv_in[0], 16 * H)
            for c in range(KC):
                pe_cols(pe, f"f3k{c}", xT, ring.slot(k_slot), c * P)
            pe.wait_ge(kv_in[1], 16 * H)
            for t in range(NT):
                pe_rows(pe, f"f3v{t}", xT, ring.slot(v_slot), t)
            for c in range(KC):
                banks.drained(pe, f"f3q{c}")
                banks.drained(pe, f"f3k{c}")
            for t in range(NT):
                banks.drained(pe, f"f3v{t}")
            for h in range(H + 2):
                if h < H:
                    scores(h)
                if h >= 2:
                    values(h - 2)
            for h in range(H):
                banks.drained(pe, f"f3o{h}")
            w = ring.slot(o_slot)
            pe.wait_ge(o_in, 16)
            for t in range(NT):
                pe_rows(pe, f"f3y{t}", o4, w, t)

        @on("act")
        def _(act, o):
            act_norm(act, NORM["f3"])
            act_transposed(act, "f3x", xT)
            b = banks.filled(act, "f3r")
            nc.scalar.activation(route[:, 4:5], b[:, 0:1], ACT.Relu, bias=c_rb1).then_inc(banks.free_of("f3r"), 1)
            banks.drained(act, "f3g")
            nc.scalar.activation(route[0:1, 12:15], route[0:1, 8:11], ACT.Exp).then_inc(gate_exp, 1)
            for c in range(KC):
                act_copy(act, f"f3q{c}", q4[:, c, :], N)
            for c in range(KC):
                act_copy(act, f"f3k{c}", k4[:, c, :], N)
            for t in range(NT):
                act_copy(act, f"f3v{t}", v4[:, t, :], D)
            for h in range(H + 2):
                if h < H:
                    act_att_exp_scores(act, f"f3h{h}", U4 + h, h % 3, float(DK) ** -0.5)
                if h >= 2:
                    g = h - 2
                    act_att_transposed(act, f"f3h{g}", g % 2)
                    r = slice(DK * (g % 2), DK * (g % 2) + DK)
                    b = banks.filled(act, f"f3o{g}")
                    nc.scalar.activation(o4[r, g // 2, :], b[r, 0:N], ACT.Copy).then_inc(banks.free_of(f"f3o{g}"), 1)

        @on("dve")
        def _(dve, od):
            dve_norm(dve, od, NORM["f3"], x, xn)
            for c in range(KC):
                banks.drained(dve, f"f3x{c}")
            od.link(nc.vector.tensor_reduce(route[:, 0:4], xT[:], AX, ALU.add))
            nc.vector.tensor_scalar(route[:, 0:4], route[:, 0:4], 1.0 / N, None, ALU.mult).then_inc(step_ready, 1)
            b = banks.filled(dve, "f3g")[0:1, 0:OPTS]
            od.link(nc.vector.tensor_reduce(route[0:1, 5:6], b, AX, ALU.max))
            nc.vector.tensor_scalar(route[0:1, 8:11], b, route[0:1, 5:6], None, ALU.subtract).then_inc(banks.free_of("f3g"), 1)
            dve.wait_ge(gate_exp, 4)
            od.link(nc.vector.tensor_reduce(route[0:1, 5:6], route[0:1, 12:15], AX, ALU.add))
            od.link(nc.vector.reciprocal(route[0:1, 5:6], route[0:1, 5:6]))
            od.link(nc.vector.tensor_scalar(route[0:1, 12:15], route[0:1, 12:15], route[0:1, 5:6], None, ALU.mult))
            od.link(nc.vector.tensor_reduce(route[0:1, 6:7], route[0:1, 12:15], AX, ALU.max))
            od.link(nc.vector.tensor_scalar(route[0:1, 16:19], route[0:1, 12:15], route[0:1, 6:7], None, ALU.is_equal))
            od.link(nc.vector.tensor_tensor(route[0:1, 16:19], route[0:1, 16:19], iota_back[0:1, 0:OPTS], ALU.mult))
            od.link(nc.vector.tensor_reduce(route[0:1, 6:7], route[0:1, 16:19], AX, ALU.min))
            nc.vector.tensor_scalar(route_i[:], route[0:1, 6:7], 64.0, None, ALU.add).then_inc(step_ready, 1)
            for h in range(H + 1):
                if h < H:
                    dve_att_max(dve, od, f"f3h{h}", h % 3, float(DK) ** -0.5)
                if h >= 1:
                    dve_att_probs(dve, od, U4 + h - 1, (h - 1) % 3, None, f"f3h{h - 1}")
            for t in range(NT):
                b = banks.filled(dve, f"f3y{t}")
                nc.vector.tensor_tensor(x[:, t, :], x[:, t, :], b, ALU.add).then_inc(banks.free_of(f"f3y{t}"), 1)
            for t in range(NT):
                banks.drained(dve, f"f3y{t}")

        block = ctx.enter_context(nc.Block())

        @block.tensor
        def _(pe):
            for f in layers["pe"]:
                f(pe, None)

        @block.scalar
        def _(act):
            o = Order(act, act_order)
            for f in layers["act"]:
                f(act, o)

        @block.vector
        def _(dve):
            od = Order(dve, dve_order)
            for f in layers["dve"]:
                f(dve, od)
            nc.vector.memset(gate[:, 15, 0:1], 0.0).then_inc(out_ready, 1)

        @block.gpsimd
        def _(pool):
            op = Order(pool, pool_order)
            for f in layers["pool"]:
                f(pool, op)

        @block.sync
        def _(sp):
            for f in layers["sp"]:
                f(sp, None)
            sp.wait_ge(out_ready, 1)
            sp.dma_start(tiled(out), x[:]).then_inc(stored, 16)
            sp.wait_ge(stored, 16)


INPUTS = ["x", "src", "dst", "edge_type_8", "edge_weight", "node_vec1"] + ["L0_gnn_" + n for n in (
    "Wv bv Ww bw Wa ba gamma beta").split()] + ["L0_ffn_" + n for n in "w_gating gamma w1 w2".split()] + [
    "L1_gnn_" + n for n in (
        "f_w1 f_b1 f_w2 f_b2 s1_w s1_b b1_w b1_b wq bq wk bk wv bv wo bo s2_w s2_b b2_w b2_b m_w1 m_b1 m_w2 m_b2").split()] + [
    "L1_ffn_" + n for n in "w_gating w1 w2".split()] + [
    "L2_gnn_" + n for n in "W a_src a_dst et_emb ln_gamma ln_beta".split()] + [
    "L2_ffn_" + n for n in "expert_weights expert_biases mixer_w mixer_b".split()] + [
    "L3_gnn_" + n for n in "Wq bq Wk bk Wv bv Wskip bskip Wlin blin gamma beta".split()] + [
    "L3_ffn_" + n for n in "r_w1 r_b1 r_w2 r_b2 wq0 wk0 wv0 wo0 wq1 wk1 wv1 wo1 wq2 wk2 wv2 wo2".split()]


def kernel(**inputs):
    import numpy as _np
    import concourse.bacc as _bacc
    from concourse import mybir as _mybir
    from concourse.bass_utils import run_bass_kernel_spmd as _run

    nc = _bacc.Bacc("TRN2", target_bir_lowering=False, num_devices=1)
    arrays, aps = {}, {}
    for name in INPUTS:
        a = _np.ascontiguousarray(inputs[name])
        arrays[f"in_{name}"] = a
        aps[name] = nc.dram_tensor(f"in_{name}", a.shape, _mybir.dt.from_np(a.dtype), kind="ExternalInput").ap()
    out = nc.dram_tensor("out_x", (N, D), F32, kind="ExternalOutput").ap()
    with nc.allow_non_contiguous_dma("bias columns and weight tiles are loaded in the layout that the engines read"):
        gnn_ffn_program(nc, aps, out)
    r = _run(nc, [arrays], core_ids=[0])
    return r.results[0]["out_x"]
```
